# Optimizing a Trainium2 kernel written in Bass

```python
import numpy as np
import jax
import jax.numpy as jnp

def _softmax(x, axis=-1):
    return jax.nn.softmax(x, axis=axis)

def _gelu(x):
    return jax.nn.gelu(x, approximate=True)

def _silu(x):
    return jax.nn.silu(x)

def _sigmoid(x):
    return jax.nn.sigmoid(x)

def _layernorm(x, axis=-1, eps=1e-05):
    m = jnp.mean(x, axis=axis, keepdims=True)
    v = jnp.var(x, axis=axis, keepdims=True)
    return (x - m) / jnp.sqrt(v + eps)

def _scatter_add(tgt, idx, src, axis=0):
    return tgt.at[idx].add(src)

def _segment_sum(src, seg, n):
    return jax.ops.segment_sum(src, seg, n)
kernel_name = 'mk_adj_resnorm_d4_adj_r2_cd9250'

def setup_inputs(seed: int=0):
    np.random.seed(seed)
    _w = jnp.asarray

    def _rec_inputs():
        import jax
        import jax.numpy as jnp
        _gk = jax.random.key(seed)
        x = -0.0002928 + 1 * jax.random.normal(jax.random.fold_in(_gk, 1), (32, 256, 128), jnp.float32)
        _a = jax.random.bernoulli(jax.random.fold_in(_gk, 2), 0.015625, (32, 256, 256))
        _a = jnp.logical_or(_a, jnp.swapaxes(_a, -1, -2))
        _a = jnp.logical_or(_a, jnp.eye(256, dtype=bool))
        adj = _a.astype(jnp.int32)
        _nm = jnp.ones((32, 256), dtype=bool)
        nodemask = jnp.where(_nm, 1.0, 0.0).astype(jnp.float32)
        return (x, adj, nodemask)
    x, adj, nodemask = _rec_inputs()

    def _L0_gnn_setup():
        import jax, jax.numpy as jnp
        import numpy as np
        B, N, F_IN, F_OUT = (8, 1024, 128, 128)
        ALPHA = 0.2
        key = jax.random.key(seed)
        k1, k2, k3, k4 = jax.random.split(key, 4)
        h = jax.random.normal(k1, (B, N, F_IN), dtype=jnp.float32)
        adj = jax.random.randint(k2, (B, N, N), 0, 2, dtype=jnp.int32)
        W = jax.random.normal(k3, (F_OUT, F_IN), dtype=jnp.float32) / np.sqrt(F_IN)
        a = jax.random.normal(k4, (1, 2 * F_OUT), dtype=jnp.float32) / np.sqrt(2 * F_OUT)
        return {'h': h, 'adj': adj, 'W': W, 'a': a}
    _L0_gnn_all = _L0_gnn_setup()
    _L0_gnn_in = {k: v for k, v in _L0_gnn_all.items() if k in ('W', 'a')}
    del _L0_gnn_all

    def _L1_gnn_setup():
        import jax, jax.numpy as jnp
        import numpy as np
        B, N, F_IN, F_OUT = (1, 4096, 128, 128)
        ALPHA = 0.2
        NEG_INF = -9000000000000000.0
        key = jax.random.key(seed)
        ks = jax.random.split(key, 8)
        feat = jax.random.normal(ks[0], (B, N, F_IN), dtype=jnp.float32)
        adj = jax.random.randint(ks[1], (B, N, N), 0, 2, dtype=jnp.int32)
        s = 1.414 * (6.0 / (F_IN + F_OUT)) ** 0.5
        W = jax.random.uniform(ks[2], (F_IN, F_OUT), minval=-s, maxval=s, dtype=jnp.float32)
        a_1 = jax.random.normal(ks[3], (F_OUT, 1), dtype=jnp.float32) * 0.1
        a_2 = jax.random.normal(ks[4], (F_OUT, 1), dtype=jnp.float32) * 0.1
        a_12 = jax.random.normal(ks[5], (F_OUT, F_OUT), dtype=jnp.float32) * (1.0 / F_OUT ** 0.5)
        W_1 = jax.random.uniform(ks[6], (F_IN, F_OUT), minval=-s, maxval=s, dtype=jnp.float32)
        W_2 = jax.random.uniform(ks[7], (F_IN, F_OUT), minval=-s, maxval=s, dtype=jnp.float32)
        return {'feat': feat, 'adj': adj, 'W': W, 'a_1': a_1, 'a_2': a_2, 'a_12': a_12, 'W_1': W_1, 'W_2': W_2}
    _L1_gnn_all = _L1_gnn_setup()
    _L1_gnn_in = {k: v for k, v in _L1_gnn_all.items() if k in ('W', 'a_1', 'a_2', 'a_12', 'W_1', 'W_2')}
    del _L1_gnn_all

    def _L2_gnn_setup():
        import jax, jax.numpy as jnp
        import numpy as np
        import math
        IN_DIM = 128
        OUT_DIM = 128
        HEADS = 4
        D_K = OUT_DIM // HEADS
        key = jax.random.key(seed)
        ks = jax.random.split(key, 10)
        B, N = (4, 2048)
        x = jax.random.normal(ks[0], (B, N, IN_DIM), dtype=jnp.float32)
        adj = jax.random.randint(ks[1], (B, N, N), 0, 2, dtype=jnp.int32)
        s = 1.0 / math.sqrt(IN_DIM)
        Wq = jax.random.normal(ks[2], (IN_DIM, OUT_DIM), dtype=jnp.float32) * s
        bq = jnp.zeros((OUT_DIM,), dtype=jnp.float32)
        Wk = jax.random.normal(ks[3], (IN_DIM, OUT_DIM), dtype=jnp.float32) * s
        bk = jnp.zeros((OUT_DIM,), dtype=jnp.float32)
        Wv = jax.random.normal(ks[4], (IN_DIM, OUT_DIM), dtype=jnp.float32) * s
        bv = jnp.zeros((OUT_DIM,), dtype=jnp.float32)
        Wo = jax.random.normal(ks[5], (OUT_DIM, OUT_DIM), dtype=jnp.float32) * (1.0 / math.sqrt(OUT_DIM))
        bo = jnp.zeros((OUT_DIM,), dtype=jnp.float32)
        return {'x': x, 'adj': adj, 'Wq': Wq, 'bq': bq, 'Wk': Wk, 'bk': bk, 'Wv': Wv, 'bv': bv, 'Wo': Wo, 'bo': bo}
    _L2_gnn_all = _L2_gnn_setup()
    _L2_gnn_in = {k: v for k, v in _L2_gnn_all.items() if k in ('Wq', 'bq', 'Wk', 'bk', 'Wv', 'bv', 'Wo', 'bo')}
    del _L2_gnn_all

    def _L3_gnn_setup():
        import jax, jax.numpy as jnp
        import numpy as np
        D_MODEL = 128
        NUM_REL = 40

        def _direction(x, W, Wg, b, bg, adj, rel_ids):
            h = x @ W.T
            g = h @ Wg.T
            vals = (h[:, :, None, :] + b) * jax.nn.sigmoid(g[:, :, None, :] + bg)
            onehot = (adj[..., None] == rel_ids).astype(h.dtype)
            return jnp.einsum('bnmr,bmrd->bnd', onehot, vals)
        key = jax.random.key(seed)
        ks = jax.random.split(key, 16)
        B, N, d = (2, 256, D_MODEL)
        s = 0.02
        inp = {'node': jax.random.normal(ks[0], (B, N, d), dtype=jnp.float32), 'node_mask': jnp.ones((B, N), dtype=jnp.float32), 'adj_mat': jax.random.randint(ks[1], (B, N, N), 0, 41, dtype=jnp.int32), 'W_fwd': jax.random.normal(ks[2], (d, d), dtype=jnp.float32) * s, 'W_bwd': jax.random.normal(ks[3], (d, d), dtype=jnp.float32) * s, 'W_loop': jax.random.normal(ks[4], (d, d), dtype=jnp.float32) * s, 'Wg_fwd': jax.random.normal(ks[5], (d, d), dtype=jnp.float32) * s, 'Wg_bwd': jax.random.normal(ks[6], (d, d), dtype=jnp.float32) * s, 'Wg_loop': jax.random.normal(ks[7], (d, d), dtype=jnp.float32) * s, 'b_fwd': jax.random.normal(ks[8], (NUM_REL - 1, d), dtype=jnp.float32) * s, 'b_bwd': jax.random.normal(ks[9], (NUM_REL - 1, d), dtype=jnp.float32) * s, 'b_loop': jax.random.normal(ks[10], (1, d), dtype=jnp.float32) * s, 'bg_fwd': jax.random.normal(ks[11], (NUM_REL - 1, d), dtype=jnp.float32) * s, 'bg_bwd': jax.random.normal(ks[12], (NUM_REL - 1, d), dtype=jnp.float32) * s, 'bg_loop': jax.random.normal(ks[13], (1, d), dtype=jnp.float32) * s}
        return inp
    _L3_gnn_all = _L3_gnn_setup()
    _L3_gnn_in = {k: v for k, v in _L3_gnn_all.items() if k in ('W_fwd', 'W_bwd', 'W_loop', 'Wg_fwd', 'Wg_bwd', 'Wg_loop', 'b_fwd', 'b_bwd', 'b_loop', 'bg_fwd', 'bg_bwd', 'bg_loop')}
    del _L3_gnn_all
    return {'x': x, 'adj': adj, 'nodemask': nodemask, 'L0_gnn_W': _L0_gnn_in['W'], 'L0_gnn_a': _L0_gnn_in['a'], 'L1_gnn_W': _L1_gnn_in['W'], 'L1_gnn_a_1': _L1_gnn_in['a_1'], 'L1_gnn_a_2': _L1_gnn_in['a_2'], 'L1_gnn_a_12': _L1_gnn_in['a_12'], 'L1_gnn_W_1': _L1_gnn_in['W_1'], 'L1_gnn_W_2': _L1_gnn_in['W_2'], 'L2_gnn_Wq': _L2_gnn_in['Wq'], 'L2_gnn_bq': _L2_gnn_in['bq'], 'L2_gnn_Wk': _L2_gnn_in['Wk'], 'L2_gnn_bk': _L2_gnn_in['bk'], 'L2_gnn_Wv': _L2_gnn_in['Wv'], 'L2_gnn_bv': _L2_gnn_in['bv'], 'L2_gnn_Wo': _L2_gnn_in['Wo'], 'L2_gnn_bo': _L2_gnn_in['bo'], 'L3_gnn_W_fwd': _L3_gnn_in['W_fwd'], 'L3_gnn_W_bwd': _L3_gnn_in['W_bwd'], 'L3_gnn_W_loop': _L3_gnn_in['W_loop'], 'L3_gnn_Wg_fwd': _L3_gnn_in['Wg_fwd'], 'L3_gnn_Wg_bwd': _L3_gnn_in['Wg_bwd'], 'L3_gnn_Wg_loop': _L3_gnn_in['Wg_loop'], 'L3_gnn_b_fwd': _L3_gnn_in['b_fwd'], 'L3_gnn_b_bwd': _L3_gnn_in['b_bwd'], 'L3_gnn_b_loop': _L3_gnn_in['b_loop'], 'L3_gnn_bg_fwd': _L3_gnn_in['bg_fwd'], 'L3_gnn_bg_bwd': _L3_gnn_in['bg_bwd'], 'L3_gnn_bg_loop': _L3_gnn_in['bg_loop']}

def reference(x, adj, nodemask, L0_gnn_W, L0_gnn_a, L1_gnn_W, L1_gnn_a_1, L1_gnn_a_2, L1_gnn_a_12, L1_gnn_W_1, L1_gnn_W_2, L2_gnn_Wq, L2_gnn_bq, L2_gnn_Wk, L2_gnn_bk, L2_gnn_Wv, L2_gnn_bv, L2_gnn_Wo, L2_gnn_bo, L3_gnn_W_fwd, L3_gnn_W_bwd, L3_gnn_W_loop, L3_gnn_Wg_fwd, L3_gnn_Wg_bwd, L3_gnn_Wg_loop, L3_gnn_b_fwd, L3_gnn_b_bwd, L3_gnn_b_loop, L3_gnn_bg_fwd, L3_gnn_bg_bwd, L3_gnn_bg_loop):
    import jax
    import jax.numpy as jnp

    def _L0_gnn_ref(h, adj, W, a):
        import jax, jax.numpy as jnp
        import numpy as np
        B, N, F_IN, F_OUT = (8, 1024, 128, 128)
        ALPHA = 0.2
        Wh = jnp.einsum('bnf,of->bno', h, W)
        Fo = Wh.shape[-1]
        a1 = a[0, :Fo]
        a2 = a[0, Fo:]
        s1 = Wh @ a1
        s2 = Wh @ a2
        e = jax.nn.leaky_relu(s1[:, :, None] + s2[:, None, :], negative_slope=ALPHA)
        mask = adj == 0
        e = jnp.where(mask, -jnp.inf, e)
        att = jax.nn.softmax(e, axis=-1)
        att = jnp.where(mask, 0.0, att)
        return jnp.einsum('bij,bjo->bio', att, Wh)

    def _L1_gnn_ref(feat, adj, W, a_1, a_2, a_12, W_1, W_2):
        import jax, jax.numpy as jnp
        import numpy as np
        B, N, F_IN, F_OUT = (1, 4096, 128, 128)
        ALPHA = 0.2
        NEG_INF = -9000000000000000.0
        h = jnp.matmul(feat, W)
        Ax = jnp.matmul(h, a_1)
        Ay = jnp.matmul(h, a_2)
        A_xy = jnp.matmul(jnp.matmul(h, a_12), jnp.swapaxes(h, 1, 2))
        logits = jnp.swapaxes(Ax, 1, 2) + Ay + A_xy
        e = jax.nn.leaky_relu(logits, negative_slope=ALPHA)
        e = jnp.where(adj > 0, e, NEG_INF)
        attention = jax.nn.softmax(e, axis=-1)
        h_prime = jnp.matmul(attention, feat)
        h_out = jnp.matmul(feat, W_1) + jnp.matmul(h_prime, W_2)
        return jax.nn.elu(h_out)

    def _L2_gnn_ref(x, adj, Wq, bq, Wk, bk, Wv, bv, Wo, bo):
        import jax, jax.numpy as jnp
        import numpy as np
        import math
        IN_DIM = 128
        OUT_DIM = 128
        HEADS = 4
        D_K = OUT_DIM // HEADS
        B, N, _ = x.shape
        q = (x @ Wq + bq).reshape(B, N, HEADS, D_K)
        k = (x @ Wk + bk).reshape(B, N, HEADS, D_K)
        v = (x @ Wv + bv).reshape(B, N, HEADS, D_K)
        scale = 1.0 / math.sqrt(D_K + 1e-09)
        scores = jnp.einsum('bnhd,bmhd->bhnm', q, k) * scale
        eye = jnp.eye(N, dtype=bool)
        mask = (adj.astype(bool) | eye)[:, None, :, :]
        min_val = jnp.finfo(scores.dtype).min
        scores = jnp.where(mask, scores, min_val)
        attn = jax.nn.softmax(scores, axis=-1)
        out = jnp.einsum('bhnm,bmhd->bnhd', attn, v).reshape(B, N, OUT_DIM)
        out = out @ Wo + bo
        return jax.nn.relu(out)

    def _L3_gnn_ref(node, node_mask, adj_mat, W_fwd, W_bwd, W_loop, Wg_fwd, Wg_bwd, Wg_loop, b_fwd, b_bwd, b_loop, bg_fwd, bg_bwd, bg_loop):
        import jax, jax.numpy as jnp
        import numpy as np
        D_MODEL = 128
        NUM_REL = 40

        def _direction(x, W, Wg, b, bg, adj, rel_ids):
            h = x @ W.T
            g = h @ Wg.T
            vals = (h[:, :, None, :] + b) * jax.nn.sigmoid(g[:, :, None, :] + bg)
            onehot = (adj[..., None] == rel_ids).astype(h.dtype)
            return jnp.einsum('bnmr,bmrd->bnd', onehot, vals)
        rels = jnp.arange(2, NUM_REL + 1, dtype=adj_mat.dtype)
        rel1 = jnp.array([1], dtype=adj_mat.dtype)
        adj_t = jnp.swapaxes(adj_mat, -1, -2)
        out = _direction(node, W_fwd, Wg_fwd, b_fwd, bg_fwd, adj_mat, rels)
        out = out + _direction(node, W_bwd, Wg_bwd, b_bwd, bg_bwd, adj_t, rels)
        out = out + _direction(node, W_loop, Wg_loop, b_loop, bg_loop, adj_t, rel1)
        return jax.nn.relu(out)
    x = _layernorm(x + _L0_gnn_ref(x, adj, L0_gnn_W, L0_gnn_a), axis=-1)
    x = _layernorm(x + _L1_gnn_ref(x, adj, L1_gnn_W, L1_gnn_a_1, L1_gnn_a_2, L1_gnn_a_12, L1_gnn_W_1, L1_gnn_W_2), axis=-1)
    x = _layernorm(x + _L2_gnn_ref(x, adj, L2_gnn_Wq, L2_gnn_bq, L2_gnn_Wk, L2_gnn_bk, L2_gnn_Wv, L2_gnn_bv, L2_gnn_Wo, L2_gnn_bo), axis=-1)
    x = _layernorm(x + _L3_gnn_ref(x, nodemask, adj, L3_gnn_W_fwd, L3_gnn_W_bwd, L3_gnn_W_loop, L3_gnn_Wg_fwd, L3_gnn_Wg_bwd, L3_gnn_Wg_loop, L3_gnn_b_fwd, L3_gnn_b_bwd, L3_gnn_b_loop, L3_gnn_bg_fwd, L3_gnn_bg_bwd, L3_gnn_bg_loop), axis=-1)
    return x

_drawn_inputs = setup_inputs


def setup_inputs(seed=0):
    import zlib

    import numpy as np

    out = dict(_drawn_inputs(seed))
    spreads = {'L2_gnn_bq': (0.0, 0.328),
     'L2_gnn_bk': (0.0, 0.8),
     'L2_gnn_bv': (0.0, 0.1),
     'L2_gnn_bo': (0.0, 0.1)}
    factors = {'L1_gnn_a_2': 6.655, 'L3_gnn_Wg_loop': 8.0, 'L3_gnn_bg_loop': 8.0}
    for name, (base, spread) in spreads.items():
        noise = np.random.default_rng([zlib.crc32(name.encode()), seed]).standard_normal(out[name].shape)
        drawn = base * np.exp(spread * noise) if base else spread * noise
        out[name] = jnp.asarray(drawn.astype(out[name].dtype))
    for name, factor in factors.items():
        out[name] = (out[name] * factor).astype(out[name].dtype)
    return out
```

```python
from contextlib import ExitStack

import numpy as np
import concourse.bass as bass
from concourse import mybir

F32 = mybir.dt.float32
BF16 = mybir.dt.bfloat16
I32 = mybir.dt.int32
ALU = mybir.AluOpType
ACT = mybir.ActivationFunctionType
AX = mybir.AxisListType

P = 128
SLOTS = 4
HEADS = 4
EPS = 1e-5
SLOPE = 0.2
NEG_INF = -1e30
NEG_L1 = -9e15
TINY = 1e-30
LOWEST = -3.0e38

RINGS = ("tp", "mm", "big")
STEPS = [
    ("xT0", [("tp", "xT_sb0", 1, 0)]),
    ("proj0", [("big", "proj0_sb", 1, 0)]),
    ("pT0", [("tp", "pT_sb0", 1, 0)]),
    ("agg0", [("mm", "agg0_read", 1, 0)]),
    ("xT1", [("tp", "xT_sb1", 1, 0)]),
    ("proj1", [("mm", "tT_sb", 1, 0), ("big", "xw_sb", 1, 0)]),
    ("scores1", [("mm", "z_sb", 1, 0)]),
    ("pT1", [("tp", "pT_sb1", 1, 0)]),
    ("agg1", [("mm", "agg1_read", 1, 0)]),
    ("xT2", [("tp", "xT_sb2", 1, 0)]),
    ("proj2", [("big", "qkv_sb", 2, 1)]),
    ("scores2", [("big", "scores2_read", 2, 0), ("big", "scores2_read", 2, 1)]),
    ("pT2", [("tp", "pT_sb2", 4, h) for h in range(4)]),
    ("agg2", [("mm", "oT_sb", 1, 0)]),
    ("o_nodes", [("tp", "o_sb", 1, 0)]),
    ("oT", [("tp", "onT_sb", 1, 0)]),
    ("wo", [("mm", "wo_read", 1, 0)]),
    ("xT3", [("tp", "xT_sb3", 1, 0)]),
    ("proj3", [("mm", "hg_read", 1, 0)]),
    ("agg3", [("mm", "agg3_read", 1, 0)]),
]
ORDER = [(step, s) for step, _ in STEPS for s in range(SLOTS)]


def ring_uses(ring):
    return [(step, s, k, sem, per, at)
            for step, uses in STEPS for s in range(SLOTS)
            for k, (r, sem, per, at) in enumerate(uses) if r == ring]


def build(nc, t, out):
    B, N, D = t["x"].shape
    T = N // P
    DK = D // HEADS
    SCALE = 1.0 / float(np.sqrt(DK + 1e-09))
    NREL = t["L3_gnn_b_fwd"].shape[0]
    assert D == P and T == 2 and B % SLOTS == 0
    rings = {r: ring_uses(r) for r in RINGS}
    assert all(len(u) % 2 == 0 for u in rings.values())

    with ExitStack() as ctx:
        def sb(name, shape, dt=F32):
            return ctx.enter_context(nc.sbuf_tensor(name, shape, dt))

        sems = {}

        def sem(name):
            if name not in sems:
                sems[name] = ctx.enter_context(nc.semaphore(name))
            return sems[name]

        ident = sb("ident", [P, P])
        not_eye = sb("not_eye", [P, T, N], BF16)
        minus_half = sb("minus_half", [P, T])
        minus_one = sb("minus_one", [P, 1])
        w_in = sb("w_in", [P, 13, P])
        W0, W1L, A12, W_1, W_2, WQ, WK, WV, WO, WL, WGL = range(11)
        cols = sb("cols", [P, 8])
        A1, A2, L1A1, L1A2, BQ, BK, BV = range(7)
        w0T1 = sb("w0T1", [P, D + 1])
        w2rep = sb("w2rep", [P, P])
        wT = sb("wT", [P, 4, P])
        M1 = sb("M1", [P, P])
        u12 = sb("u12", [P, 2])
        xw_w = sb("xw_w", [P, 2 * D + 1])
        bv_rep = sb("bv_rep", [P, P])
        bo_row = sb("bo_row", [P, D])
        hg_w = sb("hg_w", [P, 2 * D])
        hg_bias = sb("hg_bias", [P, 2 * D])
        ones_row = sb("ones_row", [P, P])
        excess_row = sb("excess_row", [P, SLOTS])
        excess_sum = sb("excess_sum", [P, 1])
        excess_all = sb("excess_all", [P, 1])
        excess_flag = sb("excess_flag", [P, 1], I32)

        x_in = sb("x_in", [P, SLOTS, T, D])
        adj_in = sb("adj_in", [P, SLOTS, T, N], I32)
        neg0 = sb("neg0", [P, SLOTS, T, N], BF16)
        neg1 = sb("neg1", [P, SLOTS, T, N], BF16)
        neg2 = sb("neg2", [P, SLOTS, T, N], BF16)
        eq1 = sb("eq1", [P, SLOTS, T, N])
        over_one = sb("over_one", [P, SLOTS, T, N], BF16)
        xT = sb("xT", [P, SLOTS, N])
        x1 = sb("x1", [P, SLOTS, T, D])
        x2 = sb("x2", [P, SLOTS, T, D])
        x3 = sb("x3", [P, SLOTS, T, D])
        x4 = sb("x4", [P, SLOTS, T, D])
        y = sb("y", [P, SLOTS, T, D])
        stats = sb("stats", [P, SLOTS, T, 6])
        mv = sb("mv", [P, SLOTS, T, 2])
        ve = sb("ve", [P, SLOTS, T])
        rstd = sb("rstd", [P, SLOTS, T])
        wh = sb("wh", [P, SLOTS, T, D + 2])
        xw = sb("xw", [P, SLOTS, T, 2 * D + 2])
        tT = sb("tT", [P, SLOTS, N])
        rowmax = sb("rowmax", [P, SLOTS, T])
        small = sb("small", [P, SLOTS, 6, T])
        rsum = sb("rsum", [P, SLOTS, T])
        hmid = sb("hmid", [P, SLOTS, T, D])
        hneg = sb("hneg", [P, SLOTS, T, D])
        hpos = sb("hpos", [P, SLOTS, T, D])
        qblk = sb("qblk", [P, SLOTS, HEADS, N])
        kT = sb("kT", [P, SLOTS, N])
        vn = sb("vn", [P, SLOTS, T, D])
        p2 = sb("p2", [P, SLOTS, T, HEADS, N])
        p2T = sb("p2T", [P, SLOTS, HEADS, T, N])
        sm, pa, pb, prob = (p2[:, :, :, :, :].rearrange("p s t h n -> p s (t h n)")[:, :, c * T * N:(c + 1) * T * N]
                            .rearrange("p s (t n) -> p s t n", t=T) for c in range(4))
        probT = p2T[:, :, 0]
        rowmax2 = sb("rowmax2", [P, SLOTS, T * HEADS])
        nmax2 = sb("nmax2", [P, SLOTS, T * HEADS])
        sum2 = sb("sum2", [P, SLOTS, T * HEADS])
        rsum2 = sb("rsum2", [P, SLOTS, T * HEADS])
        oT = sb("oT", [P, SLOTS, N])
        hg = sb("hg", [P, SLOTS, T, 2 * D])
        on = hneg
        onT = tT
        vals = hmid

        ps = ctx.enter_context(nc.psum_tensor("ps", [P, 8, 512], F32))
        FIRST_BANK = {"tp": 0, "mm": 2, "big": 4}

        def bank(step, s, k=0):
            for ring, uses in rings.items():
                for at, u in enumerate(uses):
                    if u[:3] == (step, s, k):
                        b = FIRST_BANK[ring] + (at % 2) * (2 if ring == "big" else 1)
                        return ps[:, b, :] if ring != "big" else ps[:, b:b + 2, :]
            raise KeyError((step, s, k))

        def bank_read(pe, step, s, k, n, first):
            for uses in rings.values():
                for at, u in enumerate(uses):
                    if u[:3] != (step, s, k):
                        continue
                    _, s_before, _, read, per, number = uses[at - 2]
                    graph = n - s + s_before
                    if at < 2:
                        if first:
                            return
                        graph = graph - SLOTS
                    pe.wait_ge(sem(read), graph * per + number + 1)

        x3_dram = nc.dram_tensor("x3_aside", (B, P, T * D), F32, kind="Internal").ap()

        x_v = t["x"].rearrange("b (t p) d -> b p t d", p=P)
        adj_v = t["adj"].rearrange("b (t p) j -> b p t j", p=P)
        out_v = out.rearrange("b (t p) d -> b p t d", p=P)
        loads = [
            (w_in[:, W0, :], t["L0_gnn_W"]),
            (cols[:, A1:A1 + 1], t["L0_gnn_a"][:, 0:D].rearrange("a p -> p a")),
            (cols[:, A2:A2 + 1], t["L0_gnn_a"][:, D:2 * D].rearrange("a p -> p a")),
            (w_in[:, W1L, :], t["L1_gnn_W"]), (w_in[:, A12, :], t["L1_gnn_a_12"]),
            (w_in[:, W_1, :], t["L1_gnn_W_1"]), (w_in[:, W_2, :], t["L1_gnn_W_2"]),
            (cols[:, L1A1:L1A1 + 1], t["L1_gnn_a_1"]), (cols[:, L1A2:L1A2 + 1], t["L1_gnn_a_2"]),
            (w_in[:, WQ, :], t["L2_gnn_Wq"]), (w_in[:, WK, :], t["L2_gnn_Wk"]),
            (w_in[:, WV, :], t["L2_gnn_Wv"]), (w_in[:, WO, :], t["L2_gnn_Wo"]),
            (cols[:, BQ:BQ + 1], t["L2_gnn_bq"].rearrange("(p a) -> p a", a=1)),
            (cols[:, BK:BK + 1], t["L2_gnn_bk"].rearrange("(p a) -> p a", a=1)),
            (cols[:, BV:BV + 1], t["L2_gnn_bv"].rearrange("(p a) -> p a", a=1)),
            (bo_row[:, :], t["L2_gnn_bo"].rearrange("(a d) -> a d", a=1).broadcast_to((P, D))),
            (w_in[:, WL, :], t["L3_gnn_W_loop"]), (w_in[:, WGL, :], t["L3_gnn_Wg_loop"]),
            (hg_bias[:, 0:D], t["L3_gnn_b_loop"].broadcast_to((P, D))),
            (hg_bias[:, D:2 * D], t["L3_gnn_bg_loop"].broadcast_to((P, D))),
        ]

        rel_w = qblk[:, 0, 0:2, :]
        rel_adj = adj_in[:, 0]
        rel_adj_f = eq1[:, 1]
        rel_adjT_f = eq1[:, 2]
        rel_hot = (eq1[:, 0], eq1[:, 3])
        rel_x = x1[:, 0]
        rel_xT = xT[:, 0]
        rel_hg = hg
        rel_bias = y
        rel_sum = xw
        rel_vals = (x2[:, 0], x2[:, 1])
        rel_acc = x4[:, 0]
        rel_out = x4[:, 1]
        rel_no = sb("rel_no", [P, 1])
        rel_biases = ((t["L3_gnn_b_fwd"], t["L3_gnn_bg_fwd"]), (t["L3_gnn_b_bwd"], t["L3_gnn_bg_bwd"]))
        rel_weights = [t["L3_gnn_W_fwd"], t["L3_gnn_W_bwd"], t["L3_gnn_Wg_fwd"], t["L3_gnn_Wg_bwd"]]

        def if_relations(engine):
            engine.wait_ge(sem("flag_ready"), 1)
            flag = engine.value_load(excess_flag[0:1, 0:1], min_val=0, max_val=1)
            return engine.If(flag != 0)

        block = ctx.enter_context(nc.Block())

        wait_registers = {}

        def wait_apart(engine, semaphore, value):
            if not isinstance(value, int):
                if engine not in wait_registers:
                    wait_registers[engine] = engine.alloc_register(f"awaited{len(wait_registers)}")
                engine.reg_alu(wait_registers[engine], value - 1, 1, ALU.add)
                value = wait_registers[engine]
            engine.wait_ge(sem("consts_ready"), 1)
            engine.wait_ge(semaphore, value)

        def rounds(engine, one_round):
            one_round(0, True)
            with engine.Fori(SLOTS, B - SLOTS + 1, SLOTS) as i:
                one_round(i, False)

        @block.sync
        def _(sp):
            def load(i, s, first):
                if not first:
                    sp.wait_ge(sem("masks_ready"), i + s - SLOTS + 1)
                    sp.wait_ge(sem("excess_ready"), i + s - SLOTS + 1)
                    sp.wait_ge(sem("agg0_read"), i + s - SLOTS + 1)
                sp.dma_start(adj_in[:, s], adj_v[i + s]).then_inc(sem(f"adj_loaded{s}"), 16)
                sp.dma_start(x_in[:, s], x_v[i + s]).then_inc(sem(f"x_loaded{s}"), 16)

            def store(i, s):
                sp.wait_ge(sem("x3_ready"), i + s + 1)
                sp.dma_start(x3_dram[i + s], x3[:, s].rearrange("p t d -> p (t d)"))\
                    .then_inc(sem(f"x3_aside{s}"), 16)
                sp.wait_ge(sem("x4_ready"), i + s + 1)
                sp.dma_start(out_v[i + s], x4[:, s]).then_inc(sem(f"stored{s}"), 16)

            load(0, 0, True)
            for dst, src in loads:
                sp.dma_start(dst, src).then_inc(sem("weights_loaded"), 16)
            for s in range(1, SLOTS):
                load(0, s, True)
            with sp.Fori(SLOTS, B - SLOTS + 1, SLOTS) as i:
                for s in range(SLOTS):
                    load(i, s, False)
                for s in range(SLOTS):
                    store(i - SLOTS, s)
            for s in range(SLOTS):
                store(B - SLOTS, s)
            for s in range(SLOTS):
                sp.wait_ge(sem(f"stored{s}"), 16 * (B // SLOTS))
                sp.wait_ge(sem(f"x3_aside{s}"), 16 * (B // SLOTS))
            with if_relations(sp):
                for k, w in enumerate(rel_weights):
                    sp.dma_start(w_in[:, k, :], w).then_inc(sem("rel_w_loaded"), 16)
                with sp.Fori(0, B) as g:
                    sp.wait_ge(sem("rel_graph_done"), g + 1)
                    sp.dma_start(rel_adj, adj_v[g]).then_inc(sem("rel_loaded"), 16)
                    sp.dma_start(rel_x.rearrange("p t d -> p (t d)"), x3_dram[g]).then_inc(sem("rel_loaded"), 16)
                    with sp.Fori(0, NREL) as r:
                        sp.wait_ge(sem("rel_sums_ready"), g * NREL + r + 1)
                        for way in range(2):
                            for part in range(2):
                                sp.dma_start(rel_bias[:, way, part, :],
                                             rel_biases[way][part].rearrange("r (a d) -> r a d", a=1)[r].broadcast_to((P, D)))\
                                    .then_inc(sem("rel_bias_loaded"), 16)
                    sp.wait_ge(sem("rel_out_ready"), g + 1)
                    sp.dma_start(out_v[g], rel_out).then_inc(sem("rel_stored"), 16)
                sp.wait_ge(sem("rel_stored"), 16 * B)

        @block.tensor
        def _(pe):
            def setup():
                pe.wait_ge(sem("consts_ready"), 1)
                pe.wait_ge(sem("weights_loaded"), 16 * len(loads))
                for k, w in enumerate((W0, W1L, A12, WL)):
                    last = pe.transpose(ps[:, 0, k * P:(k + 1) * P], w_in[:, w, :], ident[:, :])
                last.then_inc(sem("setup_pe"), 1)
                pe.transpose(ps[:, 1, 0:P], w_in[:, WGL, :], ident[:, :])
                pe.matmul(ps[:, 1, P:P + 1], w_in[:, W0, :], cols[:, A1:A1 + 1], start=True, stop=True)
                pe.matmul(ps[:, 5, 0:1], w_in[:, W0, :], cols[:, A2:A2 + 1],
                          start=True, stop=True).then_inc(sem("setup_pe"), 1)
                pe.wait_ge(sem("bv_ready"), 1)
                pe.matmul(ps[:, 2, 0:D], bv_rep[:, :], w_in[:, WO, :], start=True, stop=True)\
                    .then_inc(sem("setup_pe"), 1)
                pe.wait_ge(sem("setup_t_sb"), 2)
                pe.matmul(ps[:, 3, 0:P], wT[:, 1, :], wT[:, 0, :], start=True, stop=True)
                pe.matmul(ps[:, 3, P:P + 2], wT[:, 0, :], cols[:, L1A1:L1A2 + 1], start=True, stop=True)
                pe.matmul(ps[:, 3, 2 * P:3 * P], w_in[:, WL, :], wT[:, 2, :], start=True, stop=True)\
                    .then_inc(sem("setup_pe"), 1)
                pe.wait_ge(sem("setup_t_sb"), 3)
                pe.matmul(ps[:, 4, 0:P], wT[:, 0, :], wT[:, 3, :], start=True, stop=True)\
                    .then_inc(sem("setup_pe"), 1)
                pe.wait_ge(sem("weights_ready"), 2)

            def transpose_x(layer, n, s, first, src):
                o = bank(f"xT{layer}", s)
                bank_read(pe, f"xT{layer}", s, 0, n, first)
                for k in range(T):
                    last = pe.transpose(o[:, k * P:(k + 1) * P], src[:, s, k, :], ident[:, :])
                last.then_inc(sem(f"xT_ps{layer}"), 1)

            def xT0(n, s, first):
                pe.wait_ge(sem(f"x_loaded{s}"), (n - s) * (16 // SLOTS) + 16)
                transpose_x(0, n, s, first, x_in)

            def proj0(n, s, first):
                o = bank("proj0", s)
                bank_read(pe, "proj0", s, 0, n, first)
                pe.wait_ge(sem("xT_sb0"), n + 1)
                pe.matmul(o[:, 0, 0:N], w2rep[:, :], xT[:, s, :], start=True, stop=True)
                for k in range(T):
                    last = pe.matmul(o[:, 1, k * (D + 1):(k + 1) * (D + 1)], xT[:, s, k * P:(k + 1) * P],
                                     w0T1[:, :], start=True, stop=True)
                last.then_inc(sem("proj0_ps"), 1)

            def transpose_p(layer, n, s, first):
                o = bank(f"pT{layer}", s)
                bank_read(pe, f"pT{layer}", s, 0, n, first)
                pe.wait_ge(sem(f"p_ready{layer}"), n + 1)
                for j in range(T):
                    for k in range(T):
                        last = pe.transpose(o[:, j * N + k * P:j * N + (k + 1) * P],
                                            prob[:, s, k, j * P:(j + 1) * P], ident[:, :])
                last.then_inc(sem(f"pT_ps{layer}"), 1)

            def aggregate(layer, n, s, first, values):
                o = bank(f"agg{layer}", s)
                bank_read(pe, f"agg{layer}", s, 0, n, first)
                pe.wait_ge(sem(f"pT_sb{layer}"), n + 1)
                for k in range(T):
                    for j in range(T):
                        last = pe.matmul(o[:, k * (D + 1):(k + 1) * (D + 1)],
                                         probT[:, s, j, k * P:(k + 1) * P], values(j),
                                         start=(j == 0), stop=(j == T - 1))
                last.then_inc(sem(f"agg{layer}_ps"), 1)

            def agg0(n, s, first):
                pe.wait_ge(sem("wh_sb"), n + 1)
                aggregate(0, n, s, first, lambda j: wh[:, s, j, 0:D + 1])

            def xT1(n, s, first):
                pe.wait_ge(sem("x1_ready"), n + 1)
                transpose_x(1, n, s, first, x1)

            def proj1(n, s, first):
                o, o2 = bank("proj1", s, 0), bank("proj1", s, 1)
                pe.wait_ge(sem("xT_sb1"), n + 1)
                bank_read(pe, "proj1", s, 0, n, first)
                pe.matmul(o[:, 0:N], M1[:, :], xT[:, s, :], start=True, stop=True).then_inc(sem("tT_ps"), 1)
                bank_read(pe, "proj1", s, 1, n, first)
                for k in range(T):
                    last = pe.matmul(o2[:, k, 0:2 * D + 1], xT[:, s, k * P:(k + 1) * P], xw_w[:, :],
                                     start=True, stop=True)
                last.then_inc(sem("xw_ps"), 1)

            def scores1(n, s, first):
                o = bank("scores1", s)
                bank_read(pe, "scores1", s, 0, n, first)
                pe.wait_ge(sem("tT_sb"), n + 1)
                for k in range(T):
                    last = pe.matmul(o[:, k * N:(k + 1) * N], tT[:, s, k * P:(k + 1) * P], xT[:, s, :],
                                     start=True, stop=True)
                last.then_inc(sem("z_ps"), 1)

            def agg1(n, s, first):
                pe.wait_ge(sem("xw_sb"), n + 1)
                aggregate(1, n, s, first, lambda j: xw[:, s, j, D + 1:2 * D + 2])

            def xT2(n, s, first):
                pe.wait_ge(sem("x2_ready"), n + 1)
                transpose_x(2, n, s, first, x2)

            def proj2(n, s, first):
                o = bank("proj2", s)
                bank_read(pe, "proj2", s, 0, n, first)
                pe.wait_ge(sem("xT_sb2"), n + 1)
                pe.matmul(o[:, 0, 0:N], w_in[:, WQ, :], xT[:, s, :], start=True, stop=True)
                pe.matmul(o[:, 1, N:2 * N], w_in[:, WK, :], xT[:, s, :], start=True, stop=True)
                for k in range(T):
                    last = pe.matmul(o[:, 1, k * D:(k + 1) * D], xT[:, s, k * P:(k + 1) * P],
                                     w_in[:, WV, :], start=True, stop=True)
                last.then_inc(sem("qkv_ps"), 1)

            def scores2(n, s, first):
                for k in range(T):
                    o = bank("scores2", s, k)
                    if k == 0:
                        pe.wait_ge(sem("qkv_sb"), n * 2 + 2)
                        pe.wait_ge(sem("q_sb"), n + 1)
                    bank_read(pe, "scores2", s, k, n, first)
                    for h in range(HEADS):
                        last = pe.matmul(o[:, h // 2, (h % 2) * N:(h % 2 + 1) * N],
                                         qblk[:, s, h, k * P:(k + 1) * P], kT[:, s, :], start=True, stop=True)
                    last.then_inc(sem("scores2_ps"), 1)

            def pT2(n, s, first):
                pe.wait_ge(sem("p_ready2"), n + 1)
                for h in range(HEADS):
                    o = bank("pT2", s, h)
                    bank_read(pe, "pT2", s, h, n, first)
                    for j in range(T):
                        for k in range(T):
                            last = pe.transpose(o[:, j * N + k * P:j * N + (k + 1) * P],
                                                p2[:, s, k, h, j * P:(j + 1) * P], ident[:, :])
                    last.then_inc(sem("pT_ps2"), 1)

            def agg2(n, s, first):
                o = bank("agg2", s)
                bank_read(pe, "agg2", s, 0, n, first)
                pe.wait_ge(sem("pT_sb2"), n * HEADS + HEADS)
                for j in range(T):
                    for h in range(HEADS):
                        last = pe.matmul(o[h * DK:(h + 1) * DK, 0:N], vn[:, s, j, h * DK:(h + 1) * DK],
                                         p2T[:, s, h, j, :], start=(j == 0), stop=(j == T - 1))
                last.then_inc(sem("agg2_ps"), 1)

            def o_nodes(n, s, first):
                o = bank("o_nodes", s)
                bank_read(pe, "o_nodes", s, 0, n, first)
                pe.wait_ge(sem("oT_sb"), n + 1)
                for k in range(T):
                    last = pe.transpose(o[:, k * P:(k + 1) * P], oT[:, s, k * P:(k + 1) * P], ident[:, :])
                last.then_inc(sem("o_nodes_ps"), 1)

            def oT_(n, s, first):
                o = bank("oT", s)
                bank_read(pe, "oT", s, 0, n, first)
                pe.wait_ge(sem("o_sb"), n + 1)
                for k in range(T):
                    last = pe.transpose(o[:, k * P:(k + 1) * P], on[:, s, k, :], ident[:, :])
                last.then_inc(sem("onT_ps"), 1)

            def wo(n, s, first):
                o = bank("wo", s)
                bank_read(pe, "wo", s, 0, n, first)
                pe.wait_ge(sem("onT_sb"), n + 1)
                for k in range(T):
                    last = pe.matmul(o[:, k * D:(k + 1) * D], onT[:, s, k * P:(k + 1) * P], w_in[:, WO, :],
                                     start=True, stop=True)
                last.then_inc(sem("wo_ps"), 1)

            def xT3(n, s, first):
                pe.wait_ge(sem("x3_ready"), n + 1)
                transpose_x(3, n, s, first, x3)

            def proj3(n, s, first):
                o = bank("proj3", s)
                bank_read(pe, "proj3", s, 0, n, first)
                pe.wait_ge(sem("xT_sb3"), n + 1)
                for k in range(T):
                    last = pe.matmul(o[:, k * 2 * D:(k + 1) * 2 * D], xT[:, s, k * P:(k + 1) * P], hg_w[:, :],
                                     start=True, stop=True)
                last.then_inc(sem("hg_ps"), 1)

            def agg3(n, s, first):
                o = bank("agg3", s)
                bank_read(pe, "agg3", s, 0, n, first)
                pe.wait_ge(sem("vals_ready"), n + 1)
                for k in range(T):
                    for j in range(T):
                        last = pe.matmul(o[:, k * D:(k + 1) * D], eq1[:, s, j, k * P:(k + 1) * P],
                                         vals[:, s, j, :], start=(j == 0), stop=(j == T - 1))
                last.then_inc(sem("agg3_ps"), 1)

            steps = {
                "xT0": xT0, "proj0": proj0, "pT0": lambda *a: transpose_p(0, *a), "agg0": agg0,
                "xT1": xT1, "proj1": proj1, "scores1": scores1, "pT1": lambda *a: transpose_p(1, *a),
                "agg1": agg1, "xT2": xT2, "proj2": proj2, "scores2": scores2, "pT2": pT2, "agg2": agg2,
                "o_nodes": o_nodes, "oT": oT_, "wo": wo, "xT3": xT3, "proj3": proj3, "agg3": agg3,
            }

            def one_round(i, first):
                for step, s in ORDER:
                    steps[step](i + s, s, first)

            def relations():
                pe.wait_ge(sem("x4_ready"), B)
                pe.wait_ge(sem("rel_w_loaded"), 16 * len(rel_weights))
                for k in range(4):
                    last = pe.transpose(ps[:, 0, k * P:(k + 1) * P], w_in[:, k, :], ident[:, :])
                last.then_inc(sem("rel_setup_pe"), 1)
                pe.wait_ge(sem("rel_setup_sb"), 1)
                for way in range(2):
                    last = pe.matmul(ps[:, 1, way * P:(way + 1) * P], w_in[:, way, :], wT[:, way, :],
                                     start=True, stop=True)
                last.then_inc(sem("rel_setup_pe"), 1)
                pe.wait_ge(sem("rel_setup_sb"), 2)
                with pe.Fori(0, B) as g:
                    pe.wait_ge(sem("rel_adj_f_ready"), g + 1)
                    for j in range(T):
                        for k in range(T):
                            pe.transpose(ps[:, 0, j * N + k * P:j * N + (k + 1) * P],
                                         rel_adj_f[:, k, j * P:(j + 1) * P], ident[:, :])
                    for k in range(T):
                        last = pe.transpose(ps[:, 1, k * P:(k + 1) * P], rel_x[:, k, :], ident[:, :])
                    last.then_inc(sem("rel_T_ps"), 1)
                    pe.wait_ge(sem("rel_T_sb"), g + 1)
                    for way, w in enumerate((rel_w[:, 0, :], rel_w[:, 1, :], hg_w[:, :])):
                        for k in range(T):
                            last = pe.matmul(ps[:, 2 + way, k * 2 * D:(k + 1) * 2 * D],
                                             rel_xT[:, k * P:(k + 1) * P], w, start=True, stop=True)
                    last.then_inc(sem("rel_hg_ps"), 1)
                    pe.wait_ge(sem("rel_loop_vals"), g + 1)
                    for k in range(T):
                        for j in range(T):
                            last = pe.matmul(ps[:, 5, k * D:(k + 1) * D], rel_hot[0][:, j, k * P:(k + 1) * P],
                                             rel_vals[0][:, j, :], start=(j == 0), stop=(j == T - 1))
                    last.then_inc(sem("rel_loop_ps"), 1)
                    with pe.Fori(0, NREL) as r:
                        pe.wait_ge(sem("rel_vals_ready"), g * NREL + r + 1)
                        for k in range(T):
                            for way in range(2):
                                for j in range(T):
                                    last = pe.matmul(ps[:, 6, k * D:(k + 1) * D],
                                                     rel_hot[way][:, j, k * P:(k + 1) * P],
                                                     rel_vals[way][:, j, :], start=(way + j == 0),
                                                     stop=(way == 1 and j == T - 1))
                        last.then_inc(sem("rel_ps"), 1)
                        pe.wait_ge(sem("rel_added"), g * NREL + r + 1)

            setup()
            rounds(pe, one_round)
            with if_relations(pe):
                relations()

        @block.scalar
        def _(act):
            def setup():
                act.wait_ge(sem("minus_one_ready"), 1)
                act.wait_ge(sem("setup_pe"), 1)
                nc.scalar.copy(w0T1[:, 0:D], ps[:, 0, 0:P])
                nc.scalar.copy(wT[:, 0:2, :].rearrange("p a n -> p (a n)"), ps[:, 0, P:3 * P])\
                    .then_inc(sem("setup_t_sb"), 1)
                nc.scalar.mul(hg_w[:, 0:D], ps[:, 0, 3 * P:4 * P], 0.5)
                act.wait_ge(sem("setup_pe"), 2)
                nc.scalar.copy(w0T1[:, D:D + 1], ps[:, 1, P:P + 1])
                nc.scalar.copy(wT[:, 2, :], ps[:, 1, 0:P]).then_inc(sem("setup_t_sb"), 1)
                act.wait_ge(sem("setup_pe"), 4)
                nc.scalar.copy(wT[:, 3, :], ps[:, 3, 0:P]).then_inc(sem("setup_t_sb"), 1)
                nc.scalar.copy(u12[:, :], ps[:, 3, P:P + 2])
                nc.scalar.copy(xw_w[:, D:D + 1], ps[:, 3, P + 1:P + 2])
                nc.scalar.copy(hg_w[:, D:2 * D], ps[:, 3, 2 * P:3 * P])
                nc.scalar.copy(xw_w[:, 0:D], w_in[:, W_1, :])
                nc.scalar.copy(xw_w[:, D + 1:2 * D + 1], w_in[:, W_2, :])
                act.wait_ge(sem("setup_pe"), 5)
                nc.scalar.copy(M1[:, :], ps[:, 4, 0:P]).then_inc(sem("weights_ready"), 1)

            def test_adj(n, s, first):
                act.wait_ge(sem(f"adj_loaded{s}"), (n - s) * (16 // SLOTS) + 16)
                if not first:
                    act.wait_ge(sem("excess_added"), n - SLOTS + 1)
                nc.scalar.activation(over_one[:, s], adj_in[:, s], ACT.Relu, bias=minus_one[:, 0:1],
                                     accum_out=excess_row[:, s:s + 1]).then_inc(sem("excess_ready"), 1)

            def copy_xT(layer, n, s):
                act.wait_ge(sem(f"xT_ps{layer}"), n + 1)
                nc.scalar.copy(xT[:, s, :], bank(f"xT{layer}", s)[:, 0:N]).then_inc(sem(f"xT_sb{layer}"), 1)

            def proj0(n, s, first):
                act.wait_ge(sem("proj0_ps"), n + 1)
                o = bank("proj0", s)[:, 1, 0:T * (D + 1)].rearrange("p (t d) -> p t d", t=T)
                nc.scalar.copy(wh[:, s, :, D + 1:D + 2], o[:, :, D:D + 1])
                nc.scalar.copy(wh[:, s, :, 0:D], o[:, :, 0:D]).then_inc(sem("wh_sb"), 1)

            def pT0(n, s, first):
                act.wait_ge(sem("shift0_ready"), n + 1)
                for k in range(T):
                    nc.scalar.activation(pa[:, s, k, :], sm[:, s, k, :], ACT.Exp, bias=small[:, s, 2, k:k + 1])
                    last = nc.scalar.activation(pb[:, s, k, :], sm[:, s, k, :], ACT.Exp,
                                                bias=small[:, s, 3, k:k + 1], scale=SLOPE)
                last.then_inc(sem("branches_ready"), 1)

            def agg0(n, s, first):
                act.wait_ge(sem("pT_ps0"), n + 1)
                nc.scalar.copy(probT[:, s].rearrange("p t n -> p (t n)"), bank("pT0", s))\
                    .then_inc(sem("pT_sb0"), 1)

            def proj1(n, s, first):
                act.wait_ge(sem("tT_ps"), n + 1)
                nc.scalar.activation(tT[:, s, :], bank("proj1", s, 0)[:, 0:N], ACT.Identity,
                                     bias=u12[:, 0:1]).then_inc(sem("tT_sb"), 1)
                act.wait_ge(sem("xw_ps"), n + 1)
                nc.scalar.copy(xw[:, s, :, 0:2 * D + 1], bank("proj1", s, 1)[:, :, 0:2 * D + 1])\
                    .then_inc(sem("xw_sb"), 1)

            def scores1(n, s, first):
                act.wait_ge(sem("z_ps"), n + 1)
                if True:
                    act.wait_ge(sem("xw_sb"), n + 1)
                for k in range(T):
                    last = nc.scalar.activation(pa[:, s, k, :], bank("scores1", s)[:, k * N:(k + 1) * N],
                                                ACT.Identity, bias=xw[:, s, k, D:D + 1])
                last.then_inc(sem("z_sb"), 1)

            def pT1(n, s, first):
                act.wait_ge(sem("shift1_ready"), n + 1)
                for k in range(T):
                    last = nc.scalar.activation(prob[:, s, k, :], sm[:, s, k, :], ACT.Exp,
                                                bias=small[:, s, 0, k:k + 1])
                last.then_inc(sem("p_ready1"), 1)

            def agg1(n, s, first):
                act.wait_ge(sem("pT_ps1"), n + 1)
                nc.scalar.copy(probT[:, s].rearrange("p t n -> p (t n)"), bank("pT1", s))\
                    .then_inc(sem("pT_sb1"), 1)

            def elu1(n, s, first):
                act.wait_ge(sem("hneg_ready"), n + 1)
                nc.scalar.activation(hneg[:, s].rearrange("p t d -> p (t d)"),
                                     hneg[:, s].rearrange("p t d -> p (t d)"), ACT.Exp)\
                    .then_inc(sem("hexp_ready"), 1)

            def proj2(n, s, first):
                act.wait_ge(sem("qkv_ps"), n + 1)
                o = bank("proj2", s)
                for h in range(2):
                    r = slice(h * DK, (h + 1) * DK)
                    nc.scalar.activation(qblk[r, s, h, :], o[r, 0, 0:N], ACT.Identity, bias=cols[r, BQ:BQ + 1])
                nc.scalar.activation(kT[:, s, :], o[:, 1, N:2 * N], ACT.Identity, bias=cols[:, BK:BK + 1])\
                    .then_inc(sem("qkv_sb"), 1)
                act.wait_ge(sem("q_sb"), n + 1)
                nc.scalar.copy(vn[:, s].rearrange("p t d -> p (t d)"), o[:, 1, 0:T * D])\
                    .then_inc(sem("qkv_sb"), 1)

            def exp2(n, s, first):
                for k in range(T):
                    act.wait_ge(sem("shift2_ready"), n * T + k + 1)
                    for h in range(HEADS):
                        c = k * HEADS + h
                        last = nc.scalar.activation(p2[:, s, k, h, :], p2[:, s, k, h, :], ACT.Exp,
                                                    bias=nmax2[:, s, c:c + 1], scale=SCALE,
                                                    accum_out=sum2[:, s, c:c + 1])
                last.then_inc(sem("p_ready2"), 1)

            def pT2(n, s, first):
                for h in range(HEADS):
                    act.wait_ge(sem("pT_ps2"), n * HEADS + h + 1)
                    nc.scalar.copy(p2T[:, s, h].rearrange("p t n -> p (t n)"), bank("pT2", s, h))\
                        .then_inc(sem("pT_sb2"), 1)

            def agg2(n, s, first):
                act.wait_ge(sem("agg2_ps"), n + 1)
                nc.scalar.copy(oT[:, s, :], bank("agg2", s)[:, 0:N]).then_inc(sem("oT_sb"), 1)

            def oT_(n, s, first):
                act.wait_ge(sem("onT_ps"), n + 1)
                nc.scalar.copy(onT[:, s, :], bank("oT", s)[:, 0:N]).then_inc(sem("onT_sb"), 1)

            def gate3(n, s, first):
                act.wait_ge(sem("hg_read"), n + 1)
                nc.scalar.activation(hg[:, s, :, D:2 * D], hg[:, s, :, D:2 * D], ACT.Tanh, scale=0.5)\
                    .then_inc(sem("gate_ready"), 1)

            steps = {
                "test_adj": test_adj, "xT0": lambda n, s, f: copy_xT(0, n, s), "proj0": proj0, "exp0": pT0, "pT0": agg0,
                "xT1": lambda n, s, f: copy_xT(1, n, s), "proj1": proj1, "scores1": scores1, "exp1": pT1,
                "pT1": agg1, "elu1": elu1, "xT2": lambda n, s, f: copy_xT(2, n, s), "proj2": proj2,
                "exp2": exp2, "pT2": pT2, "agg2": agg2, "oT": oT_,
                "xT3": lambda n, s, f: copy_xT(3, n, s), "gate3": gate3,
            }

            def one_round(i, first):
                for step in ("test_adj", "xT0", "proj0", "exp0", "pT0", "xT1", "proj1", "scores1", "exp1", "pT1", "elu1",
                             "xT2", "proj2", "exp2", "pT2", "agg2", "oT", "xT3", "gate3"):
                    for s in range(SLOTS):
                        steps[step](i + s, s, first)

            def relations():
                act.wait_ge(sem("rel_setup_pe"), 1)
                for way in range(2):
                    nc.scalar.mul(rel_w[:, way, 0:D], ps[:, 0, way * P:(way + 1) * P], 0.5)
                nc.scalar.copy(wT[:, 0:2, :].rearrange("p a n -> p (a n)"), ps[:, 0, 2 * P:4 * P])\
                    .then_inc(sem("rel_setup_sb"), 1)
                act.wait_ge(sem("rel_setup_pe"), 2)
                nc.scalar.copy(rel_w[:, :, D:2 * D], ps[:, 1, 0:2 * P].rearrange("p (a n) -> p a n", a=2))\
                    .then_inc(sem("rel_setup_sb"), 1)
                with act.Fori(0, B) as g:
                    act.wait_ge(sem("rel_T_ps"), g + 1)
                    nc.scalar.copy(rel_adjT_f.rearrange("p t n -> p (t n)"), ps[:, 0, :])
                    nc.scalar.copy(rel_xT, ps[:, 1, 0:N]).then_inc(sem("rel_T_sb"), 1)
                    act.wait_ge(sem("rel_hg_ps"), g + 1)
                    nc.scalar.copy(rel_hg[:, 0:3].rearrange("p w t d -> p w (t d)"), ps[:, 2:5, :])\
                        .then_inc(sem("rel_hg_sb"), 1)
                    act.wait_ge(sem("rel_loop_sum"), g + 1)
                    nc.scalar.activation(rel_hg[:, 2, :, D:2 * D], rel_hg[:, 2, :, D:2 * D], ACT.Tanh, scale=0.5)\
                        .then_inc(sem("rel_loop_gate"), 1)
                    with act.Fori(0, NREL) as r:
                        act.wait_ge(sem("rel_sums_ready"), g * NREL + r + 2)
                        for way in range(2):
                            last = nc.scalar.activation(rel_sum[:, way, :, D:2 * D], rel_sum[:, way, :, D:2 * D],
                                                        ACT.Tanh, scale=0.5)
                        last.then_inc(sem("rel_gates"), 1)

            setup()
            rounds(act, one_round)
            with if_relations(act):
                relations()

        @block.vector
        def _(dve):
            order = {"count": 0, "base": 0}

            def done(ins, apart=False):
                order["count"] += 1
                ins.then_inc(sem("dve_order"), 1)
                if apart:
                    wait_apart(dve, sem("dve_order"), order["base"] + order["count"])
                else:
                    dve.wait_ge(sem("dve_order"), order["base"] + order["count"])

            def setup():
                nc.vector.memset(ones_row[:, :], 1.0).then_inc(sem("ones_ready"), 1)
                nc.vector.memset(minus_half[:, :], -0.5)
                nc.vector.memset(minus_one[:, :], -1.0).then_inc(sem("minus_one_ready"), 1)
                nc.vector.memset(wh[:, :, :, D:D + 1], 1.0)
                nc.vector.memset(xw[:, :, :, 2 * D + 1:2 * D + 2], 1.0)
                nc.vector.memset(qblk[:, :, :, :], 0.0)
                dve.wait_ge(sem("ones_ready"), 1)
                dve.wait_ge(sem("weights_loaded"), 16 * len(loads))
                nc.vector.tensor_scalar(bv_rep[:, :], ones_row[:, :], cols[:, BV:BV + 1], None, ALU.mult)\
                    .then_inc(sem("bv_ready"), 1)
                nc.vector.tensor_scalar(hg_bias[:, 0:D], hg_bias[:, 0:D], 0.5, None, ALU.mult)
                dve.wait_ge(sem("setup_pe"), 2)
                nc.vector.tensor_scalar(w2rep[:, :], ones_row[:, :], ps[:, 5, 0:1], None, ALU.mult)
                dve.wait_ge(sem("setup_pe"), 3)
                nc.vector.tensor_tensor(bo_row[:, :], ps[:, 2, 0:D], bo_row[:, :], ALU.add)\
                    .then_inc(sem("weights_ready"), 1)

            def masks(n, s, first):
                dve.wait_ge(sem(f"adj_loaded{s}"), (n - s) * (16 // SLOTS) + 16)
                nc.vector.tensor_scalar(neg0[:, s], adj_in[:, s], 0.0, NEG_INF, ALU.is_equal, ALU.mult)
                nc.vector.tensor_scalar(neg1[:, s], adj_in[:, s], 0.0, NEG_L1, ALU.is_le, ALU.mult)
                nc.vector.tensor_scalar(eq1[:, s], adj_in[:, s], 1.0, None, ALU.is_equal)\
                    .then_inc(sem("masks_ready"), 1)

            def layernorm(n, s, dst, ready, layer):
                for k in range(T):
                    last = nc.vector.bn_stats(stats[:, s, k, :], y[:, s, k, :])
                done(last, apart=True)
                for k in range(T):
                    last = nc.vector.bn_aggr(mv[:, s, k, :], stats[:, s, k, :])
                last.then_inc(sem(f"mv{layer}_ready"), 1)
                dve.wait_ge(sem(f"rstd{layer}_ready"), n + 1)
                for k in range(T):
                    last = nc.vector.tensor_scalar(dst[:, s, k, :], y[:, s, k, :], mv[:, s, k, 0:1],
                                                   rstd[:, s, k:k + 1], ALU.subtract, ALU.mult)
                last.then_inc(sem(ready), 1)

            def shift0(n, s, first):
                dve.wait_ge(sem("masks_ready"), n + 1)
                wait_apart(dve, sem("proj0_ps"), n + 1)
                o = bank("proj0", s)
                for k in range(T):
                    last = nc.vector.tensor_tensor_reduce(sm[:, s, k, :], o[:, 0, 0:N], neg0[:, s, k, :], 1.0, LOWEST,
                                                          ALU.add, ALU.max, rowmax[:, s, k:k + 1])
                done(last)
                dve.wait_ge(sem("wh_sb"), n + 1)
                s1 = wh[:, s, :, D + 1]
                nc.vector.scalar_tensor_tensor(out=small[:, s, 0, :], in0=rowmax[:, s, :], scalar=0.1 * NEG_INF,
                                               in1=s1, op0=ALU.max, op1=ALU.add).then_inc(sem("proj0_sb"), 1)
                dve.wait_ge(sem("proj0_sb"), n + 1)
                done(nc.vector.scalar_tensor_tensor(out=small[:, s, 1, :], in0=small[:, s, 0, :], scalar=SLOPE,
                                                    in1=small[:, s, 0, :], op0=ALU.mult, op1=ALU.max))
                nc.vector.tensor_tensor(small[:, s, 2, :], s1, small[:, s, 1, :], ALU.subtract)
                nc.vector.scalar_tensor_tensor(out=small[:, s, 3, :], in0=s1, scalar=SLOPE, in1=small[:, s, 1, :],
                                               op0=ALU.mult, op1=ALU.subtract).then_inc(sem("shift0_ready"), 1)

            def row_sums(s, o):
                done(nc.vector.tensor_scalar(small[:, s, 4, :], o[:, :, D], TINY, None, ALU.max))
                done(nc.vector.reciprocal(rsum[:, s, :], small[:, s, 4, :]))

            def max0(n, s, first):
                dve.wait_ge(sem("branches_ready"), n + 1)
                nc.vector.tensor_tensor(prob[:, s], pa[:, s], pb[:, s], ALU.max).then_inc(sem("p_ready0"), 1)

            def norm0(n, s, first):
                dve.wait_ge(sem("agg0_ps"), n + 1)
                o = bank("agg0", s)[:, 0:T * (D + 1)].rearrange("p (t d) -> p t d", t=T)
                row_sums(s, o)
                for k in range(T):
                    last = nc.vector.scalar_tensor_tensor(out=y[:, s, k, :], in0=o[:, k, 0:D], scalar=rsum[:, s, k:k + 1],
                                                          in1=x_in[:, s, k, :], op0=ALU.mult, op1=ALU.add)
                last.then_inc(sem("agg0_read"), 1)
                dve.wait_ge(sem("agg0_read"), n + 1)
                layernorm(n, s, x1, "x1_ready", 0)

            def shift1(n, s, first):
                dve.wait_ge(sem("z_sb"), n + 1)
                done(nc.vector.scalar_tensor_tensor(out=pb[:, s], in0=pa[:, s], scalar=SLOPE, in1=pa[:, s],
                                                    op0=ALU.mult, op1=ALU.max), apart=True)
                for k in range(T):
                    last = nc.vector.tensor_tensor_reduce(sm[:, s, k, :], pb[:, s, k, :], neg1[:, s, k, :], 1.0, LOWEST,
                                                          ALU.add, ALU.max, rowmax[:, s, k:k + 1])
                done(last)
                nc.vector.tensor_scalar(small[:, s, 0, :], rowmax[:, s, :], -1.0, None, ALU.mult)\
                    .then_inc(sem("shift1_ready"), 1)

            def elu1(n, s, first):
                dve.wait_ge(sem("agg1_ps"), n + 1)
                o = bank("agg1", s)[:, 0:T * (D + 1)].rearrange("p (t d) -> p t d", t=T)
                done(nc.vector.reciprocal(rsum[:, s, :], o[:, :, D]))
                for k in range(T):
                    last = nc.vector.scalar_tensor_tensor(out=hmid[:, s, k, :], in0=o[:, k, 0:D], scalar=rsum[:, s, k:k + 1],
                                                          in1=xw[:, s, k, 0:D], op0=ALU.mult, op1=ALU.add)
                last.then_inc(sem("agg1_read"), 1)
                dve.wait_ge(sem("agg1_read"), n + 1)
                nc.vector.tensor_scalar(hneg[:, s], hmid[:, s], 0.0, None, ALU.min).then_inc(sem("hneg_ready"), 1)
                nc.vector.scalar_tensor_tensor(out=hpos[:, s], in0=hmid[:, s], scalar=0.0, in1=x1[:, s],
                                               op0=ALU.max, op1=ALU.add).then_inc(sem("hpos_ready"), 1)

            def norm1(n, s, first):
                dve.wait_ge(sem("hexp_ready"), n + 1)
                dve.wait_ge(sem("hpos_ready"), n + 1)
                done(nc.vector.scalar_tensor_tensor(out=y[:, s], in0=hneg[:, s], scalar=-1.0, in1=hpos[:, s],
                                                    op0=ALU.add, op1=ALU.add))
                layernorm(n, s, x2, "x2_ready", 1)

            def proj2(n, s, first):
                dve.wait_ge(sem("qkv_ps"), n + 1)
                o = bank("proj2", s)
                for h in range(2, 4):
                    r = slice(h * DK, (h + 1) * DK)
                    last = nc.vector.tensor_scalar(qblk[r, s, h, :], o[r, 0, 0:N], cols[r, BQ:BQ + 1], None, ALU.add)
                last.then_inc(sem("q_sb"), 1)

            def shift2(n, s, first):
                wait_apart(dve, sem("neg2_ready"), n + 1)
                for k in range(T):
                    o = bank("scores2", s, k)
                    wait_apart(dve, sem("scores2_ps"), n * T + k + 1)
                    for h in range(HEADS):
                        c = k * HEADS + h
                        last = nc.vector.tensor_tensor_reduce(
                            p2[:, s, k, h, :], o[:, h // 2, (h % 2) * N:(h % 2 + 1) * N], neg2[:, s, k, :], 1.0, LOWEST,
                            ALU.add, ALU.max, rowmax2[:, s, c:c + 1])
                    last.then_inc(sem("scores2_read"), 1)
                    dve.wait_ge(sem("scores2_read"), n * T + k + 1)
                    nc.vector.tensor_scalar(nmax2[:, s, k * HEADS:(k + 1) * HEADS],
                                            rowmax2[:, s, k * HEADS:(k + 1) * HEADS], -SCALE, None, ALU.mult)\
                        .then_inc(sem("shift2_ready"), 1)

            def rsum2_(n, s, first):
                dve.wait_ge(sem("p_ready2"), n + 1)
                nc.vector.reciprocal(rsum2[:, s, :], sum2[:, s, :]).then_inc(sem("rsum2_ready"), 1)

            def o_nodes(n, s, first):
                dve.wait_ge(sem("o_nodes_ps"), n + 1)
                dve.wait_ge(sem("rsum2_ready"), n + 1)
                o = bank("o_nodes", s)[:, 0:N].rearrange("p (c d) -> p c d", c=T * HEADS)
                r = rsum2[:, s, :].rearrange("p (c a) -> p c a", a=1).to_broadcast([P, T * HEADS, DK])
                nc.vector.tensor_tensor(on[:, s].rearrange("p t (h d) -> p (t h) d", h=HEADS), o, r, ALU.mult)\
                    .then_inc(sem("o_sb"), 1)

            def norm2(n, s, first):
                dve.wait_ge(sem("wo_ps"), n + 1)
                o = bank("wo", s)[:, 0:T * D].rearrange("p (t d) -> p t d", t=T)
                b = bo_row[:, :].rearrange("p (a d) -> p a d", a=1).to_broadcast([P, T, D])
                nc.vector.tensor_tensor(hmid[:, s], o, b, ALU.add).then_inc(sem("wo_read"), 1)
                dve.wait_ge(sem("wo_read"), n + 1)
                done(nc.vector.scalar_tensor_tensor(out=y[:, s], in0=hmid[:, s], scalar=0.0, in1=x2[:, s],
                                                    op0=ALU.max, op1=ALU.add))
                if not first:
                    dve.wait_ge(sem(f"x3_aside{s}"), (n - s) * (16 // SLOTS))
                layernorm(n, s, x3, "x3_ready", 2)

            def proj3(n, s, first):
                dve.wait_ge(sem("hg_ps"), n + 1)
                b = hg_bias[:, :].rearrange("p (a d) -> p a d", a=1).to_broadcast([P, T, 2 * D])
                nc.vector.tensor_tensor(hg[:, s], bank("proj3", s).rearrange("p (t d) -> p t d", t=T), b, ALU.add)\
                    .then_inc(sem("hg_read"), 1)

            def vals3(n, s, first):
                dve.wait_ge(sem("gate_ready"), n + 1)
                nc.vector.scalar_tensor_tensor(out=vals[:, s], in0=hg[:, s, :, D:2 * D], scalar=1.0, in1=hg[:, s, :, 0:D],
                                               op0=ALU.add, op1=ALU.mult).then_inc(sem("vals_ready"), 1)

            def norm3(n, s, first):
                dve.wait_ge(sem("agg3_ps"), n + 1)
                o = bank("agg3", s)[:, 0:T * D].rearrange("p (t d) -> p t d", t=T)
                nc.vector.scalar_tensor_tensor(out=y[:, s], in0=o, scalar=0.0, in1=x3[:, s],
                                               op0=ALU.max, op1=ALU.add).then_inc(sem("agg3_read"), 1)
                dve.wait_ge(sem("agg3_read"), n + 1)
                if not first:
                    dve.wait_ge(sem(f"stored{s}"), (n - s) * (16 // SLOTS))
                layernorm(n, s, x4, "x4_ready", 3)

            steps = [masks, shift0, max0, norm0, shift1, elu1, norm1, proj2, shift2, rsum2_, o_nodes, norm2, proj3,
                     vals3, norm3]

            def one_round(i, first):
                for step in steps:
                    for s in range(SLOTS):
                        step(i + s, s, first)

            setup()
            one_round(0, True)
            per_round = order["count"]
            assert per_round % SLOTS == 0
            with dve.Fori(SLOTS, B - SLOTS + 1, SLOTS) as i:
                order["base"], order["count"] = i * (per_round // SLOTS), 0
                one_round(i, False)

            dve.wait_ge(sem("excess_all_ready"), 1)
            nc.vector.tensor_scalar(excess_flag[:, :], excess_all[:, :], 0.0, None, ALU.is_gt)\
                .then_inc(sem("flag_ready"), 1)

            def relations():
                def relation_steps(k):
                    dve.wait_ge(sem("rel_bias_loaded"), k * 64 + 64)
                    for way in range(2):
                        nc.vector.scalar_tensor_tensor(
                            out=rel_sum[:, way, :, 0:D],
                            in0=rel_bias[:, way, 0:1, :].to_broadcast([P, T, D]), scalar=0.5,
                            in1=rel_hg[:, way, :, 0:D], op0=ALU.mult, op1=ALU.add)
                        last = nc.vector.tensor_tensor(rel_sum[:, way, :, D:2 * D], rel_hg[:, way, :, D:2 * D],
                                                       rel_bias[:, way, 1:2, :].to_broadcast([P, T, D]), ALU.add)
                    last.then_inc(sem("rel_sums_ready"), 1)
                    for way, a in enumerate((rel_adjT_f, rel_adj_f)):
                        last = nc.vector.tensor_scalar(rel_hot[way], a, rel_no[:, 0:1], None, ALU.is_equal)
                    last.then_inc(sem("rel_hot_ready"), 1)
                    dve.wait_ge(sem("rel_hot_ready"), k + 1)
                    nc.vector.tensor_scalar(rel_no[:, :], rel_no[:, :], 1.0, None, ALU.add)\
                        .then_inc(sem("rel_no_ready"), 1)
                    dve.wait_ge(sem("rel_no_ready"), k + 1)
                    dve.wait_ge(sem("rel_gates"), k + 1)
                    for way in range(2):
                        last = nc.vector.scalar_tensor_tensor(
                            out=rel_vals[way], in0=rel_sum[:, way, :, D:2 * D], scalar=1.0,
                            in1=rel_sum[:, way, :, 0:D], op0=ALU.add, op1=ALU.mult)
                    last.then_inc(sem("rel_vals_ready"), 1)
                    dve.wait_ge(sem("rel_ps"), k + 1)
                    o = ps[:, 6, 0:T * D].rearrange("p (t d) -> p t d", t=T)
                    nc.vector.tensor_tensor(rel_acc, o, rel_acc, ALU.add).then_inc(sem("rel_added"), 1)
                    dve.wait_ge(sem("rel_added"), k + 1)

                dve.wait_ge(sem("x4_ready"), B)
                nc.vector.memset(rel_no[:, :], 0.0).then_inc(sem("rel_graph_done"), 1)
                nc.vector.memset(small[:, 0, 5, :], 0.0).then_inc(sem("rel_sums_ready"), 1)
                with dve.Fori(0, B) as g:
                    dve.wait_ge(sem("rel_graph_done"), g + 1)
                    dve.wait_ge(sem("rel_loaded"), g * 32 + 32)
                    nc.vector.memset(rel_no[:, :], 2.0).then_inc(sem("rel_first_no"), 1)
                    nc.vector.tensor_copy(rel_adj_f, rel_adj).then_inc(sem("rel_adj_f_ready"), 1)
                    dve.wait_ge(sem("rel_adj_f_ready"), g + 1)
                    nc.vector.tensor_scalar(rel_hot[0], rel_adj_f, 1.0, None, ALU.is_equal)
                    dve.wait_ge(sem("rel_hg_sb"), g + 1)
                    b = hg_bias[:, :].rearrange("p (a d) -> p a d", a=1).to_broadcast([P, T, 2 * D])
                    nc.vector.tensor_tensor(rel_hg[:, 2], rel_hg[:, 2], b, ALU.add).then_inc(sem("rel_loop_sum"), 1)
                    dve.wait_ge(sem("rel_loop_gate"), g + 1)
                    nc.vector.scalar_tensor_tensor(out=rel_vals[0], in0=rel_hg[:, 2, :, D:2 * D], scalar=1.0,
                                                   in1=rel_hg[:, 2, :, 0:D], op0=ALU.add, op1=ALU.mult)\
                        .then_inc(sem("rel_loop_vals"), 1)
                    dve.wait_ge(sem("rel_loop_ps"), g + 1)
                    nc.vector.tensor_copy(rel_acc, ps[:, 5, 0:T * D].rearrange("p (t d) -> p t d", t=T))\
                        .then_inc(sem("rel_acc_ready"), 1)
                    with dve.Fori(0, NREL) as r:
                        dve.wait_ge(sem("rel_acc_ready"), g + 1)
                        dve.wait_ge(sem("rel_first_no"), g + 1)
                        relation_steps(g * NREL + r)
                    nc.vector.scalar_tensor_tensor(out=hmid[:, 0], in0=rel_acc, scalar=0.0, in1=rel_x,
                                                   op0=ALU.max, op1=ALU.add).then_inc(sem("rel_y_ready"), 1)
                    dve.wait_ge(sem("rel_y_ready"), g + 1)
                    for k in range(T):
                        last = nc.vector.bn_stats(stats[:, 0, k, :], hmid[:, 0, k, :])
                    last.then_inc(sem("rel_stats"), 1)
                    wait_apart(dve, sem("rel_stats"), g + 1)
                    for k in range(T):
                        last = nc.vector.bn_aggr(mv[:, 0, k, :], stats[:, 0, k, :])
                    last.then_inc(sem("rel_mv"), 1)
                    dve.wait_ge(sem("rel_rstd"), g + 1)
                    for k in range(T):
                        last = nc.vector.tensor_scalar(rel_out[:, k, :], hmid[:, 0, k, :], mv[:, 0, k, 0:1],
                                                       rstd[:, 0, k:k + 1], ALU.subtract, ALU.mult)
                    last.then_inc(sem("rel_out_ready"), 1)
                    dve.wait_ge(sem("rel_stored"), g * 16 + 16)
                    nc.vector.memset(small[:, 0, 5, :], 0.0).then_inc(sem("rel_graph_done"), 1)

            with if_relations(dve):
                relations()

        @block.gpsimd
        def _(pool):
            def setup():
                nc.gpsimd.memset(ident[:, :], 0.0)
                nc.gpsimd.memset(excess_sum[:, :], 0.0)
                nc.gpsimd.memset(not_eye[:, :, :], 1.0).then_inc(sem("pool_setup"), 1)
                pool.wait_ge(sem("pool_setup"), 1)
                nc.gpsimd.affine_select(out=ident[:, :], in_=ident[:, :], compare_op=ALU.not_equal, fill=1.0,
                                        base=0, pattern=[[-1, P]], channel_multiplier=1)\
                    .then_inc(sem("consts_ready"), 1)
                for k in range(T):
                    last = nc.gpsimd.affine_select(out=not_eye[:, k, :], in_=not_eye[:, k, :],
                                                   compare_op=ALU.not_equal, fill=0.0, base=k * P,
                                                   pattern=[[-1, N]], channel_multiplier=1)
                last.then_inc(sem("pool_setup"), 1)
                pool.wait_ge(sem("pool_setup"), 2)

            def mask2(n, s, first):
                pool.wait_ge(sem("masks_ready"), n + 1)
                nc.gpsimd.tensor_tensor(neg2[:, s], neg0[:, s], not_eye[:, :, :], ALU.mult)\
                    .then_inc(sem("neg2_ready"), 1)

            def add_excess(n, s, first):
                pool.wait_ge(sem("excess_ready"), n + 1)
                nc.gpsimd.tensor_tensor(excess_sum[:, :], excess_sum[:, :], excess_row[:, s:s + 1], ALU.add)\
                    .then_inc(sem("excess_added"), 1)
                pool.wait_ge(sem("excess_added"), n + 1)

            def rsqrt(layer, n, s):
                wait_apart(pool, sem(f"mv{layer}_ready"), n + 1)
                nc.gpsimd.tensor_scalar(ve[:, s, :], mv[:, s, :, 1], 1.0, EPS, ALU.mult, ALU.add)\
                    .then_inc(sem(f"ve{layer}_ready"), 1)
                pool.wait_ge(sem(f"ve{layer}_ready"), n + 1)
                nc.gpsimd.tensor_tensor(rstd[:, s, :], ve[:, s, :], minus_half[:, :], ALU.pow)\
                    .then_inc(sem(f"rstd{layer}_ready"), 1)

            steps = [mask2, add_excess, lambda n, s, f: rsqrt(0, n, s), lambda n, s, f: rsqrt(1, n, s),
                     lambda n, s, f: rsqrt(2, n, s), lambda n, s, f: rsqrt(3, n, s)]

            def one_round(i, first):
                for step in steps:
                    for s in range(SLOTS):
                        step(i + s, s, first)

            def relations():
                with pool.Fori(0, B) as g:
                    wait_apart(pool, sem("rel_mv"), g + 1)
                    nc.gpsimd.tensor_scalar(ve[:, 0, :], mv[:, 0, :, 1], 1.0, EPS, ALU.mult, ALU.add)\
                        .then_inc(sem("rel_ve"), 1)
                    pool.wait_ge(sem("rel_ve"), g + 1)
                    nc.gpsimd.tensor_tensor(rstd[:, 0, :], ve[:, 0, :], minus_half[:, :], ALU.pow)\
                        .then_inc(sem("rel_rstd"), 1)

            setup()
            rounds(pool, one_round)
            nc.gpsimd.partition_all_reduce(excess_all[:, :], excess_sum[:, :], P, bass.bass_isa.ReduceOp.max)\
                .then_inc(sem("excess_all_ready"), 1)
            with if_relations(pool):
                relations()


_INS = ['x', 'adj', 'L0_gnn_W', 'L0_gnn_a', 'L1_gnn_W', 'L1_gnn_a_1', 'L1_gnn_a_2', 'L1_gnn_a_12', 'L1_gnn_W_1',
        'L1_gnn_W_2', 'L2_gnn_Wq', 'L2_gnn_bq', 'L2_gnn_Wk', 'L2_gnn_bk', 'L2_gnn_Wv', 'L2_gnn_bv', 'L2_gnn_Wo',
        'L2_gnn_bo', 'L3_gnn_W_fwd', 'L3_gnn_W_bwd', 'L3_gnn_W_loop', 'L3_gnn_Wg_fwd', 'L3_gnn_Wg_bwd',
        'L3_gnn_Wg_loop', 'L3_gnn_b_fwd', 'L3_gnn_b_bwd', 'L3_gnn_b_loop', 'L3_gnn_bg_fwd', 'L3_gnn_bg_bwd',
        'L3_gnn_bg_loop']


def kernel(**inputs):
    import numpy as _np
    import concourse.bacc as _bacc
    from concourse import mybir as _mybir
    from concourse.bass_utils import run_bass_kernel_spmd as _run

    nc = _bacc.Bacc("TRN2", target_bir_lowering=False, num_devices=1)
    arrays, args = {}, {}
    for name in _INS:
        a = _np.ascontiguousarray(inputs[name])
        arrays[f"in_{name}_dram"] = a
        args[name] = nc.dram_tensor(f"in_{name}_dram", a.shape, _mybir.dt.from_np(a.dtype),
                                    kind="ExternalInput").ap()
    shape = _np.shape(inputs["x"])
    out = nc.dram_tensor("out_0_dram", shape, _mybir.dt.float32, kind="ExternalOutput").ap()
    build(nc, args, out)
    r = _run(nc, [arrays], core_ids=[0])
    return r.results[0]["out_0_dram"]
```

```python
from contextlib import ExitStack

import numpy as np
import concourse.bass as bass
from concourse import mybir

F32 = mybir.dt.float32
BF16 = mybir.dt.bfloat16
I32 = mybir.dt.int32
ALU = mybir.AluOpType
ACT = mybir.ActivationFunctionType
AX = mybir.AxisListType

P = 128
SLOTS = 4
HEADS = 4
EPS = 1e-5
SLOPE = 0.2
NEG_INF = -1e30
NEG_L1 = -9e15
TINY = 1e-30
LOWEST = -3.0e38

PLAN = {
    "sync": [("load", 106), ("aside", 705), ("store", 724)],
    "tensor": [("xT0", 46), ("proj0", 60), ("pT0", 135), ("agg0", 150), ("xT1", 178), ("proj1", 184),
        ("scores1", 212), ("pT1", 285), ("agg1", 313), ("xT2", 368), ("proj2", 400), ("scores2a", 446),
        ("scores2b", 515), ("pT2a", 533), ("pT2b", 577), ("agg2", 595), ("o_nodes", 618), ("oT", 665),
        ("wo", 689), ("xT3", 717), ("proj3", 727), ("agg3", 739)],
    "scalar": [("c_xT0", 86), ("c_proj0", 110), ("exp0", 160), ("c_pT0", 167), ("c_xT1", 200), ("c_tT", 217),
        ("c_xw", 245), ("c_z", 267), ("test_adj", 286), ("exp1", 312), ("c_pT1", 346), ("c_elu", 356),
        ("c_xT2", 404), ("c_qk", 453), ("c_v", 489), ("exp2a", 545), ("exp2b", 561), ("c_pT2a", 579),
        ("c_pT2b", 623), ("c_oT", 648), ("c_onT", 712), ("c_xT3", 737), ("gate3", 754)],
    "vector": [("masks", 45), ("shift0", 58), ("max0", 92), ("sum0", 132), ("norm0", 142), ("shift1", 241),
        ("elu1", 281), ("sum1", 307), ("norm1", 336), ("q_dve", 424), ("shift2a", 454), ("shift2b", 492),
        ("rsum2", 599), ("norm_o", 625), ("sum2", 653), ("norm2", 680), ("vals3", 705), ("sum3", 754),
        ("norm3", 754)],
    "gpsimd": [("rstd0", 87), ("mask2", 206), ("rstd1", 277), ("excess", 337), ("rstd2", 646), ("rstd3", 714)],
}
CYCLE = 760

RINGS = ("tp", "mm", "big")
PSUM_USES = {
    "xT0": [("tp", "xT_sb0", 1, 0)],
    "proj0": [("mm", "rowmax0_ready", 1, 0), ("mm", "wh_sb", 1, 0)],
    "pT0": [("tp", "pT_sb0", 1, 0)],
    "agg0": [("mm", "agg0_read", 1, 0)],
    "xT1": [("tp", "xT_sb1", 1, 0)],
    "proj1": [("mm", "tT_sb", 1, 0), ("big", "xw_sb", 1, 0)],
    "scores1": [("mm", "z_sb", 1, 0)],
    "pT1": [("tp", "pT_sb1", 1, 0)],
    "agg1": [("mm", "agg1_read", 1, 0)],
    "xT2": [("tp", "xT_sb2", 1, 0)],
    "proj2": [("big", "qkv_sb", 2, 1)],
    "scores2a": [("big", "scores2_read", 2, 0)],
    "scores2b": [("big", "scores2_read", 2, 1)],
    "pT2a": [("tp", "pT_sb2", 4, 0), ("tp", "pT_sb2", 4, 1)],
    "pT2b": [("tp", "pT_sb2", 4, 2), ("tp", "pT_sb2", 4, 3)],
    "agg2": [("mm", "oT_sb", 1, 0)],
    "o_nodes": [("tp", "o_sb", 1, 0)],
    "oT": [("tp", "onT_sb", 1, 0)],
    "wo": [("mm", "wo_read", 1, 0)],
    "xT3": [("tp", "xT_sb3", 1, 0)],
    "proj3": [("mm", "vals_ready", 1, 0)],
    "agg3": [("mm", "agg3_read", 1, 0)],
}


def one_cycle(engine):
    order = []
    for k, (name, place) in enumerate(PLAN[engine]):
        for s in range(SLOTS):
            at = place + s * CYCLE // SLOTS
            order.append((at % CYCLE, s, at // CYCLE, k, name))
    return [(name, s, late) for _, s, late, _, name in sorted(order)]


def ring_uses(ring):
    return [(step, s, k, late, read, per, at)
            for step, s, late in one_cycle("tensor")
            for k, (r, read, per, at) in enumerate(PSUM_USES[step]) if r == ring]


def build(nc, t, out):
    B, N, D = t["x"].shape
    T = N // P
    DK = D // HEADS
    SCALE = 1.0 / float(np.sqrt(DK + 1e-09))
    NREL = t["L3_gnn_b_fwd"].shape[0]
    assert D == P and T == 2
    rings = {r: ring_uses(r) for r in RINGS}
    assert all(len(u) % 2 == 0 for u in rings.values())

    with ExitStack() as ctx:
        def sb(name, shape, dt=F32):
            return ctx.enter_context(nc.sbuf_tensor(name, shape, dt))

        sems = {}

        def sem(name):
            if name not in sems:
                sems[name] = ctx.enter_context(nc.semaphore(name))
            return sems[name]

        ident = sb("ident", [P, P])
        not_eye = sb("not_eye", [P, T, N], BF16)
        minus_half = sb("minus_half", [P, T])
        minus_one = sb("minus_one", [P, 1])
        w_in = sb("w_in", [P, 11, P])
        W0, W1L, A12, W_1, W_2, WQ, WK, WV, WO, WL, WGL = range(11)
        cols = sb("cols", [P, 8])
        A1, A2, L1A1, L1A2, BQ, BK, BV = range(7)
        w0T1 = sb("w0T1", [P, D + 1])
        w2rep = sb("w2rep", [P, P])
        wT = sb("wT", [P, 4, P])
        M1 = sb("M1", [P, P])
        u12 = sb("u12", [P, 2])
        xw_w = sb("xw_w", [P, 2 * D + 1])
        bv_rep = sb("bv_rep", [P, P])
        bo_row = sb("bo_row", [P, D])
        hg_w = sb("hg_w", [P, 2 * D])
        bias_part = sb("bias_part", [P, 3, 2 * D], BF16)
        hg_bias = sb("hg_bias", [P, 2 * D])
        ones_row = sb("ones_row", [P, P])
        ones_bf = sb("ones_bf", [P, P], BF16)
        bo_parts = sb("bo_parts", [P, D], BF16)
        hg_parts = sb("hg_parts", [P, 2 * D], BF16)
        excess_row = sb("excess_row", [P, SLOTS])
        excess_sum = sb("excess_sum", [P, 1])
        excess_all = sb("excess_all", [P, 1])
        excess_flag = sb("excess_flag", [P, 1], I32)

        x_in = sb("x_in", [P, SLOTS, T, D])
        adj_in = sb("adj_in", [P, SLOTS, T, N], I32)
        neg0 = sb("neg0", [P, SLOTS, T, N], BF16)
        neg1 = sb("neg1", [P, SLOTS, T, N], BF16)
        neg2 = sb("neg2", [P, SLOTS, T, N], BF16)
        eq1 = sb("eq1", [P, SLOTS, T, N])
        xT = sb("xT", [P, SLOTS, N])
        x1 = sb("x1", [P, SLOTS, T, D])
        x2 = sb("x2", [P, SLOTS, T, D])
        x3 = sb("x3", [P, SLOTS, T, D])
        y = sb("y", [P, SLOTS, T, D])
        stats = sb("stats", [P, SLOTS, T, 6])
        mv = sb("mv", [P, SLOTS, T, 2])
        ve = sb("ve", [P, SLOTS, T])
        rstd = sb("rstd", [P, SLOTS, T])
        xw = sb("xw", [P, SLOTS, T, 2 * D + 2])
        tT = sb("tT", [P, SLOTS, N])
        rowmax = sb("rowmax", [P, SLOTS, T])
        small = sb("small", [P, SLOTS, 6, T])
        rsum = sb("rsum", [P, SLOTS, T])
        hmid = sb("hmid", [P, SLOTS, T, D])
        hexp = sb("hexp", [P, SLOTS, T, D])
        qblk = sb("qblk", [P, SLOTS, HEADS, N])
        p2 = sb("p2", [P, SLOTS, T, HEADS, N])
        p2T = sb("p2T", [P, SLOTS, HEADS, T, N])
        sm, pa, pb, prob = (p2[:, :, :, :, :].rearrange("p s t h n -> p s (t h n)")[:, :, c * T * N:(c + 1) * T * N]
                            .rearrange("p s (t n) -> p s t n", t=T) for c in range(4))
        probT = p2T[:, :, 0]
        rowmax2 = sb("rowmax2", [P, SLOTS, T * HEADS])
        nmax2 = sb("nmax2", [P, SLOTS, T * HEADS])
        sum2 = sb("sum2", [P, SLOTS, T * HEADS])
        rsum2 = sb("rsum2", [P, SLOTS, T * HEADS])
        over_one = neg2
        kT, vn = tT, hexp
        oT = xT
        on, onT = hexp, tT
        gate = xw[:, :, :, 0:D]
        x4 = x1
        vals = hmid

        ps = ctx.enter_context(nc.psum_tensor("ps", [P, 8, 512], F32))
        FIRST_BANK = {"tp": 0, "mm": 2, "big": 4}

        def bank(step, s, k=0):
            for ring, uses in rings.items():
                for at, u in enumerate(uses):
                    if u[:3] == (step, s, k):
                        b = FIRST_BANK[ring] + (at % 2) * (2 if ring == "big" else 1)
                        return ps[:, b, :] if ring != "big" else ps[:, b:b + 2, :]
            raise KeyError((step, s, k))

        def bank_read(pe, step, s, k, n):
            for uses in rings.values():
                for at, u in enumerate(uses):
                    if u[:3] != (step, s, k):
                        continue
                    back = at
                    while True:
                        back -= 2
                        _, s_before, _, late_before, read, per, number = uses[back % len(uses)]
                        graph = n - s + SLOTS * (u[3] - late_before + back // len(uses)) + s_before
                        if not isinstance(graph, int) or 0 <= graph < B:
                            break
                        if graph < 0 and back < -len(uses):
                            return
                    pe.wait_ge(sem(read), graph * per + number + 1)

        x3_dram = nc.dram_tensor("x3_aside", (B, P, T * D), F32, kind="Internal").ap()

        x_v = t["x"].rearrange("b (t p) d -> b p t d", p=P)
        adj_v = t["adj"].rearrange("b (t p) j -> b p t j", p=P)
        out_v = out.rearrange("b (t p) d -> b p t d", p=P)
        loads = [
            (w_in[:, W0, :], t["L0_gnn_W"]),
            (cols[:, A1:A1 + 1], t["L0_gnn_a"][:, 0:D].rearrange("a p -> p a")),
            (cols[:, A2:A2 + 1], t["L0_gnn_a"][:, D:2 * D].rearrange("a p -> p a")),
            (w_in[:, W1L, :], t["L1_gnn_W"]), (w_in[:, A12, :], t["L1_gnn_a_12"]),
            (w_in[:, W_1, :], t["L1_gnn_W_1"]), (w_in[:, W_2, :], t["L1_gnn_W_2"]),
            (cols[:, L1A1:L1A1 + 1], t["L1_gnn_a_1"]), (cols[:, L1A2:L1A2 + 1], t["L1_gnn_a_2"]),
            (w_in[:, WQ, :], t["L2_gnn_Wq"]), (w_in[:, WK, :], t["L2_gnn_Wk"]),
            (w_in[:, WV, :], t["L2_gnn_Wv"]), (w_in[:, WO, :], t["L2_gnn_Wo"]),
            (cols[:, BQ:BQ + 1], t["L2_gnn_bq"].rearrange("(p a) -> p a", a=1)),
            (cols[:, BK:BK + 1], t["L2_gnn_bk"].rearrange("(p a) -> p a", a=1)),
            (cols[:, BV:BV + 1], t["L2_gnn_bv"].rearrange("(p a) -> p a", a=1)),
            (bo_row[:, :], t["L2_gnn_bo"].rearrange("(a d) -> a d", a=1).broadcast_to((P, D))),
            (w_in[:, WL, :], t["L3_gnn_W_loop"]), (w_in[:, WGL, :], t["L3_gnn_Wg_loop"]),
            (hg_bias[:, 0:D], t["L3_gnn_b_loop"].broadcast_to((P, D))),
            (hg_bias[:, D:2 * D], t["L3_gnn_bg_loop"].broadcast_to((P, D))),
        ]

        rel_w = qblk[:, 0, 0:2, :]
        rel_adj = adj_in[:, 0]
        rel_adj_f = eq1[:, 1]
        rel_adjT_f = eq1[:, 2]
        rel_hot = (eq1[:, 0], eq1[:, 3])
        rel_x = x1[:, 0]
        rel_xT = xT[:, 0]
        rel_hg = (p2[:, 0].rearrange("p t h n -> p (t h n)")[:, 0:3 * T * 2 * D]
                  .rearrange("p (w t d) -> p w t d", w=3, t=T))
        rel_bias = y
        rel_sum = xw
        rel_vals = (x2[:, 0], x2[:, 1])
        rel_acc = x2[:, 2]
        rel_out = x2[:, 3]
        rel_no = sb("rel_no", [P, 1])
        rel_biases = ((t["L3_gnn_b_fwd"], t["L3_gnn_bg_fwd"]), (t["L3_gnn_b_bwd"], t["L3_gnn_bg_bwd"]))
        rel_weights = [t["L3_gnn_W_fwd"], t["L3_gnn_W_bwd"], t["L3_gnn_Wg_fwd"], t["L3_gnn_Wg_bwd"]]

        def if_relations(engine):
            engine.wait_ge(sem("flag_ready"), 1)
            flag = engine.value_load(excess_flag[0:1, 0:1], min_val=0, max_val=1)
            return engine.If(flag != 0)

        block = ctx.enter_context(nc.Block())

        wait_registers = {}

        def wait_apart(engine, semaphore, value):
            if not isinstance(value, int):
                if engine not in wait_registers:
                    wait_registers[engine] = engine.alloc_register(f"awaited{len(wait_registers)}")
                engine.reg_alu(wait_registers[engine], value - 1, 1, ALU.add)
                value = wait_registers[engine]
            engine.wait_ge(sem("consts_ready"), 1)
            engine.wait_ge(semaphore, value)

        def rounds(engine, name, steps):
            def one_round(i):
                for step, s, late in one_cycle(name):
                    r = i - late
                    n = r * SLOTS + s
                    if isinstance(n, int) and not 0 <= n < B:
                        continue
                    steps[step](n, s, r)

            full = B // SLOTS
            one_round(0)
            one_round(1)
            with engine.Fori(2, full) as i:
                one_round(i)
            for i in range(full, (B - 1) // SLOTS + 2):
                one_round(i)

        def fresh(r):
            return isinstance(r, int) and r == 0

        @block.sync
        def _(sp):
            def load(n, s, r):
                if not fresh(r):
                    sp.wait_ge(sem("masks_ready"), n - SLOTS + 1)
                    sp.wait_ge(sem("excess_ready"), n - SLOTS + 1)
                    sp.wait_ge(sem("agg0_read"), n - SLOTS + 1)
                sp.dma_start(adj_in[:, s], adj_v[n]).then_inc(sem(f"adj_loaded{s}"), 16)
                sp.dma_start(x_in[:, s], x_v[n]).then_inc(sem(f"x_loaded{s}"), 16)
                if isinstance(n, int) and n == 0:
                    for dst, src in loads:
                        sp.dma_start(dst, src).then_inc(sem("weights_loaded"), 16)

            def aside(n, s, r):
                sp.wait_ge(sem("x3_ready"), n + 1)
                sp.dma_start(x3_dram[n], x3[:, s].rearrange("p t d -> p (t d)"))\
                    .then_inc(sem(f"x3_aside{s}"), 16)

            def store(n, s, r):
                sp.wait_ge(sem("x4_ready"), n + 1)
                sp.dma_start(out_v[n], x4[:, s]).then_inc(sem(f"stored{s}"), 16)

            rounds(sp, "sync", {"load": load, "aside": aside, "store": store})
            for s in range(SLOTS):
                sp.wait_ge(sem(f"stored{s}"), 16 * len(range(s, B, SLOTS)))
                sp.wait_ge(sem(f"x3_aside{s}"), 16 * len(range(s, B, SLOTS)))
            with if_relations(sp):
                for k, w in enumerate(rel_weights):
                    sp.dma_start(w_in[:, k, :], w).then_inc(sem("rel_w_loaded"), 16)
                with sp.Fori(0, B) as g:
                    sp.wait_ge(sem("rel_graph_done"), g + 1)
                    sp.dma_start(rel_adj, adj_v[g]).then_inc(sem("rel_loaded"), 16)
                    sp.dma_start(rel_x.rearrange("p t d -> p (t d)"), x3_dram[g]).then_inc(sem("rel_loaded"), 16)
                    with sp.Fori(0, NREL) as r:
                        sp.wait_ge(sem("rel_sums_ready"), g * NREL + r + 1)
                        for way in range(2):
                            for part in range(2):
                                sp.dma_start(rel_bias[:, way, part, :],
                                             rel_biases[way][part].rearrange("r (a d) -> r a d", a=1)[r].broadcast_to((P, D)))\
                                    .then_inc(sem("rel_bias_loaded"), 16)
                    sp.wait_ge(sem("rel_out_ready"), g + 1)
                    sp.dma_start(out_v[g], rel_out).then_inc(sem("rel_stored"), 16)
                sp.wait_ge(sem("rel_stored"), 16 * B)

        @block.tensor
        def _(pe):
            def setup():
                pe.wait_ge(sem("consts_ready"), 1)
                pe.wait_ge(sem("weights_loaded"), 16 * len(loads))
                for k, w in enumerate((W0, W1L, A12, WL)):
                    last = pe.transpose(ps[:, 0, k * P:(k + 1) * P], w_in[:, w, :], ident[:, :])
                last.then_inc(sem("setup_pe"), 1)
                pe.transpose(ps[:, 1, 0:P], w_in[:, WGL, :], ident[:, :])
                pe.matmul(ps[:, 1, P:P + 1], w_in[:, W0, :], cols[:, A1:A1 + 1], start=True, stop=True)
                pe.matmul(ps[:, 5, 0:1], w_in[:, W0, :], cols[:, A2:A2 + 1],
                          start=True, stop=True).then_inc(sem("setup_pe"), 1)
                pe.wait_ge(sem("bv_ready"), 1)
                pe.matmul(ps[:, 2, 0:D], bv_rep[:, :], w_in[:, WO, :], start=True, stop=True)\
                    .then_inc(sem("setup_pe"), 1)
                pe.wait_ge(sem("setup_t_sb"), 2)
                pe.matmul(ps[:, 3, 0:P], wT[:, 1, :], wT[:, 0, :], start=True, stop=True)
                pe.matmul(ps[:, 3, P:P + 2], wT[:, 0, :], cols[:, L1A1:L1A2 + 1], start=True, stop=True)
                pe.matmul(ps[:, 3, 2 * P:3 * P], w_in[:, WL, :], wT[:, 2, :], start=True, stop=True)\
                    .then_inc(sem("setup_pe"), 1)
                pe.wait_ge(sem("setup_t_sb"), 3)
                pe.matmul(ps[:, 4, 0:P], wT[:, 0, :], wT[:, 3, :], start=True, stop=True)\
                    .then_inc(sem("setup_pe"), 1)
                pe.wait_ge(sem("weights_ready"), 2)

            def transpose_x(layer, n, s, r, src):
                o = bank(f"xT{layer}", s)
                bank_read(pe, f"xT{layer}", s, 0, n)
                for k in range(T):
                    last = pe.transpose(o[:, k * P:(k + 1) * P], src[:, s, k, :], ident[:, :])
                last.then_inc(sem(f"xT_ps{layer}"), 1)

            def xT0(n, s, r):
                pe.wait_ge(sem(f"x_loaded{s}"), r * 16 + 16)
                transpose_x(0, n, s, r, x_in)

            def proj0(n, s, r):
                o, o2 = bank("proj0", s, 0), bank("proj0", s, 1)
                bank_read(pe, "proj0", s, 0, n)
                pe.wait_ge(sem("xT_sb0"), n + 1)
                pe.matmul(o[:, 0:N], w2rep[:, :], xT[:, s, :], start=True, stop=True).then_inc(sem("s2_ps"), 1)
                bank_read(pe, "proj0", s, 1, n)
                for k in range(T):
                    last = pe.matmul(o2[:, k * (D + 1):(k + 1) * (D + 1)], xT[:, s, k * P:(k + 1) * P],
                                     w0T1[:, :], start=True, stop=True)
                last.then_inc(sem("wh_ps"), 1)

            def transpose_p(layer, n, s, r):
                o = bank(f"pT{layer}", s)
                bank_read(pe, f"pT{layer}", s, 0, n)
                pe.wait_ge(sem(f"p_ready{layer}"), n + 1)
                for j in range(T):
                    for k in range(T):
                        last = pe.transpose(o[:, j * N + k * P:j * N + (k + 1) * P],
                                            prob[:, s, k, j * P:(j + 1) * P], ident[:, :])
                last.then_inc(sem(f"pT_ps{layer}"), 1)

            def aggregate(layer, n, s, r, values):
                o = bank(f"agg{layer}", s)
                bank_read(pe, f"agg{layer}", s, 0, n)
                pe.wait_ge(sem(f"pT_sb{layer}"), n + 1)
                for k in range(T):
                    for j in range(T):
                        last = pe.matmul(o[:, k * (D + 1):(k + 1) * (D + 1)],
                                         probT[:, s, j, k * P:(k + 1) * P], values(j),
                                         start=(j == 0), stop=(j == T - 1))
                last.then_inc(sem(f"agg{layer}_ps"), 1)

            def agg0(n, s, r):
                pe.wait_ge(sem("wh_sb"), n + 1)
                aggregate(0, n, s, r, lambda j: xw[:, s, j, D + 1:2 * D + 2])

            def xT1(n, s, r):
                pe.wait_ge(sem("x1_ready"), n + 1)
                transpose_x(1, n, s, r, x1)

            def proj1(n, s, r):
                o, o2 = bank("proj1", s, 0), bank("proj1", s, 1)
                pe.wait_ge(sem("xT_sb1"), n + 1)
                bank_read(pe, "proj1", s, 0, n)
                pe.matmul(o[:, 0:N], M1[:, :], xT[:, s, :], start=True, stop=True).then_inc(sem("tT_ps"), 1)
                bank_read(pe, "proj1", s, 1, n)
                for k in range(T):
                    last = pe.matmul(o2[:, k, 0:2 * D + 1], xT[:, s, k * P:(k + 1) * P], xw_w[:, :],
                                     start=True, stop=True)
                last.then_inc(sem("xw_ps"), 1)

            def scores1(n, s, r):
                o = bank("scores1", s)
                bank_read(pe, "scores1", s, 0, n)
                pe.wait_ge(sem("tT_sb"), n + 1)
                for k in range(T):
                    last = pe.matmul(o[:, k * N:(k + 1) * N], tT[:, s, k * P:(k + 1) * P], xT[:, s, :],
                                     start=True, stop=True)
                last.then_inc(sem("z_ps"), 1)

            def agg1(n, s, r):
                pe.wait_ge(sem("xw_sb"), n + 1)
                aggregate(1, n, s, r, lambda j: xw[:, s, j, D + 1:2 * D + 2])

            def xT2(n, s, r):
                pe.wait_ge(sem("x2_ready"), n + 1)
                transpose_x(2, n, s, r, x2)

            def proj2(n, s, r):
                o = bank("proj2", s)
                bank_read(pe, "proj2", s, 0, n)
                pe.wait_ge(sem("xT_sb2"), n + 1)
                pe.matmul(o[:, 0, 0:N], w_in[:, WQ, :], xT[:, s, :], start=True, stop=True)
                pe.matmul(o[:, 1, N:2 * N], w_in[:, WK, :], xT[:, s, :], start=True, stop=True)
                for k in range(T):
                    last = pe.matmul(o[:, 1, k * D:(k + 1) * D], xT[:, s, k * P:(k + 1) * P],
                                     w_in[:, WV, :], start=True, stop=True)
                last.then_inc(sem("qkv_ps"), 1)

            def scores2(k, n, s):
                step = "scores2" + "ab"[k]
                o = bank(step, s)
                pe.wait_ge(sem("qkv_sb"), n * 2 + 1)
                pe.wait_ge(sem("q_sb"), n + 1)
                bank_read(pe, step, s, 0, n)
                for h in range(HEADS):
                    last = pe.matmul(o[:, h // 2, (h % 2) * N:(h % 2 + 1) * N],
                                     qblk[:, s, h, k * P:(k + 1) * P], kT[:, s, :], start=True, stop=True)
                last.then_inc(sem("scores2_ps"), 1)

            def pT2(k, n, s):
                step = "pT2" + "ab"[k]
                pe.wait_ge(sem("p_ready2"), n * T + k + 1)
                for j in range(T):
                    o = bank(step, s, j)
                    bank_read(pe, step, s, j, n)
                    for h in range(HEADS):
                        last = pe.transpose(o[:, h * P:(h + 1) * P], p2[:, s, k, h, j * P:(j + 1) * P],
                                            ident[:, :])
                    last.then_inc(sem("pT_ps2"), 1)

            def agg2(n, s, r):
                o = bank("agg2", s)
                bank_read(pe, "agg2", s, 0, n)
                pe.wait_ge(sem("pT_sb2"), n * 4 + 4)
                pe.wait_ge(sem("qkv_sb"), n * 2 + 2)
                for j in range(T):
                    for h in range(HEADS):
                        last = pe.matmul(o[h * DK:(h + 1) * DK, 0:N], vn[:, s, j, h * DK:(h + 1) * DK],
                                         p2T[:, s, h, j, :], start=(j == 0), stop=(j == T - 1))
                last.then_inc(sem("agg2_ps"), 1)

            def o_nodes(n, s, r):
                o = bank("o_nodes", s)
                bank_read(pe, "o_nodes", s, 0, n)
                pe.wait_ge(sem("oT_sb"), n + 1)
                for k in range(T):
                    last = pe.transpose(o[:, k * P:(k + 1) * P], oT[:, s, k * P:(k + 1) * P], ident[:, :])
                last.then_inc(sem("o_nodes_ps"), 1)

            def oT_(n, s, r):
                o = bank("oT", s)
                bank_read(pe, "oT", s, 0, n)
                pe.wait_ge(sem("o_sb"), n + 1)
                for k in range(T):
                    last = pe.transpose(o[:, k * P:(k + 1) * P], on[:, s, k, :], ident[:, :])
                last.then_inc(sem("onT_ps"), 1)

            def wo(n, s, r):
                o = bank("wo", s)
                bank_read(pe, "wo", s, 0, n)
                pe.wait_ge(sem("onT_sb"), n + 1)
                for k in range(T):
                    pe.matmul(o[:, k * D:(k + 1) * D], onT[:, s, k * P:(k + 1) * P], w_in[:, WO, :],
                              start=True, stop=False)
                    last = pe.matmul(o[:, k * D:(k + 1) * D], ones_bf[:, :], bo_parts[:, :],
                                     start=False, stop=True)
                last.then_inc(sem("wo_ps"), 1)

            def xT3(n, s, r):
                pe.wait_ge(sem("x3_ready"), n + 1)
                transpose_x(3, n, s, r, x3)

            def proj3(n, s, r):
                o = bank("proj3", s)
                bank_read(pe, "proj3", s, 0, n)
                pe.wait_ge(sem("xT_sb3"), n + 1)
                for k in range(T):
                    pe.matmul(o[:, k * 2 * D:(k + 1) * 2 * D], xT[:, s, k * P:(k + 1) * P], hg_w[:, :],
                              start=True, stop=False)
                    last = pe.matmul(o[:, k * 2 * D:(k + 1) * 2 * D], ones_bf[:, :], hg_parts[:, :],
                                     start=False, stop=True)
                last.then_inc(sem("hg_ps"), 1)

            def agg3(n, s, r):
                o = bank("agg3", s)
                bank_read(pe, "agg3", s, 0, n)
                pe.wait_ge(sem("vals_ready"), n + 1)
                for k in range(T):
                    for j in range(T):
                        last = pe.matmul(o[:, k * D:(k + 1) * D], eq1[:, s, j, k * P:(k + 1) * P],
                                         vals[:, s, j, :], start=(j == 0), stop=(j == T - 1))
                last.then_inc(sem("agg3_ps"), 1)

            steps = {
                "xT0": xT0, "proj0": proj0, "pT0": lambda *a: transpose_p(0, *a), "agg0": agg0,
                "xT1": xT1, "proj1": proj1, "scores1": scores1, "pT1": lambda *a: transpose_p(1, *a),
                "agg1": agg1, "xT2": xT2, "proj2": proj2,
                "scores2a": lambda n, s, r: scores2(0, n, s), "scores2b": lambda n, s, r: scores2(1, n, s),
                "pT2a": lambda n, s, r: pT2(0, n, s), "pT2b": lambda n, s, r: pT2(1, n, s),
                "agg2": agg2, "o_nodes": o_nodes, "oT": oT_, "wo": wo, "xT3": xT3, "proj3": proj3,
                "agg3": agg3,
            }

            def relations():
                pe.wait_ge(sem("x4_ready"), B)
                pe.wait_ge(sem("rel_w_loaded"), 16 * len(rel_weights))
                for k in range(4):
                    last = pe.transpose(ps[:, 0, k * P:(k + 1) * P], w_in[:, k, :], ident[:, :])
                last.then_inc(sem("rel_setup_pe"), 1)
                pe.wait_ge(sem("rel_setup_sb"), 1)
                for way in range(2):
                    last = pe.matmul(ps[:, 1, way * P:(way + 1) * P], w_in[:, way, :], wT[:, way, :],
                                     start=True, stop=True)
                last.then_inc(sem("rel_setup_pe"), 1)
                pe.wait_ge(sem("rel_setup_sb"), 2)
                with pe.Fori(0, B) as g:
                    pe.wait_ge(sem("rel_adj_f_ready"), g + 1)
                    for j in range(T):
                        for k in range(T):
                            pe.transpose(ps[:, 0, j * N + k * P:j * N + (k + 1) * P],
                                         rel_adj_f[:, k, j * P:(j + 1) * P], ident[:, :])
                    for k in range(T):
                        last = pe.transpose(ps[:, 1, k * P:(k + 1) * P], rel_x[:, k, :], ident[:, :])
                    last.then_inc(sem("rel_T_ps"), 1)
                    pe.wait_ge(sem("rel_T_sb"), g + 1)
                    for way, w in enumerate((rel_w[:, 0, :], rel_w[:, 1, :], hg_w[:, :])):
                        for k in range(T):
                            last = pe.matmul(ps[:, 2 + way, k * 2 * D:(k + 1) * 2 * D],
                                             rel_xT[:, k * P:(k + 1) * P], w, start=True, stop=True)
                    last.then_inc(sem("rel_hg_ps"), 1)
                    pe.wait_ge(sem("rel_loop_vals"), g + 1)
                    for k in range(T):
                        for j in range(T):
                            last = pe.matmul(ps[:, 5, k * D:(k + 1) * D], rel_hot[0][:, j, k * P:(k + 1) * P],
                                             rel_vals[0][:, j, :], start=(j == 0), stop=(j == T - 1))
                    last.then_inc(sem("rel_loop_ps"), 1)
                    with pe.Fori(0, NREL) as r:
                        pe.wait_ge(sem("rel_vals_ready"), g * NREL + r + 1)
                        for k in range(T):
                            for way in range(2):
                                for j in range(T):
                                    last = pe.matmul(ps[:, 6, k * D:(k + 1) * D],
                                                     rel_hot[way][:, j, k * P:(k + 1) * P],
                                                     rel_vals[way][:, j, :], start=(way + j == 0),
                                                     stop=(way == 1 and j == T - 1))
                        last.then_inc(sem("rel_ps"), 1)
                        pe.wait_ge(sem("rel_added"), g * NREL + r + 1)

            setup()
            rounds(pe, "tensor", steps)
            with if_relations(pe):
                relations()

        @block.scalar
        def _(act):
            def setup():
                act.wait_ge(sem("minus_one_ready"), 1)
                act.wait_ge(sem("setup_pe"), 1)
                nc.scalar.copy(w0T1[:, 0:D], ps[:, 0, 0:P])
                nc.scalar.copy(wT[:, 0:2, :].rearrange("p a n -> p (a n)"), ps[:, 0, P:3 * P])\
                    .then_inc(sem("setup_t_sb"), 1)
                nc.scalar.mul(hg_w[:, 0:D], ps[:, 0, 3 * P:4 * P], 0.5)
                act.wait_ge(sem("setup_pe"), 2)
                nc.scalar.copy(w0T1[:, D:D + 1], ps[:, 1, P:P + 1])
                nc.scalar.copy(wT[:, 2, :], ps[:, 1, 0:P]).then_inc(sem("setup_t_sb"), 1)
                act.wait_ge(sem("setup_pe"), 4)
                nc.scalar.copy(wT[:, 3, :], ps[:, 3, 0:P]).then_inc(sem("setup_t_sb"), 1)
                nc.scalar.copy(u12[:, :], ps[:, 3, P:P + 2])
                nc.scalar.copy(xw_w[:, D:D + 1], ps[:, 3, P + 1:P + 2])
                nc.scalar.copy(hg_w[:, D:2 * D], ps[:, 3, 2 * P:3 * P])
                nc.scalar.copy(xw_w[:, 0:D], w_in[:, W_1, :])
                nc.scalar.copy(xw_w[:, D + 1:2 * D + 1], w_in[:, W_2, :])
                act.wait_ge(sem("setup_pe"), 5)
                nc.scalar.copy(M1[:, :], ps[:, 4, 0:P]).then_inc(sem("weights_ready"), 1)

            def test_adj(n, s, r):
                act.wait_ge(sem(f"adj_loaded{s}"), r * 16 + 16)
                if not fresh(r):
                    act.wait_ge(sem("excess_added"), n - SLOTS + 1)
                nc.scalar.activation(over_one[:, s], adj_in[:, s], ACT.Relu, bias=minus_one[:, 0:1],
                                     accum_out=excess_row[:, s:s + 1]).then_inc(sem("excess_ready"), 1)

            def copy_xT(layer, n, s):
                act.wait_ge(sem(f"xT_ps{layer}"), n + 1)
                nc.scalar.copy(xT[:, s, :], bank(f"xT{layer}", s)[:, 0:N]).then_inc(sem(f"xT_sb{layer}"), 1)

            def proj0(n, s, r):
                act.wait_ge(sem("wh_ps"), n + 1)
                o = bank("proj0", s, 1)[:, 0:T * (D + 1)].rearrange("p (t d) -> p t d", t=T)
                nc.scalar.copy(xw[:, s, :, D:D + 1], o[:, :, D:D + 1])
                nc.scalar.copy(xw[:, s, :, D + 1:2 * D + 1], o[:, :, 0:D]).then_inc(sem("wh_sb"), 1)

            def pT0(n, s, r):
                act.wait_ge(sem("shift0_ready"), n + 1)
                for k in range(T):
                    nc.scalar.activation(pa[:, s, k, :], sm[:, s, k, :], ACT.Exp, bias=small[:, s, 2, k:k + 1])
                    last = nc.scalar.activation(pb[:, s, k, :], sm[:, s, k, :], ACT.Exp,
                                                bias=small[:, s, 3, k:k + 1], scale=SLOPE)
                last.then_inc(sem("branches_ready"), 1)

            def agg0(n, s, r):
                act.wait_ge(sem("pT_ps0"), n + 1)
                nc.scalar.copy(probT[:, s].rearrange("p t n -> p (t n)"), bank("pT0", s))\
                    .then_inc(sem("pT_sb0"), 1)

            def proj1(n, s, r):
                act.wait_ge(sem("tT_ps"), n + 1)
                nc.scalar.activation(tT[:, s, :], bank("proj1", s, 0)[:, 0:N], ACT.Identity,
                                     bias=u12[:, 0:1]).then_inc(sem("tT_sb"), 1)

            def copy_xw(n, s, r):
                act.wait_ge(sem("xw_ps"), n + 1)
                nc.scalar.copy(xw[:, s, :, 0:2 * D + 1], bank("proj1", s, 1)[:, :, 0:2 * D + 1])\
                    .then_inc(sem("xw_sb"), 1)

            def scores1(n, s, r):
                act.wait_ge(sem("z_ps"), n + 1)
                act.wait_ge(sem("xw_sb"), n + 1)
                for k in range(T):
                    last = nc.scalar.activation(pa[:, s, k, :], bank("scores1", s)[:, k * N:(k + 1) * N],
                                                ACT.Identity, bias=xw[:, s, k, D:D + 1])
                last.then_inc(sem("z_sb"), 1)

            def pT1(n, s, r):
                act.wait_ge(sem("shift1_ready"), n + 1)
                for k in range(T):
                    last = nc.scalar.activation(prob[:, s, k, :], sm[:, s, k, :], ACT.Exp,
                                                bias=small[:, s, 0, k:k + 1])
                last.then_inc(sem("p_ready1"), 1)

            def agg1(n, s, r):
                act.wait_ge(sem("pT_ps1"), n + 1)
                nc.scalar.copy(probT[:, s].rearrange("p t n -> p (t n)"), bank("pT1", s))\
                    .then_inc(sem("pT_sb1"), 1)

            def elu1(n, s, r):
                act.wait_ge(sem("agg1_read"), n + 1)
                nc.scalar.activation(hexp[:, s], hmid[:, s], ACT.Exp).then_inc(sem("hexp_ready"), 1)

            def proj2(n, s, r):
                act.wait_ge(sem("qkv_ps"), n + 1)
                o = bank("proj2", s)
                for h in range(2):
                    r = slice(h * DK, (h + 1) * DK)
                    nc.scalar.activation(qblk[r, s, h, :], o[r, 0, 0:N], ACT.Identity, bias=cols[r, BQ:BQ + 1])
                nc.scalar.activation(kT[:, s, :], o[:, 1, N:2 * N], ACT.Identity, bias=cols[:, BK:BK + 1])\
                    .then_inc(sem("qkv_sb"), 1)

            def copy_v(n, s, r):
                act.wait_ge(sem("q_sb"), n + 1)
                o = bank("proj2", s)
                nc.scalar.copy(vn[:, s].rearrange("p t d -> p (t d)"), o[:, 1, 0:T * D])\
                    .then_inc(sem("qkv_sb"), 1)

            def exp2(k, n, s):
                act.wait_ge(sem("shift2_ready"), n * T + k + 1)
                for h in range(HEADS):
                    c = k * HEADS + h
                    last = nc.scalar.activation(p2[:, s, k, h, :], p2[:, s, k, h, :], ACT.Exp,
                                                bias=nmax2[:, s, c:c + 1], scale=SCALE,
                                                accum_out=sum2[:, s, c:c + 1])
                last.then_inc(sem("p_ready2"), 1)

            def pT2(k, n, s):
                for j in range(T):
                    act.wait_ge(sem("pT_ps2"), n * 4 + k * T + j + 1)
                    nc.scalar.copy(p2T[:, s, :, j, k * P:(k + 1) * P],
                                   bank("pT2" + "ab"[k], s, j).rearrange("p (h i) -> p h i", h=HEADS))\
                        .then_inc(sem("pT_sb2"), 1)

            def agg2(n, s, r):
                act.wait_ge(sem("agg2_ps"), n + 1)
                nc.scalar.copy(oT[:, s, :], bank("agg2", s)[:, 0:N]).then_inc(sem("oT_sb"), 1)

            def oT_(n, s, r):
                act.wait_ge(sem("onT_ps"), n + 1)
                nc.scalar.copy(onT[:, s, :], bank("oT", s)[:, 0:N]).then_inc(sem("onT_sb"), 1)

            def gate3(n, s, r):
                act.wait_ge(sem("hg_ps"), n + 1)
                o = bank("proj3", s).rearrange("p (t d) -> p t d", t=T)
                nc.scalar.activation(gate[:, s], o[:, :, D:2 * D], ACT.Tanh, scale=0.5)\
                    .then_inc(sem("gate_ready"), 1)

            steps = {
                "test_adj": test_adj, "c_xT0": lambda n, s, r: copy_xT(0, n, s), "c_proj0": proj0, "exp0": pT0,
                "c_pT0": agg0, "c_xT1": lambda n, s, r: copy_xT(1, n, s), "c_tT": proj1, "c_xw": copy_xw,
                "c_z": scores1, "exp1": pT1, "c_pT1": agg1, "c_elu": elu1,
                "c_xT2": lambda n, s, r: copy_xT(2, n, s), "c_qk": proj2, "c_v": copy_v,
                "exp2a": lambda n, s, r: exp2(0, n, s), "exp2b": lambda n, s, r: exp2(1, n, s),
                "c_pT2a": lambda n, s, r: pT2(0, n, s), "c_pT2b": lambda n, s, r: pT2(1, n, s),
                "c_oT": agg2, "c_onT": oT_, "c_xT3": lambda n, s, r: copy_xT(3, n, s), "gate3": gate3,
            }

            def relations():
                act.wait_ge(sem("rel_setup_pe"), 1)
                for way in range(2):
                    nc.scalar.mul(rel_w[:, way, 0:D], ps[:, 0, way * P:(way + 1) * P], 0.5)
                nc.scalar.copy(wT[:, 0:2, :].rearrange("p a n -> p (a n)"), ps[:, 0, 2 * P:4 * P])\
                    .then_inc(sem("rel_setup_sb"), 1)
                act.wait_ge(sem("rel_setup_pe"), 2)
                nc.scalar.copy(rel_w[:, :, D:2 * D], ps[:, 1, 0:2 * P].rearrange("p (a n) -> p a n", a=2))\
                    .then_inc(sem("rel_setup_sb"), 1)
                with act.Fori(0, B) as g:
                    act.wait_ge(sem("rel_T_ps"), g + 1)
                    nc.scalar.copy(rel_adjT_f.rearrange("p t n -> p (t n)"), ps[:, 0, :])
                    nc.scalar.copy(rel_xT, ps[:, 1, 0:N]).then_inc(sem("rel_T_sb"), 1)
                    act.wait_ge(sem("rel_hg_ps"), g + 1)
                    nc.scalar.copy(rel_hg[:, 0:3].rearrange("p w t d -> p w (t d)"), ps[:, 2:5, :])\
                        .then_inc(sem("rel_hg_sb"), 1)
                    act.wait_ge(sem("rel_loop_sum"), g + 1)
                    nc.scalar.activation(rel_hg[:, 2, :, D:2 * D], rel_hg[:, 2, :, D:2 * D], ACT.Tanh, scale=0.5)\
                        .then_inc(sem("rel_loop_gate"), 1)
                    with act.Fori(0, NREL) as r:
                        act.wait_ge(sem("rel_sums_ready"), g * NREL + r + 2)
                        for way in range(2):
                            last = nc.scalar.activation(rel_sum[:, way, :, D:2 * D], rel_sum[:, way, :, D:2 * D],
                                                        ACT.Tanh, scale=0.5)
                        last.then_inc(sem("rel_gates"), 1)

            setup()
            rounds(act, "scalar", steps)
            with if_relations(act):
                relations()

        @block.vector
        def _(dve):
            def done(ins, signal, value, apart=False):
                ins.then_inc(sem(signal), 1)
                if apart:
                    wait_apart(dve, sem(signal), value)
                else:
                    dve.wait_ge(sem(signal), value)

            def setup():
                nc.vector.memset(ones_row[:, :], 1.0).then_inc(sem("ones_ready"), 1)
                nc.vector.memset(minus_half[:, :], -0.5)
                nc.vector.memset(minus_one[:, :], -1.0).then_inc(sem("minus_one_ready"), 1)
                nc.vector.memset(xw[:, :, :, 2 * D + 1:2 * D + 2], 1.0)
                nc.vector.memset(ones_bf[:, :], 1.0)
                dve.wait_ge(sem("ones_ready"), 1)
                dve.wait_ge(sem("weights_loaded"), 16 * len(loads))
                nc.vector.tensor_scalar(bv_rep[:, :], ones_row[:, :], cols[:, BV:BV + 1], None, ALU.mult)\
                    .then_inc(sem("bv_ready"), 1)
                done(nc.vector.tensor_scalar(hg_bias[:, 0:D], hg_bias[:, 0:D], 0.5, None, ALU.mult),
                     "hg_bias_ready", 1)
                dve.wait_ge(sem("setup_pe"), 2)
                nc.vector.tensor_scalar(w2rep[:, :], ones_row[:, :], ps[:, 5, 0:1], None, ALU.mult)
                dve.wait_ge(sem("setup_pe"), 3)
                done(nc.vector.tensor_tensor(bo_row[:, :], ps[:, 2, 0:D], bo_row[:, :], ALU.add),
                     "bias_row_ready", 1)
                dve.wait_ge(sem("consts_ready"), 1)

                def split(dst, row, width, steps_before):
                    part = p2[:, 0, 0, 0:3, 0:width]
                    at = steps_before
                    low = [bias_part[:, k, 0:width] for k in range(3)]
                    done(nc.vector.tensor_copy(low[0], row), "split_step", at + 1)
                    done(nc.vector.tensor_tensor(part[:, 0, :], row, low[0], ALU.subtract), "split_step", at + 2)
                    done(nc.vector.tensor_copy(low[1], part[:, 0, :]), "split_step", at + 3)
                    done(nc.vector.tensor_tensor(part[:, 1, :], part[:, 0, :], low[1], ALU.subtract),
                         "split_step", at + 4)
                    done(nc.vector.tensor_copy(low[2], part[:, 1, :]), "split_step", at + 5)
                    done(nc.vector.tensor_scalar(dst, low[0], ident[:, 0:1], None, ALU.mult), "split_step", at + 6)
                    for k in (1, 2):
                        done(nc.vector.scalar_tensor_tensor(out=dst, in0=low[k], scalar=ident[:, k:k + 1], in1=dst,
                                                            op0=ALU.mult, op1=ALU.add), "split_step", at + 6 + k)
                    return at + 8

                at = split(bo_parts[:, :], bo_row[:, :], D, 0)
                split(hg_parts[:, :], hg_bias[:, :], 2 * D, at)
                nc.vector.memset(qblk[:, :, :, :], 0.0).then_inc(sem("weights_ready"), 1)

            def masks(n, s, r):
                dve.wait_ge(sem(f"adj_loaded{s}"), r * 16 + 16)
                nc.vector.tensor_scalar(neg0[:, s], adj_in[:, s], 0.0, NEG_INF, ALU.is_equal, ALU.mult)
                nc.vector.tensor_scalar(neg1[:, s], adj_in[:, s], 0.0, NEG_L1, ALU.is_le, ALU.mult)
                nc.vector.tensor_scalar(eq1[:, s], adj_in[:, s], 1.0, None, ALU.is_equal)\
                    .then_inc(sem("masks_ready"), 1)

            def moments(layer, n, s):
                for k in range(T):
                    last = nc.vector.bn_stats(stats[:, s, k, :], y[:, s, k, :])
                done(last, f"stats{layer}_ready", n + 1, apart=True)
                for k in range(T):
                    last = nc.vector.bn_aggr(mv[:, s, k, :], stats[:, s, k, :])
                last.then_inc(sem(f"mv{layer}_ready"), 1)

            def norm(layer, n, s, r):
                dst = (x1, x2, x3, x4)[layer]
                if not fresh(r) and layer in (0, 2):
                    dve.wait_ge(sem(f"stored{s}" if layer == 0 else f"x3_aside{s}"), r * 16)
                dve.wait_ge(sem(f"rstd{layer}_ready"), n + 1)
                for k in range(T):
                    last = nc.vector.tensor_scalar(dst[:, s, k, :], y[:, s, k, :], mv[:, s, k, 0:1],
                                                   rstd[:, s, k:k + 1], ALU.subtract, ALU.mult)
                last.then_inc(sem(f"x{layer + 1}_ready"), 1)

            def shift0(n, s, r):
                dve.wait_ge(sem("masks_ready"), n + 1)
                wait_apart(dve, sem("s2_ps"), n + 1)
                o = bank("proj0", s)
                for k in range(T):
                    last = nc.vector.tensor_tensor_reduce(sm[:, s, k, :], o[:, 0:N], neg0[:, s, k, :], 1.0, LOWEST,
                                                          ALU.add, ALU.max, rowmax[:, s, k:k + 1])
                done(last, "rowmax0_ready", n + 1)
                dve.wait_ge(sem("wh_sb"), n + 1)
                s1 = xw[:, s, :, D]
                done(nc.vector.scalar_tensor_tensor(out=small[:, s, 0, :], in0=rowmax[:, s, :], scalar=0.1 * NEG_INF,
                                                    in1=s1, op0=ALU.max, op1=ALU.add), "s12_ready", n + 1)
                done(nc.vector.scalar_tensor_tensor(out=small[:, s, 1, :], in0=small[:, s, 0, :], scalar=SLOPE,
                                                    in1=small[:, s, 0, :], op0=ALU.mult, op1=ALU.max),
                     "m0_ready", n + 1)
                nc.vector.tensor_tensor(small[:, s, 2, :], s1, small[:, s, 1, :], ALU.subtract)
                nc.vector.scalar_tensor_tensor(out=small[:, s, 3, :], in0=s1, scalar=SLOPE, in1=small[:, s, 1, :],
                                               op0=ALU.mult, op1=ALU.subtract).then_inc(sem("shift0_ready"), 1)

            def row_sums(n, s, o):
                done(nc.vector.tensor_scalar(small[:, s, 4, :], o[:, :, D], TINY, None, ALU.max),
                     "sum0_ready", n + 1)
                done(nc.vector.reciprocal(rsum[:, s, :], small[:, s, 4, :]), "rsum0_ready", n + 1)

            def max0(n, s, r):
                dve.wait_ge(sem("branches_ready"), n + 1)
                nc.vector.tensor_tensor(prob[:, s], pa[:, s], pb[:, s], ALU.max).then_inc(sem("p_ready0"), 1)

            def norm0(n, s, r):
                dve.wait_ge(sem("agg0_ps"), n + 1)
                o = bank("agg0", s)[:, 0:T * (D + 1)].rearrange("p (t d) -> p t d", t=T)
                row_sums(n, s, o)
                for k in range(T):
                    last = nc.vector.scalar_tensor_tensor(out=y[:, s, k, :], in0=o[:, k, 0:D], scalar=rsum[:, s, k:k + 1],
                                                          in1=x_in[:, s, k, :], op0=ALU.mult, op1=ALU.add)
                last.then_inc(sem("agg0_read"), 1)
                dve.wait_ge(sem("agg0_read"), n + 1)
                moments(0, n, s)

            def shift1(n, s, r):
                dve.wait_ge(sem("z_sb"), n + 1)
                done(nc.vector.scalar_tensor_tensor(out=pb[:, s], in0=pa[:, s], scalar=SLOPE, in1=pa[:, s],
                                                    op0=ALU.mult, op1=ALU.max),
                     "leaky1_ready", n + 1, apart=True)
                for k in range(T):
                    last = nc.vector.tensor_tensor_reduce(sm[:, s, k, :], pb[:, s, k, :], neg1[:, s, k, :], 1.0, LOWEST,
                                                          ALU.add, ALU.max, rowmax[:, s, k:k + 1])
                done(last, "rowmax1_ready", n + 1)
                nc.vector.tensor_scalar(small[:, s, 0, :], rowmax[:, s, :], -1.0, None, ALU.mult)\
                    .then_inc(sem("shift1_ready"), 1)

            def elu1(n, s, r):
                dve.wait_ge(sem("agg1_ps"), n + 1)
                o = bank("agg1", s)[:, 0:T * (D + 1)].rearrange("p (t d) -> p t d", t=T)
                done(nc.vector.reciprocal(rsum[:, s, :], o[:, :, D]), "rsum1_ready", n + 1)
                for k in range(T):
                    last = nc.vector.scalar_tensor_tensor(out=hmid[:, s, k, :], in0=o[:, k, 0:D], scalar=rsum[:, s, k:k + 1],
                                                          in1=xw[:, s, k, 0:D], op0=ALU.mult, op1=ALU.add)
                last.then_inc(sem("agg1_read"), 1)
                dve.wait_ge(sem("agg1_read"), n + 1)
                nc.vector.scalar_tensor_tensor(out=y[:, s], in0=hmid[:, s], scalar=0.0, in1=x1[:, s],
                                               op0=ALU.max, op1=ALU.add).then_inc(sem("hpos_ready"), 1)

            def norm1(n, s, r):
                dve.wait_ge(sem("hexp_ready"), n + 1)
                dve.wait_ge(sem("hpos_ready"), n + 1)
                done(nc.vector.scalar_tensor_tensor(out=y[:, s], in0=hexp[:, s], scalar=1.0, in1=y[:, s],
                                                    op0=ALU.min, op1=ALU.add), "y1_ready", n + 1)
                moments(1, n, s)

            def proj2(n, s, r):
                dve.wait_ge(sem("qkv_ps"), n + 1)
                o = bank("proj2", s)
                for h in range(2, 4):
                    r = slice(h * DK, (h + 1) * DK)
                    last = nc.vector.tensor_scalar(qblk[r, s, h, :], o[r, 0, 0:N], cols[r, BQ:BQ + 1], None, ALU.add)
                last.then_inc(sem("q_sb"), 1)

            def shift2(k, n, s):
                dve.wait_ge(sem("neg2_ready"), n + 1)
                wait_apart(dve, sem("scores2_ps"), n * T + k + 1)
                o = bank("scores2" + "ab"[k], s)
                for h in range(HEADS):
                    c = k * HEADS + h
                    last = nc.vector.tensor_tensor_reduce(
                        p2[:, s, k, h, :], o[:, h // 2, (h % 2) * N:(h % 2 + 1) * N], neg2[:, s, k, :], 1.0, LOWEST,
                        ALU.add, ALU.max, rowmax2[:, s, c:c + 1])
                last.then_inc(sem("scores2_read"), 1)
                dve.wait_ge(sem("scores2_read"), n * T + k + 1)
                nc.vector.tensor_scalar(nmax2[:, s, k * HEADS:(k + 1) * HEADS],
                                        rowmax2[:, s, k * HEADS:(k + 1) * HEADS], -SCALE, None, ALU.mult)\
                    .then_inc(sem("shift2_ready"), 1)

            def rsum2_(n, s, r):
                dve.wait_ge(sem("p_ready2"), n * T + T)
                nc.vector.reciprocal(rsum2[:, s, :], sum2[:, s, :]).then_inc(sem("rsum2_ready"), 1)

            def o_nodes(n, s, r):
                dve.wait_ge(sem("o_nodes_ps"), n + 1)
                dve.wait_ge(sem("rsum2_ready"), n + 1)
                o = bank("o_nodes", s)[:, 0:N].rearrange("p (c d) -> p c d", c=T * HEADS)
                r = rsum2[:, s, :].rearrange("p (c a) -> p c a", a=1).to_broadcast([P, T * HEADS, DK])
                nc.vector.tensor_tensor(on[:, s].rearrange("p t (h d) -> p (t h) d", h=HEADS), o, r, ALU.mult)\
                    .then_inc(sem("o_sb"), 1)

            def norm2(n, s, r):
                dve.wait_ge(sem("wo_ps"), n + 1)
                o = bank("wo", s)[:, 0:T * D].rearrange("p (t d) -> p t d", t=T)
                nc.vector.scalar_tensor_tensor(out=y[:, s], in0=o, scalar=0.0, in1=x2[:, s],
                                               op0=ALU.max, op1=ALU.add).then_inc(sem("wo_read"), 1)
                dve.wait_ge(sem("wo_read"), n + 1)
                moments(2, n, s)

            def vals3(n, s, r):
                dve.wait_ge(sem("gate_ready"), n + 1)
                o = bank("proj3", s).rearrange("p (t d) -> p t d", t=T)
                nc.vector.scalar_tensor_tensor(out=vals[:, s], in0=gate[:, s], scalar=1.0, in1=o[:, :, 0:D],
                                               op0=ALU.add, op1=ALU.mult).then_inc(sem("vals_ready"), 1)

            def norm3(n, s, r):
                dve.wait_ge(sem("agg3_ps"), n + 1)
                o = bank("agg3", s)[:, 0:T * D].rearrange("p (t d) -> p t d", t=T)
                nc.vector.scalar_tensor_tensor(out=y[:, s], in0=o, scalar=0.0, in1=x3[:, s],
                                               op0=ALU.max, op1=ALU.add).then_inc(sem("agg3_read"), 1)
                dve.wait_ge(sem("agg3_read"), n + 1)
                moments(3, n, s)

            steps = {
                "masks": masks, "shift0": shift0, "max0": max0, "sum0": norm0, "shift1": shift1, "elu1": elu1,
                "sum1": norm1, "q_dve": proj2,
                "shift2a": lambda n, s, r: shift2(0, n, s), "shift2b": lambda n, s, r: shift2(1, n, s),
                "rsum2": rsum2_, "norm_o": o_nodes, "sum2": norm2, "vals3": vals3, "sum3": norm3,
                "norm0": lambda *a: norm(0, *a), "norm1": lambda *a: norm(1, *a),
                "norm2": lambda *a: norm(2, *a), "norm3": lambda *a: norm(3, *a),
            }

            setup()
            rounds(dve, "vector", steps)

            dve.wait_ge(sem("excess_all_ready"), 1)
            nc.vector.tensor_scalar(excess_flag[:, :], excess_all[:, :], 0.0, None, ALU.is_gt)\
                .then_inc(sem("flag_ready"), 1)

            def relations():
                def relation_steps(k):
                    dve.wait_ge(sem("rel_bias_loaded"), k * 64 + 64)
                    for way in range(2):
                        nc.vector.scalar_tensor_tensor(
                            out=rel_sum[:, way, :, 0:D],
                            in0=rel_bias[:, way, 0:1, :].to_broadcast([P, T, D]), scalar=0.5,
                            in1=rel_hg[:, way, :, 0:D], op0=ALU.mult, op1=ALU.add)
                        last = nc.vector.tensor_tensor(rel_sum[:, way, :, D:2 * D], rel_hg[:, way, :, D:2 * D],
                                                       rel_bias[:, way, 1:2, :].to_broadcast([P, T, D]), ALU.add)
                    last.then_inc(sem("rel_sums_ready"), 1)
                    for way, a in enumerate((rel_adjT_f, rel_adj_f)):
                        last = nc.vector.tensor_scalar(rel_hot[way], a, rel_no[:, 0:1], None, ALU.is_equal)
                    last.then_inc(sem("rel_hot_ready"), 1)
                    dve.wait_ge(sem("rel_hot_ready"), k + 1)
                    nc.vector.tensor_scalar(rel_no[:, :], rel_no[:, :], 1.0, None, ALU.add)\
                        .then_inc(sem("rel_no_ready"), 1)
                    dve.wait_ge(sem("rel_no_ready"), k + 1)
                    dve.wait_ge(sem("rel_gates"), k + 1)
                    for way in range(2):
                        last = nc.vector.scalar_tensor_tensor(
                            out=rel_vals[way], in0=rel_sum[:, way, :, D:2 * D], scalar=1.0,
                            in1=rel_sum[:, way, :, 0:D], op0=ALU.add, op1=ALU.mult)
                    last.then_inc(sem("rel_vals_ready"), 1)
                    dve.wait_ge(sem("rel_ps"), k + 1)
                    o = ps[:, 6, 0:T * D].rearrange("p (t d) -> p t d", t=T)
                    nc.vector.tensor_tensor(rel_acc, o, rel_acc, ALU.add).then_inc(sem("rel_added"), 1)
                    dve.wait_ge(sem("rel_added"), k + 1)

                dve.wait_ge(sem("x4_ready"), B)
                nc.vector.memset(rel_no[:, :], 0.0).then_inc(sem("rel_graph_done"), 1)
                nc.vector.memset(small[:, 0, 5, :], 0.0).then_inc(sem("rel_sums_ready"), 1)
                with dve.Fori(0, B) as g:
                    dve.wait_ge(sem("rel_graph_done"), g + 1)
                    dve.wait_ge(sem("rel_loaded"), g * 32 + 32)
                    nc.vector.memset(rel_no[:, :], 2.0).then_inc(sem("rel_first_no"), 1)
                    nc.vector.tensor_copy(rel_adj_f, rel_adj).then_inc(sem("rel_adj_f_ready"), 1)
                    dve.wait_ge(sem("rel_adj_f_ready"), g + 1)
                    nc.vector.tensor_scalar(rel_hot[0], rel_adj_f, 1.0, None, ALU.is_equal)
                    dve.wait_ge(sem("rel_hg_sb"), g + 1)
                    b = hg_bias[:, :].rearrange("p (a d) -> p a d", a=1).to_broadcast([P, T, 2 * D])
                    nc.vector.tensor_tensor(rel_hg[:, 2], rel_hg[:, 2], b, ALU.add).then_inc(sem("rel_loop_sum"), 1)
                    dve.wait_ge(sem("rel_loop_gate"), g + 1)
                    nc.vector.scalar_tensor_tensor(out=rel_vals[0], in0=rel_hg[:, 2, :, D:2 * D], scalar=1.0,
                                                   in1=rel_hg[:, 2, :, 0:D], op0=ALU.add, op1=ALU.mult)\
                        .then_inc(sem("rel_loop_vals"), 1)
                    dve.wait_ge(sem("rel_loop_ps"), g + 1)
                    nc.vector.tensor_copy(rel_acc, ps[:, 5, 0:T * D].rearrange("p (t d) -> p t d", t=T))\
                        .then_inc(sem("rel_acc_ready"), 1)
                    with dve.Fori(0, NREL) as r:
                        dve.wait_ge(sem("rel_acc_ready"), g + 1)
                        dve.wait_ge(sem("rel_first_no"), g + 1)
                        relation_steps(g * NREL + r)
                    nc.vector.scalar_tensor_tensor(out=hmid[:, 0], in0=rel_acc, scalar=0.0, in1=rel_x,
                                                   op0=ALU.max, op1=ALU.add).then_inc(sem("rel_y_ready"), 1)
                    dve.wait_ge(sem("rel_y_ready"), g + 1)
                    for k in range(T):
                        last = nc.vector.bn_stats(stats[:, 0, k, :], hmid[:, 0, k, :])
                    last.then_inc(sem("rel_stats"), 1)
                    wait_apart(dve, sem("rel_stats"), g + 1)
                    for k in range(T):
                        last = nc.vector.bn_aggr(mv[:, 0, k, :], stats[:, 0, k, :])
                    last.then_inc(sem("rel_mv"), 1)
                    dve.wait_ge(sem("rel_rstd"), g + 1)
                    for k in range(T):
                        last = nc.vector.tensor_scalar(rel_out[:, k, :], hmid[:, 0, k, :], mv[:, 0, k, 0:1],
                                                       rstd[:, 0, k:k + 1], ALU.subtract, ALU.mult)
                    last.then_inc(sem("rel_out_ready"), 1)
                    dve.wait_ge(sem("rel_stored"), g * 16 + 16)
                    nc.vector.memset(small[:, 0, 5, :], 0.0).then_inc(sem("rel_graph_done"), 1)

            with if_relations(dve):
                relations()

        @block.gpsimd
        def _(pool):
            def setup():
                nc.gpsimd.memset(ident[:, :], 0.0)
                nc.gpsimd.memset(excess_sum[:, :], 0.0)
                nc.gpsimd.memset(not_eye[:, :, :], 1.0).then_inc(sem("pool_setup"), 1)
                pool.wait_ge(sem("pool_setup"), 1)
                nc.gpsimd.affine_select(out=ident[:, :], in_=ident[:, :], compare_op=ALU.not_equal, fill=1.0,
                                        base=0, pattern=[[-1, P]], channel_multiplier=1)\
                    .then_inc(sem("consts_ready"), 1)
                for k in range(T):
                    last = nc.gpsimd.affine_select(out=not_eye[:, k, :], in_=not_eye[:, k, :],
                                                   compare_op=ALU.not_equal, fill=0.0, base=k * P,
                                                   pattern=[[-1, N]], channel_multiplier=1)
                last.then_inc(sem("pool_setup"), 1)
                pool.wait_ge(sem("pool_setup"), 2)

            def mask2(n, s, r):
                pool.wait_ge(sem("masks_ready"), n + 1)
                pool.wait_ge(sem("excess_ready"), n + 1)
                nc.gpsimd.tensor_tensor(neg2[:, s], neg0[:, s], not_eye[:, :, :], ALU.mult)\
                    .then_inc(sem("neg2_ready"), 1)

            def add_excess(n, s, r):
                pool.wait_ge(sem("excess_ready"), n + 1)
                nc.gpsimd.tensor_tensor(excess_sum[:, :], excess_sum[:, :], excess_row[:, s:s + 1], ALU.add)\
                    .then_inc(sem("excess_added"), 1)
                pool.wait_ge(sem("excess_added"), n + 1)

            def rsqrt(layer, n, s):
                wait_apart(pool, sem(f"mv{layer}_ready"), n + 1)
                nc.gpsimd.tensor_scalar(ve[:, s, :], mv[:, s, :, 1], 1.0, EPS, ALU.mult, ALU.add)\
                    .then_inc(sem(f"ve{layer}_ready"), 1)
                pool.wait_ge(sem(f"ve{layer}_ready"), n + 1)
                nc.gpsimd.tensor_tensor(rstd[:, s, :], ve[:, s, :], minus_half[:, :], ALU.pow)\
                    .then_inc(sem(f"rstd{layer}_ready"), 1)

            steps = {
                "mask2": mask2, "excess": add_excess, "rstd0": lambda n, s, r: rsqrt(0, n, s),
                "rstd1": lambda n, s, r: rsqrt(1, n, s), "rstd2": lambda n, s, r: rsqrt(2, n, s),
                "rstd3": lambda n, s, r: rsqrt(3, n, s),
            }

            def relations():
                with pool.Fori(0, B) as g:
                    wait_apart(pool, sem("rel_mv"), g + 1)
                    nc.gpsimd.tensor_scalar(ve[:, 0, :], mv[:, 0, :, 1], 1.0, EPS, ALU.mult, ALU.add)\
                        .then_inc(sem("rel_ve"), 1)
                    pool.wait_ge(sem("rel_ve"), g + 1)
                    nc.gpsimd.tensor_tensor(rstd[:, 0, :], ve[:, 0, :], minus_half[:, :], ALU.pow)\
                        .then_inc(sem("rel_rstd"), 1)

            setup()
            rounds(pool, "gpsimd", steps)
            nc.gpsimd.partition_all_reduce(excess_all[:, :], excess_sum[:, :], P, bass.bass_isa.ReduceOp.max)\
                .then_inc(sem("excess_all_ready"), 1)
            with if_relations(pool):
                relations()


_INS = ['x', 'adj', 'L0_gnn_W', 'L0_gnn_a', 'L1_gnn_W', 'L1_gnn_a_1', 'L1_gnn_a_2', 'L1_gnn_a_12', 'L1_gnn_W_1',
        'L1_gnn_W_2', 'L2_gnn_Wq', 'L2_gnn_bq', 'L2_gnn_Wk', 'L2_gnn_bk', 'L2_gnn_Wv', 'L2_gnn_bv', 'L2_gnn_Wo',
        'L2_gnn_bo', 'L3_gnn_W_fwd', 'L3_gnn_W_bwd', 'L3_gnn_W_loop', 'L3_gnn_Wg_fwd', 'L3_gnn_Wg_bwd',
        'L3_gnn_Wg_loop', 'L3_gnn_b_fwd', 'L3_gnn_b_bwd', 'L3_gnn_b_loop', 'L3_gnn_bg_fwd', 'L3_gnn_bg_bwd',
        'L3_gnn_bg_loop']


def kernel(**inputs):
    import numpy as _np
    import concourse.bacc as _bacc
    from concourse import mybir as _mybir
    from concourse.bass_utils import run_bass_kernel_spmd as _run

    nc = _bacc.Bacc("TRN2", target_bir_lowering=False, num_devices=1)
    arrays, args = {}, {}
    for name in _INS:
        a = _np.ascontiguousarray(inputs[name])
        arrays[f"in_{name}_dram"] = a
        args[name] = nc.dram_tensor(f"in_{name}_dram", a.shape, _mybir.dt.from_np(a.dtype),
                                    kind="ExternalInput").ap()
    shape = _np.shape(inputs["x"])
    out = nc.dram_tensor("out_0_dram", shape, _mybir.dt.float32, kind="ExternalOutput").ap()
    build(nc, args, out)
    r = _run(nc, [arrays], core_ids=[0])
    return r.results[0]["out_0_dram"]
```

```python
from contextlib import ExitStack

import numpy as np
import concourse.bass as bass
from concourse import mybir

F32 = mybir.dt.float32
BF16 = mybir.dt.bfloat16
I32 = mybir.dt.int32
ALU = mybir.AluOpType
ACT = mybir.ActivationFunctionType
AX = mybir.AxisListType

P = 128
SLOTS = 5
HEADS = 4
EPS = 1e-5
SLOPE = 0.2
NEG_INF = -1e30
NEG_L1 = -9e15
TINY = 1e-30
LOWEST = -3.0e38

PLAN = {
    "sync": [("load", 249), ("aside", 833), ("store", 923)],
    "tensor": [("xT0", 35), ("proj0", 63), ("s2_rows", 141), ("pT0", 206), ("agg0", 223), ("xT1", 283),
        ("proj1", 313), ("scores1", 368), ("pT1", 439), ("agg1", 460), ("xT2", 550), ("proj2", 563),
        ("scores2a", 602), ("scores2b", 625), ("pT2a", 674), ("pT2b", 702), ("agg2", 724), ("rsum_rows", 746),
        ("wo", 762), ("xT3", 831), ("proj3", 848), ("agg3", 896)],
    "scalar": [("c_xT0", 55), ("c_proj0", 70), ("exp0", 168), ("c_pT0", 215), ("test_adj", 233),
        ("c_xT1", 292), ("c_tT", 331), ("c_xw", 371), ("c_z", 382), ("exp1", 429), ("c_pT1", 445),
        ("c_elu", 503), ("c_xT2", 554), ("q_rest", 578), ("c_qk", 590), ("c_v", 606), ("exp2a", 636),
        ("exp2b", 665), ("c_pT2a", 691), ("c_pT2b", 713), ("c_rsum", 750), ("c_xT3", 844), ("gate3", 870)],
    "vector": [("masks", 119), ("shift0", 151), ("max0", 185), ("sum0", 234), ("norm0", 273), ("shift1", 397),
        ("elu1", 479), ("sum1", 509), ("shift2a", 619), ("shift2b", 645), ("rsum2", 693), ("norm_o", 754),
        ("sum2", 777), ("norm2", 823), ("vals3", 874), ("sum3", 907)],
    "gpsimd": [("rstd0", 253), ("mask2", 261), ("norm1", 532), ("rep_rsum", 696), ("rstd2", 790),
        ("excess", 828), ("norm3", 924)],
}
CYCLE = 925

RINGS = ("tp", "mm", "big")
PSUM_USES = {
    "xT0": [("tp", "xT_sb0", 1, 0)],
    "proj0": [("mm", "wh_sb", 1, 0)],
    "s2_rows": [("mm", "rowmax0_ready", 1, 0)],
    "pT0": [("tp", "pT_sb0", 1, 0)],
    "agg0": [("mm", "y0_ready", 2, 1)],
    "xT1": [("tp", "xT_sb1", 1, 0)],
    "proj1": [("mm", "tT_sb", 1, 0), ("big", "xw_sb", 1, 0)],
    "scores1": [("mm", "z_sb", 1, 0)],
    "pT1": [("tp", "pT_sb1", 1, 0)],
    "agg1": [("mm", "agg1_read", 1, 0)],
    "xT2": [("tp", "xT_sb2", 1, 0)],
    "proj2": [("big", "qkv_sb", 2, 1)],
    "scores2a": [("big", "scores2_read", 2, 0)],
    "scores2b": [("big", "scores2_read", 2, 1)],
    "pT2a": [("tp", "pT_sb2", 4, 0), ("tp", "pT_sb2", 4, 1)],
    "pT2b": [("tp", "pT_sb2", 4, 2), ("tp", "pT_sb2", 4, 3)],
    "rsum_rows": [("tp", "rsum_rows_sb", 1, 0), ("tp", "rsum_rows_sb", 1, 0)],
    "agg2": [("mm", "onT_sb", 1, 0)],
    "wo": [("mm", "y2_ready", 2, 1)],
    "xT3": [("tp", "xT_sb3", 1, 0)],
    "proj3": [("mm", "vals_ready", 1, 0)],
    "agg3": [("mm", "y3_ready", 2, 1)],
}


def one_cycle(engine):
    order = []
    for k, (name, place) in enumerate(PLAN[engine]):
        for s in range(SLOTS):
            at = place + s * CYCLE // SLOTS
            order.append((at % CYCLE, s, at // CYCLE, k, name))
    return [(name, s, late) for _, s, late, _, name in sorted(order)]


def ring_uses(ring):
    return [(step, s, k, late, read, per, at)
            for step, s, late in one_cycle("tensor")
            for k, (r, read, per, at) in enumerate(PSUM_USES[step]) if r == ring]


def build(nc, t, out):
    B, N, D = t["x"].shape
    T = N // P
    DK = D // HEADS
    SCALE = 1.0 / float(np.sqrt(DK + 1e-09))
    NREL = t["L3_gnn_b_fwd"].shape[0]
    assert D == P and T == 2
    rings = {r: ring_uses(r) for r in RINGS}
    assert all(len(u) % 2 == 0 for u in rings.values())

    with ExitStack() as ctx:
        def sb(name, shape, dt=F32):
            return ctx.enter_context(nc.sbuf_tensor(name, shape, dt))

        sems = {}

        def sem(name):
            if name not in sems:
                sems[name] = ctx.enter_context(nc.semaphore(name))
            return sems[name]

        ident = sb("ident", [P, P])
        not_eye = sb("not_eye", [P, T, N], BF16)
        minus_half = sb("minus_half", [P, T])
        minus_one = sb("minus_one", [P, 1])
        w_in = sb("w_in", [P, 11, P])
        W0, W1L, A12, W_1, W_2, WQ, WK, WV, WO, WL, WGL = range(11)
        cols = sb("cols", [P, 8])
        A1, A2, L1A1, L1A2, BQ, BK, BV = range(7)
        w0T12 = sb("w0T12", [P, D + 2])
        wT = sb("wT", [P, 4, P])
        M1 = sb("M1", [P, P])
        u12 = sb("u12", [P, 2])
        xw_w = sb("xw_w", [P, 2 * D + 1])
        bv_rep = sb("bv_rep", [P, P])
        bo_row = sb("bo_row", [P, D])
        hg_w = sb("hg_w", [P, 2 * D])
        hg_bias = sb("hg_bias", [P, 2 * D])
        ones_row = sb("ones_row", [P, P])
        ones_bf = sb("ones_bf", [P, P], BF16)
        bo_parts = sb("bo_parts", [P, D], BF16)
        hg_parts = sb("hg_parts", [P, 2 * D], BF16)
        excess_row = sb("excess_row", [P, SLOTS])
        excess_sum = sb("excess_sum", [P, 1])
        excess_all = sb("excess_all", [P, 1])
        excess_flag = sb("excess_flag", [P, 1], I32)

        x_in = sb("x_in", [P, SLOTS, T, D])
        adj_in = sb("adj_in", [P, SLOTS, T, N], I32)
        neg0 = sb("neg0", [P, SLOTS, T, N], BF16)
        neg1 = sb("neg1", [P, SLOTS, T, N], BF16)
        neg2 = sb("neg2", [P, SLOTS, T, N], BF16)
        eq1 = sb("eq1", [P, SLOTS, T, N])
        xT = sb("xT", [P, SLOTS, N])
        x1 = sb("x1", [P, SLOTS, T, D])
        x2 = sb("x2", [P, SLOTS, T, D])
        x3 = sb("x3", [P, SLOTS, T, D])
        y = sb("y", [P, SLOTS, T, D])
        stats = sb("stats", [P, SLOTS, T, 6])
        mv = sb("mv", [P, SLOTS, T, 2])
        ve = sb("ve", [P, SLOTS, T])
        rstd = sb("rstd", [P, SLOTS, T])
        xw = sb("xw", [P, SLOTS, T, 2 * D + 2])
        tT = sb("tT", [P, SLOTS, N])
        rowmax = sb("rowmax", [P, SLOTS, T])
        small = sb("small", [P, SLOTS, 8, T])
        rsum = sb("rsum", [P, SLOTS, T])
        hmid = sb("hmid", [P, SLOTS, T, D])
        hexp = sb("hexp", [P, SLOTS, T, D])
        qblk = sb("qblk", [P, SLOTS, HEADS, N])
        p2 = sb("p2", [P, SLOTS, T, HEADS, N])
        p2T = sb("p2T", [P, SLOTS, HEADS, T, N])
        sm, pa, pb, prob = (p2[:, :, :, :, :].rearrange("p s t h n -> p s (t h n)")[:, :, c * T * N:(c + 1) * T * N]
                            .rearrange("p s (t n) -> p s t n", t=T) for c in range(4))
        probT = p2T[:, :, 0]
        rowmax2 = sb("rowmax2", [P, SLOTS, T * HEADS])
        nmax2 = sb("nmax2", [P, SLOTS, T * HEADS])
        sum2 = sb("sum2", [P, SLOTS, T * HEADS])
        rsum2 = sb("rsum2", [P, SLOTS, T * HEADS])
        over_one = neg2
        kT, vn = tT, hexp
        rsum_rep = y
        rsum_rows = hmid.rearrange("p s t d -> p s (t d)")
        onT = xT
        gate = xw[:, :, :, 0:D]
        x4 = x1
        vals = hmid

        ps = ctx.enter_context(nc.psum_tensor("ps", [P, 8, 512], F32))
        FIRST_BANK = {"tp": 0, "mm": 2, "big": 4}

        def bank(step, s, k=0):
            for ring, uses in rings.items():
                for at, u in enumerate(uses):
                    if u[:3] == (step, s, k):
                        b = FIRST_BANK[ring] + (at % 2) * (2 if ring == "big" else 1)
                        return ps[:, b, :] if ring != "big" else ps[:, b:b + 2, :]
            raise KeyError((step, s, k))

        def bank_read(pe, step, s, k, n):
            for uses in rings.values():
                for at, u in enumerate(uses):
                    if u[:3] != (step, s, k):
                        continue
                    back = at
                    while True:
                        back -= 2
                        _, s_before, _, late_before, read, per, number = uses[back % len(uses)]
                        graph = n - s + SLOTS * (u[3] - late_before + back // len(uses)) + s_before
                        if not isinstance(graph, int) or 0 <= graph < B:
                            break
                        if graph < 0 and back < -len(uses):
                            return
                    pe.wait_ge(sem(read), graph * per + number + 1)

        x3_dram = nc.dram_tensor("x3_aside", (B, P, T * D), F32, kind="Internal").ap()

        x_v = t["x"].rearrange("b (t p) d -> b p t d", p=P)
        adj_v = t["adj"].rearrange("b (t p) j -> b p t j", p=P)
        out_v = out.rearrange("b (t p) d -> b p t d", p=P)
        loads = [
            (w_in[:, W0, :], t["L0_gnn_W"]),
            (cols[:, A1:A1 + 1], t["L0_gnn_a"][:, 0:D].rearrange("a p -> p a")),
            (cols[:, A2:A2 + 1], t["L0_gnn_a"][:, D:2 * D].rearrange("a p -> p a")),
            (w_in[:, W1L, :], t["L1_gnn_W"]), (w_in[:, A12, :], t["L1_gnn_a_12"]),
            (w_in[:, W_1, :], t["L1_gnn_W_1"]), (w_in[:, W_2, :], t["L1_gnn_W_2"]),
            (cols[:, L1A1:L1A1 + 1], t["L1_gnn_a_1"]), (cols[:, L1A2:L1A2 + 1], t["L1_gnn_a_2"]),
            (w_in[:, WQ, :], t["L2_gnn_Wq"]), (w_in[:, WK, :], t["L2_gnn_Wk"]),
            (w_in[:, WV, :], t["L2_gnn_Wv"]), (w_in[:, WO, :], t["L2_gnn_Wo"]),
            (cols[:, BQ:BQ + 1], t["L2_gnn_bq"].rearrange("(p a) -> p a", a=1)),
            (cols[:, BK:BK + 1], t["L2_gnn_bk"].rearrange("(p a) -> p a", a=1)),
            (cols[:, BV:BV + 1], t["L2_gnn_bv"].rearrange("(p a) -> p a", a=1)),
            (bo_row[:, :], t["L2_gnn_bo"].rearrange("(a d) -> a d", a=1).broadcast_to((P, D))),
            (w_in[:, WL, :], t["L3_gnn_W_loop"]), (w_in[:, WGL, :], t["L3_gnn_Wg_loop"]),
            (hg_bias[:, 0:D], t["L3_gnn_b_loop"].broadcast_to((P, D))),
            (hg_bias[:, D:2 * D], t["L3_gnn_bg_loop"].broadcast_to((P, D))),
        ]

        W0_LOADS = 3
        WEIGHTS_LOADED = 16 * (len(loads) - W0_LOADS)

        rel_w = qblk[:, 0, 0:2, :]
        rel_adj = adj_in[:, 0]
        rel_adj_f = eq1[:, 1]
        rel_adjT_f = eq1[:, 2]
        rel_hot = (eq1[:, 0], eq1[:, 3])
        rel_x = x1[:, 0]
        rel_xT = xT[:, 0]
        rel_hg = (p2[:, 0].rearrange("p t h n -> p (t h n)")[:, 0:3 * T * 2 * D]
                  .rearrange("p (w t d) -> p w t d", w=3, t=T))
        rel_bias = y
        rel_sum = xw
        rel_vals = (x2[:, 0], x2[:, 1])
        rel_acc = x2[:, 2]
        rel_out = x2[:, 3]
        rel_no = sb("rel_no", [P, 1])
        rel_biases = ((t["L3_gnn_b_fwd"], t["L3_gnn_bg_fwd"]), (t["L3_gnn_b_bwd"], t["L3_gnn_bg_bwd"]))
        rel_weights = [t["L3_gnn_W_fwd"], t["L3_gnn_W_bwd"], t["L3_gnn_Wg_fwd"], t["L3_gnn_Wg_bwd"]]

        def if_relations(engine):
            engine.wait_ge(sem("flag_ready"), 1)
            flag = engine.value_load(excess_flag[0:1, 0:1], min_val=0, max_val=1)
            return engine.If(flag != 0)

        block = ctx.enter_context(nc.Block())

        wait_registers = {}

        def wait_apart(engine, semaphore, value):
            if not isinstance(value, int):
                if engine not in wait_registers:
                    wait_registers[engine] = engine.alloc_register(f"awaited{len(wait_registers)}")
                engine.reg_alu(wait_registers[engine], value - 1, 1, ALU.add)
                value = wait_registers[engine]
            engine.wait_ge(sem("consts_ready"), 1)
            engine.wait_ge(semaphore, value)

        def rounds(engine, name, steps, full=B // SLOTS, unrolled=2):
            def one_round(i):
                for step, s, late in one_cycle(name):
                    r = i - late
                    n = r * SLOTS + s
                    if isinstance(n, int) and not 0 <= n < B:
                        continue
                    steps[step](n, s, r)

            one_round(0)
            one_round(1)
            assert (full - 2) % unrolled == 0
            with engine.Fori(2, full - unrolled + 1, unrolled) as i:
                for k in range(unrolled):
                    one_round(i + k)
            for i in range(full, (B - 1) // SLOTS + 2):
                one_round(i)

        def is_first(n):
            return isinstance(n, int) and n == 0

        def fresh(r):
            return isinstance(r, int) and r == 0

        @block.sync
        def _(sp):
            def load_graph(n, s):
                sp.dma_start(adj_in[:, s], adj_v[n]).then_inc(sem(f"adj_loaded{s}"), 16)
                sp.dma_start(x_in[:, s], x_v[n]).then_inc(sem(f"x_loaded{s}"), 16)

            def load_next(n, s, r):
                if isinstance(n, int) and n + SLOTS >= B:
                    return
                sp.wait_ge(sem("masks_ready"), n + 1)
                sp.wait_ge(sem("excess_ready"), n + 1)
                sp.wait_ge(sem("y0_ready"), n * T + T)
                load_graph(n + SLOTS, s)

            def aside(n, s, r):
                sp.wait_ge(sem("x3_ready"), n + 1)
                sp.dma_start(x3_dram[n], x3[:, s].rearrange("p t d -> p (t d)"))\
                    .then_inc(sem(f"x3_aside{s}"), 16)

            def store(n, s, r):
                sp.wait_ge(sem("x4_ready"), n + 1)
                sp.dma_start(out_v[n], x4[:, s]).then_inc(sem(f"stored{s}"), 16)

            for dst, src in loads[:W0_LOADS]:
                sp.dma_start(dst, src).then_inc(sem("w0_loaded"), 16)
            for s in range(SLOTS):
                load_graph(s, s)
                if s == 0:
                    for dst, src in loads[W0_LOADS:]:
                        sp.dma_start(dst, src).then_inc(sem("weights_loaded"), 16)
            rounds(sp, "sync", {"load": load_next, "aside": aside, "store": store}, B // SLOTS - 1, 1)
            for s in range(SLOTS):
                sp.wait_ge(sem(f"stored{s}"), 16 * len(range(s, B, SLOTS)))
                sp.wait_ge(sem(f"x3_aside{s}"), 16 * len(range(s, B, SLOTS)))
            with if_relations(sp):
                for k, w in enumerate(rel_weights):
                    sp.dma_start(w_in[:, k, :], w).then_inc(sem("rel_w_loaded"), 16)
                with sp.Fori(0, B) as g:
                    sp.wait_ge(sem("rel_graph_done"), g + 1)
                    sp.dma_start(rel_adj, adj_v[g]).then_inc(sem("rel_loaded"), 16)
                    sp.dma_start(rel_x.rearrange("p t d -> p (t d)"), x3_dram[g]).then_inc(sem("rel_loaded"), 16)
                    with sp.Fori(0, NREL) as r:
                        sp.wait_ge(sem("rel_sums_ready"), g * NREL + r + 1)
                        for way in range(2):
                            for part in range(2):
                                sp.dma_start(rel_bias[:, way, part, :],
                                             rel_biases[way][part].rearrange("r (a d) -> r a d", a=1)[r].broadcast_to((P, D)))\
                                    .then_inc(sem("rel_bias_loaded"), 16)
                    sp.wait_ge(sem("rel_out_ready"), g + 1)
                    sp.dma_start(out_v[g], rel_out).then_inc(sem("rel_stored"), 16)
                sp.wait_ge(sem("rel_stored"), 16 * B)

        @block.tensor
        def _(pe):
            def setup():
                pe.wait_ge(sem("consts_ready"), 1)
                pe.wait_ge(sem("w0_loaded"), 16 * W0_LOADS)
                pe.transpose(ps[:, 4, 0:P], w_in[:, W0, :], ident[:, :])
                pe.matmul(ps[:, 4, P:P + 2], w_in[:, W0, :], cols[:, A1:A2 + 1],
                          start=True, stop=True).then_inc(sem("setup_pe"), 1)

            def setup_later():
                pe.wait_ge(sem("weights_loaded"), WEIGHTS_LOADED)
                for k, w in enumerate((W1L, A12, WGL, WL)):
                    last = pe.transpose(ps[:, 4, k * P:(k + 1) * P], w_in[:, w, :], ident[:, :])
                last.then_inc(sem("setup_pe"), 1)
                pe.wait_ge(sem("setup_t_sb"), 1)
                pe.matmul(ps[:, 5, 0:P], wT[:, 1, :], wT[:, 0, :], start=True, stop=True)
                pe.matmul(ps[:, 5, P:P + 2], wT[:, 0, :], cols[:, L1A1:L1A2 + 1], start=True, stop=True)
                pe.matmul(ps[:, 5, 2 * P:3 * P], w_in[:, WL, :], wT[:, 2, :], start=True, stop=True)\
                    .then_inc(sem("setup_pe"), 1)
                pe.wait_ge(sem("setup_t_sb"), 2)
                pe.matmul(ps[:, 6, 0:P], wT[:, 0, :], wT[:, 3, :], start=True, stop=True)\
                    .then_inc(sem("setup_pe"), 1)
                pe.wait_ge(sem("bv_ready"), 1)
                pe.matmul(ps[:, 7, 0:D], bv_rep[:, :], w_in[:, WO, :], start=True, stop=True)\
                    .then_inc(sem("setup_pe"), 1)
                pe.wait_ge(sem("weights_ready"), 2)

            def transpose_x(layer, n, s, r, src):
                o = bank(f"xT{layer}", s)
                bank_read(pe, f"xT{layer}", s, 0, n)
                for k in range(T):
                    last = pe.transpose(o[:, k * P:(k + 1) * P], src[:, s, k, :], ident[:, :])
                last.then_inc(sem(f"xT_ps{layer}"), 1)

            def xT0(n, s, r):
                pe.wait_ge(sem(f"x_loaded{s}"), r * 16 + 16)
                transpose_x(0, n, s, r, x_in)

            def proj0(n, s, r):
                o = bank("proj0", s)
                bank_read(pe, "proj0", s, 0, n)
                if is_first(n):
                    pe.wait_ge(sem("weights_ready"), 1)
                pe.wait_ge(sem("xT_sb0"), n + 1)
                for k in range(T):
                    last = pe.matmul(o[:, k * (D + 2):(k + 1) * (D + 2)], xT[:, s, k * P:(k + 1) * P],
                                     w0T12[:, :], start=True, stop=True)
                last.then_inc(sem("wh_ps"), 1)

            def s2_rows(n, s, r):
                o = bank("s2_rows", s)
                bank_read(pe, "s2_rows", s, 0, n)
                pe.wait_ge(sem("wh_sb"), n + 1)
                for k in range(T):
                    last = pe.transpose(o[:, k * P:(k + 1) * P], xw[:, s, k, 1:2].to_broadcast([P, P]),
                                        ident[:, :])
                last.then_inc(sem("s2_ps"), 1)

            def transpose_p(layer, n, s, r):
                o = bank(f"pT{layer}", s)
                bank_read(pe, f"pT{layer}", s, 0, n)
                pe.wait_ge(sem(f"p_ready{layer}"), n + 1)
                for j in range(T):
                    for k in range(T):
                        last = pe.transpose(o[:, j * N + k * P:j * N + (k + 1) * P],
                                            prob[:, s, k, j * P:(j + 1) * P], ident[:, :])
                last.then_inc(sem(f"pT_ps{layer}"), 1)

            def aggregate(layer, n, s, r, values):
                o = bank(f"agg{layer}", s)
                bank_read(pe, f"agg{layer}", s, 0, n)
                pe.wait_ge(sem(f"pT_sb{layer}"), n + 1)
                for k in range(T):
                    for j in range(T):
                        last = pe.matmul(o[:, k * (D + 1):(k + 1) * (D + 1)],
                                         probT[:, s, j, k * P:(k + 1) * P], values(j),
                                         start=(j == 0), stop=(j == T - 1))
                last.then_inc(sem(f"agg{layer}_ps"), 1)

            def agg0(n, s, r):
                pe.wait_ge(sem("wh_sb"), n + 1)
                aggregate(0, n, s, r, lambda j: xw[:, s, j, D + 1:2 * D + 2])

            def xT1(n, s, r):
                if is_first(n):
                    setup_later()
                pe.wait_ge(sem("x1_ready"), n + 1)
                transpose_x(1, n, s, r, x1)

            def proj1(n, s, r):
                o, o2 = bank("proj1", s, 0), bank("proj1", s, 1)
                pe.wait_ge(sem("xT_sb1"), n + 1)
                bank_read(pe, "proj1", s, 0, n)
                pe.matmul(o[:, 0:N], M1[:, :], xT[:, s, :], start=True, stop=True).then_inc(sem("tT_ps"), 1)
                bank_read(pe, "proj1", s, 1, n)
                for k in range(T):
                    last = pe.matmul(o2[:, k, 0:2 * D + 1], xT[:, s, k * P:(k + 1) * P], xw_w[:, :],
                                     start=True, stop=True)
                last.then_inc(sem("xw_ps"), 1)

            def scores1(n, s, r):
                o = bank("scores1", s)
                bank_read(pe, "scores1", s, 0, n)
                pe.wait_ge(sem("tT_sb"), n + 1)
                for k in range(T):
                    last = pe.matmul(o[:, k * N:(k + 1) * N], tT[:, s, k * P:(k + 1) * P], xT[:, s, :],
                                     start=True, stop=True)
                last.then_inc(sem("z_ps"), 1)

            def agg1(n, s, r):
                pe.wait_ge(sem("xw_sb"), n + 1)
                aggregate(1, n, s, r, lambda j: xw[:, s, j, D + 1:2 * D + 2])

            def xT2(n, s, r):
                pe.wait_ge(sem("x2_ready"), n + 1)
                transpose_x(2, n, s, r, x2)

            def proj2(n, s, r):
                o = bank("proj2", s)
                bank_read(pe, "proj2", s, 0, n)
                pe.wait_ge(sem("xT_sb2"), n + 1)
                pe.matmul(o[:, 0, 0:N], w_in[:, WQ, :], xT[:, s, :], start=True, stop=True)
                pe.matmul(o[:, 1, N:2 * N], w_in[:, WK, :], xT[:, s, :], start=True, stop=True)
                for k in range(T):
                    last = pe.matmul(o[:, 1, k * D:(k + 1) * D], xT[:, s, k * P:(k + 1) * P],
                                     w_in[:, WV, :], start=True, stop=True)
                last.then_inc(sem("qkv_ps"), 1)

            def scores2(k, n, s):
                step = "scores2" + "ab"[k]
                o = bank(step, s)
                pe.wait_ge(sem("qkv_sb"), n * 2 + 1)
                pe.wait_ge(sem("q_sb"), n + 1)
                bank_read(pe, step, s, 0, n)
                for h in range(HEADS):
                    last = pe.matmul(o[:, h // 2, (h % 2) * N:(h % 2 + 1) * N],
                                     qblk[:, s, h, k * P:(k + 1) * P], kT[:, s, :], start=True, stop=True)
                last.then_inc(sem("scores2_ps"), 1)

            def pT2(k, n, s):
                step = "pT2" + "ab"[k]
                pe.wait_ge(sem("p_ready2"), n * T + k + 1)
                for j in range(T):
                    o = bank(step, s, j)
                    bank_read(pe, step, s, j, n)
                    for h in range(HEADS):
                        last = pe.transpose(o[:, h * P:(h + 1) * P], p2[:, s, k, h, j * P:(j + 1) * P],
                                            ident[:, :])
                    last.then_inc(sem("pT_ps2"), 1)

            def agg2(n, s, r):
                o = bank("agg2", s)
                bank_read(pe, "agg2", s, 0, n)
                pe.wait_ge(sem("pT_sb2"), n * 4 + 4)
                pe.wait_ge(sem("qkv_sb"), n * 2 + 2)
                for j in range(T):
                    for h in range(HEADS):
                        last = pe.matmul(o[h * DK:(h + 1) * DK, 0:N], vn[:, s, j, h * DK:(h + 1) * DK],
                                         p2T[:, s, h, j, :], start=(j == 0), stop=(j == T - 1))
                last.then_inc(sem("agg2_ps"), 1)

            def rsum_rows_(n, s, r):
                o = bank("rsum_rows", s, 0)
                bank_read(pe, "rsum_rows", s, 0, n)
                pe.wait_ge(sem("rsum_rep_ready"), n + 1)
                for k in range(T):
                    last = pe.transpose(o[:, k * P:(k + 1) * P], rsum_rep[:, s, k, :], ident[:, :])
                last.then_inc(sem("rsum_rows_ps"), 1)

            def wo(n, s, r):
                if is_first(n):
                    pe.wait_ge(sem("split_step"), 16)
                o = bank("wo", s)
                bank_read(pe, "wo", s, 0, n)
                pe.wait_ge(sem("onT_sb"), n + 1)
                for k in range(T):
                    pe.matmul(o[:, k * D:(k + 1) * D], onT[:, s, k * P:(k + 1) * P], w_in[:, WO, :],
                              start=True, stop=False)
                    last = pe.matmul(o[:, k * D:(k + 1) * D], ones_bf[:, :], bo_parts[:, :],
                                     start=False, stop=True)
                last.then_inc(sem("wo_ps"), 1)

            def xT3(n, s, r):
                pe.wait_ge(sem("x3_ready"), n + 1)
                transpose_x(3, n, s, r, x3)

            def proj3(n, s, r):
                o = bank("proj3", s)
                bank_read(pe, "proj3", s, 0, n)
                pe.wait_ge(sem("xT_sb3"), n + 1)
                for k in range(T):
                    pe.matmul(o[:, k * 2 * D:(k + 1) * 2 * D], xT[:, s, k * P:(k + 1) * P], hg_w[:, :],
                              start=True, stop=False)
                    last = pe.matmul(o[:, k * 2 * D:(k + 1) * 2 * D], ones_bf[:, :], hg_parts[:, :],
                                     start=False, stop=True)
                last.then_inc(sem("hg_ps"), 1)

            def agg3(n, s, r):
                o = bank("agg3", s)
                bank_read(pe, "agg3", s, 0, n)
                pe.wait_ge(sem("vals_ready"), n + 1)
                for k in range(T):
                    for j in range(T):
                        last = pe.matmul(o[:, k * D:(k + 1) * D], eq1[:, s, j, k * P:(k + 1) * P],
                                         vals[:, s, j, :], start=(j == 0), stop=(j == T - 1))
                last.then_inc(sem("agg3_ps"), 1)

            steps = {
                "xT0": xT0, "proj0": proj0, "s2_rows": s2_rows, "pT0": lambda *a: transpose_p(0, *a), "agg0": agg0,
                "xT1": xT1, "proj1": proj1, "scores1": scores1, "pT1": lambda *a: transpose_p(1, *a),
                "agg1": agg1, "xT2": xT2, "proj2": proj2,
                "scores2a": lambda n, s, r: scores2(0, n, s), "scores2b": lambda n, s, r: scores2(1, n, s),
                "pT2a": lambda n, s, r: pT2(0, n, s), "pT2b": lambda n, s, r: pT2(1, n, s),
                "rsum_rows": rsum_rows_, "agg2": agg2, "wo": wo, "xT3": xT3, "proj3": proj3,
                "agg3": agg3,
            }

            def relations():
                pe.wait_ge(sem("x4_ready"), B)
                pe.wait_ge(sem("rel_w_loaded"), 16 * len(rel_weights))
                for k in range(4):
                    last = pe.transpose(ps[:, 0, k * P:(k + 1) * P], w_in[:, k, :], ident[:, :])
                last.then_inc(sem("rel_setup_pe"), 1)
                pe.wait_ge(sem("rel_setup_sb"), 1)
                for way in range(2):
                    last = pe.matmul(ps[:, 1, way * P:(way + 1) * P], w_in[:, way, :], wT[:, way, :],
                                     start=True, stop=True)
                last.then_inc(sem("rel_setup_pe"), 1)
                pe.wait_ge(sem("rel_setup_sb"), 2)
                with pe.Fori(0, B) as g:
                    pe.wait_ge(sem("rel_adj_f_ready"), g + 1)
                    for j in range(T):
                        for k in range(T):
                            pe.transpose(ps[:, 0, j * N + k * P:j * N + (k + 1) * P],
                                         rel_adj_f[:, k, j * P:(j + 1) * P], ident[:, :])
                    for k in range(T):
                        last = pe.transpose(ps[:, 1, k * P:(k + 1) * P], rel_x[:, k, :], ident[:, :])
                    last.then_inc(sem("rel_T_ps"), 1)
                    pe.wait_ge(sem("rel_T_sb"), g + 1)
                    for way, w in enumerate((rel_w[:, 0, :], rel_w[:, 1, :], hg_w[:, :])):
                        for k in range(T):
                            last = pe.matmul(ps[:, 2 + way, k * 2 * D:(k + 1) * 2 * D],
                                             rel_xT[:, k * P:(k + 1) * P], w, start=True, stop=True)
                    last.then_inc(sem("rel_hg_ps"), 1)
                    pe.wait_ge(sem("rel_loop_vals"), g + 1)
                    for k in range(T):
                        for j in range(T):
                            last = pe.matmul(ps[:, 5, k * D:(k + 1) * D], rel_hot[0][:, j, k * P:(k + 1) * P],
                                             rel_vals[0][:, j, :], start=(j == 0), stop=(j == T - 1))
                    last.then_inc(sem("rel_loop_ps"), 1)
                    with pe.Fori(0, NREL) as r:
                        pe.wait_ge(sem("rel_vals_ready"), g * NREL + r + 1)
                        for k in range(T):
                            for way in range(2):
                                for j in range(T):
                                    last = pe.matmul(ps[:, 6, k * D:(k + 1) * D],
                                                     rel_hot[way][:, j, k * P:(k + 1) * P],
                                                     rel_vals[way][:, j, :], start=(way + j == 0),
                                                     stop=(way == 1 and j == T - 1))
                        last.then_inc(sem("rel_ps"), 1)
                        pe.wait_ge(sem("rel_added"), g * NREL + r + 1)

            setup()
            rounds(pe, "tensor", steps)
            with if_relations(pe):
                relations()

        @block.scalar
        def _(act):
            def setup():
                act.wait_ge(sem("setup_pe"), 1)
                nc.scalar.copy(w0T12[:, :], ps[:, 4, 0:P + 2]).then_inc(sem("weights_ready"), 1)
                act.wait_ge(sem("dve_setup"), 2)

            def setup_later():
                act.wait_ge(sem("setup_pe"), 2)
                nc.scalar.copy(wT[:, 0:3, :].rearrange("p a n -> p (a n)"), ps[:, 4, 0:3 * P])\
                    .then_inc(sem("setup_t_sb"), 1)
                nc.scalar.mul(hg_w[:, 0:D], ps[:, 4, 3 * P:4 * P], 0.5)
                act.wait_ge(sem("setup_pe"), 3)
                nc.scalar.copy(wT[:, 3, :], ps[:, 5, 0:P]).then_inc(sem("setup_t_sb"), 1)
                nc.scalar.copy(u12[:, :], ps[:, 5, P:P + 2])
                nc.scalar.copy(xw_w[:, D:D + 1], ps[:, 5, P + 1:P + 2])
                nc.scalar.copy(hg_w[:, D:2 * D], ps[:, 5, 2 * P:3 * P])
                nc.scalar.copy(xw_w[:, 0:D], w_in[:, W_1, :])
                nc.scalar.copy(xw_w[:, D + 1:2 * D + 1], w_in[:, W_2, :])
                act.wait_ge(sem("setup_pe"), 4)
                nc.scalar.copy(M1[:, :], ps[:, 6, 0:P])
                act.wait_ge(sem("setup_pe"), 5)
                nc.scalar.copy(w_in[:, W0, :], ps[:, 7, 0:D]).then_inc(sem("weights_ready"), 1)

            def test_adj(n, s, r):
                act.wait_ge(sem(f"adj_loaded{s}"), r * 16 + 16)
                if not fresh(r):
                    act.wait_ge(sem("excess_added"), n - SLOTS + 1)
                nc.scalar.activation(over_one[:, s], adj_in[:, s], ACT.Relu, bias=minus_one[:, 0:1],
                                     accum_out=excess_row[:, s:s + 1]).then_inc(sem("excess_ready"), 1)

            def copy_xT(layer, n, s):
                if is_first(n) and layer == 1:
                    setup_later()
                act.wait_ge(sem(f"xT_ps{layer}"), n + 1)
                nc.scalar.copy(xT[:, s, :], bank(f"xT{layer}", s)[:, 0:N]).then_inc(sem(f"xT_sb{layer}"), 1)

            def proj0(n, s, r):
                act.wait_ge(sem("wh_ps"), n + 1)
                o = bank("proj0", s)[:, 0:T * (D + 2)].rearrange("p (t d) -> p t d", t=T)
                nc.scalar.copy(xw[:, s, :, 0:2], o[:, :, D:D + 2])
                nc.scalar.copy(xw[:, s, :, D + 1:2 * D + 1], o[:, :, 0:D]).then_inc(sem("wh_sb"), 1)

            def pT0(n, s, r):
                act.wait_ge(sem("shift0_ready"), n + 1)
                for k in range(T):
                    nc.scalar.activation(pa[:, s, k, :], sm[:, s, k, :], ACT.Exp, bias=small[:, s, 2, k:k + 1])
                    last = nc.scalar.activation(pb[:, s, k, :], sm[:, s, k, :], ACT.Exp,
                                                bias=small[:, s, 3, k:k + 1], scale=SLOPE)
                last.then_inc(sem("branches_ready"), 1)

            def agg0(n, s, r):
                act.wait_ge(sem("pT_ps0"), n + 1)
                nc.scalar.copy(probT[:, s].rearrange("p t n -> p (t n)"), bank("pT0", s))\
                    .then_inc(sem("pT_sb0"), 1)

            def proj1(n, s, r):
                act.wait_ge(sem("tT_ps"), n + 1)
                nc.scalar.activation(tT[:, s, :], bank("proj1", s, 0)[:, 0:N], ACT.Identity,
                                     bias=u12[:, 0:1]).then_inc(sem("tT_sb"), 1)

            def copy_xw(n, s, r):
                act.wait_ge(sem("xw_ps"), n + 1)
                nc.scalar.copy(xw[:, s, :, 0:2 * D + 1], bank("proj1", s, 1)[:, :, 0:2 * D + 1])\
                    .then_inc(sem("xw_sb"), 1)

            def scores1(n, s, r):
                act.wait_ge(sem("z_ps"), n + 1)
                act.wait_ge(sem("xw_sb"), n + 1)
                for k in range(T):
                    last = nc.scalar.activation(pa[:, s, k, :], bank("scores1", s)[:, k * N:(k + 1) * N],
                                                ACT.Identity, bias=xw[:, s, k, D:D + 1])
                last.then_inc(sem("z_sb"), 1)

            def pT1(n, s, r):
                act.wait_ge(sem("shift1_ready"), n + 1)
                for k in range(T):
                    last = nc.scalar.activation(prob[:, s, k, :], sm[:, s, k, :], ACT.Exp,
                                                bias=small[:, s, 0, k:k + 1])
                last.then_inc(sem("p_ready1"), 1)

            def agg1(n, s, r):
                act.wait_ge(sem("pT_ps1"), n + 1)
                nc.scalar.copy(probT[:, s].rearrange("p t n -> p (t n)"), bank("pT1", s))\
                    .then_inc(sem("pT_sb1"), 1)

            def elu1(n, s, r):
                act.wait_ge(sem("agg1_read"), n + 1)
                nc.scalar.activation(hexp[:, s], hmid[:, s], ACT.Exp).then_inc(sem("hexp_ready"), 1)

            def proj2(n, s, r):
                if is_first(n):
                    act.wait_ge(sem("pool_setup"), 3)
                act.wait_ge(sem("qkv_ps"), n + 1)
                o = bank("proj2", s)
                for h in range(2):
                    r = slice(h * DK, (h + 1) * DK)
                    nc.scalar.activation(qblk[r, s, h, :], o[r, 0, 0:N], ACT.Identity, bias=cols[r, BQ:BQ + 1])
                nc.scalar.activation(kT[:, s, :], o[:, 1, N:2 * N], ACT.Identity, bias=cols[:, BK:BK + 1])\
                    .then_inc(sem("qkv_sb"), 1)

            def q_rest(n, s, r):
                if is_first(n):
                    act.wait_ge(sem("pool_setup"), 3)
                act.wait_ge(sem("qkv_ps"), n + 1)
                o = bank("proj2", s)
                for h in range(2, 4):
                    rows = slice(h * DK, (h + 1) * DK)
                    last = nc.scalar.activation(qblk[rows, s, h, :], o[rows, 0, 0:N], ACT.Identity,
                                                bias=cols[rows, BQ:BQ + 1])
                last.then_inc(sem("q_sb"), 1)

            def copy_v(n, s, r):
                act.wait_ge(sem("qkv_ps"), n + 1)
                o = bank("proj2", s)
                nc.scalar.copy(vn[:, s].rearrange("p t d -> p (t d)"), o[:, 1, 0:T * D])\
                    .then_inc(sem("qkv_sb"), 1)

            def exp2(k, n, s):
                act.wait_ge(sem("shift2_ready"), n * T + k + 1)
                for h in range(HEADS):
                    c = k * HEADS + h
                    last = nc.scalar.activation(p2[:, s, k, h, :], p2[:, s, k, h, :], ACT.Exp,
                                                bias=nmax2[:, s, c:c + 1], scale=SCALE,
                                                accum_out=sum2[:, s, c:c + 1])
                last.then_inc(sem("p_ready2"), 1)

            def pT2(k, n, s):
                for j in range(T):
                    act.wait_ge(sem("pT_ps2"), n * 4 + k * T + j + 1)
                    nc.scalar.copy(p2T[:, s, :, j, k * P:(k + 1) * P],
                                   bank("pT2" + "ab"[k], s, j).rearrange("p (h i) -> p h i", h=HEADS))\
                        .then_inc(sem("pT_sb2"), 1)

            def copy_rsum_rows(n, s, r):
                act.wait_ge(sem("rsum_rows_ps"), n + 1)
                nc.scalar.copy(rsum_rows[:, s, :], bank("rsum_rows", s, 0)[:, 0:N])\
                    .then_inc(sem("rsum_rows_sb"), 1)

            def gate3(n, s, r):
                act.wait_ge(sem("hg_ps"), n + 1)
                o = bank("proj3", s).rearrange("p (t d) -> p t d", t=T)
                nc.scalar.activation(gate[:, s], o[:, :, D:2 * D], ACT.Tanh, scale=0.5)\
                    .then_inc(sem("gate_ready"), 1)

            steps = {
                "test_adj": test_adj, "c_xT0": lambda n, s, r: copy_xT(0, n, s), "c_proj0": proj0, "exp0": pT0,
                "c_pT0": agg0, "c_xT1": lambda n, s, r: copy_xT(1, n, s), "c_tT": proj1, "c_xw": copy_xw,
                "c_z": scores1, "exp1": pT1, "c_pT1": agg1, "c_elu": elu1,
                "c_xT2": lambda n, s, r: copy_xT(2, n, s), "c_qk": proj2, "q_rest": q_rest, "c_v": copy_v,
                "exp2a": lambda n, s, r: exp2(0, n, s), "exp2b": lambda n, s, r: exp2(1, n, s),
                "c_pT2a": lambda n, s, r: pT2(0, n, s), "c_pT2b": lambda n, s, r: pT2(1, n, s),
                "c_rsum": copy_rsum_rows, "c_xT3": lambda n, s, r: copy_xT(3, n, s), "gate3": gate3,
            }

            def relations():
                act.wait_ge(sem("rel_setup_pe"), 1)
                for way in range(2):
                    nc.scalar.mul(rel_w[:, way, 0:D], ps[:, 0, way * P:(way + 1) * P], 0.5)
                nc.scalar.copy(wT[:, 0:2, :].rearrange("p a n -> p (a n)"), ps[:, 0, 2 * P:4 * P])\
                    .then_inc(sem("rel_setup_sb"), 1)
                act.wait_ge(sem("rel_setup_pe"), 2)
                nc.scalar.copy(rel_w[:, :, D:2 * D], ps[:, 1, 0:2 * P].rearrange("p (a n) -> p a n", a=2))\
                    .then_inc(sem("rel_setup_sb"), 1)
                with act.Fori(0, B) as g:
                    act.wait_ge(sem("rel_T_ps"), g + 1)
                    nc.scalar.copy(rel_adjT_f.rearrange("p t n -> p (t n)"), ps[:, 0, :])
                    nc.scalar.copy(rel_xT, ps[:, 1, 0:N]).then_inc(sem("rel_T_sb"), 1)
                    act.wait_ge(sem("rel_hg_ps"), g + 1)
                    nc.scalar.copy(rel_hg[:, 0:3].rearrange("p w t d -> p w (t d)"), ps[:, 2:5, :])\
                        .then_inc(sem("rel_hg_sb"), 1)
                    act.wait_ge(sem("rel_loop_sum"), g + 1)
                    nc.scalar.activation(rel_hg[:, 2, :, D:2 * D], rel_hg[:, 2, :, D:2 * D], ACT.Tanh, scale=0.5)\
                        .then_inc(sem("rel_loop_gate"), 1)
                    with act.Fori(0, NREL) as r:
                        act.wait_ge(sem("rel_sums_ready"), g * NREL + r + 2)
                        for way in range(2):
                            last = nc.scalar.activation(rel_sum[:, way, :, D:2 * D], rel_sum[:, way, :, D:2 * D],
                                                        ACT.Tanh, scale=0.5)
                        last.then_inc(sem("rel_gates"), 1)

            setup()
            rounds(act, "scalar", steps)
            with if_relations(act):
                relations()

        @block.vector
        def _(dve):
            def done(ins, signal, value, apart=False):
                ins.then_inc(sem(signal), 1)
                if apart:
                    wait_apart(dve, sem(signal), value)
                else:
                    dve.wait_ge(sem(signal), value)

            def setup():
                nc.vector.memset(ones_row[:, :], 1.0).then_inc(sem("dve_setup"), 1)
                nc.vector.memset(minus_half[:, :], -0.5)
                nc.vector.memset(minus_one[:, :], -1.0).then_inc(sem("dve_setup"), 1)
                nc.vector.memset(xw[:, :, :, 2 * D + 1:2 * D + 2], 1.0)
                nc.vector.memset(ones_bf[:, :], 1.0)

            def setup_later():
                dve.wait_ge(sem("dve_setup"), 1)
                dve.wait_ge(sem("weights_loaded"), WEIGHTS_LOADED)
                nc.vector.tensor_scalar(bv_rep[:, :], ones_row[:, :], cols[:, BV:BV + 1], None, ALU.mult)\
                    .then_inc(sem("bv_ready"), 1)
                done(nc.vector.tensor_scalar(hg_bias[:, 0:D], hg_bias[:, 0:D], 0.5, None, ALU.mult),
                     "hg_bias_ready", 1)

            def setup_biases():
                dve.wait_ge(sem("weights_ready"), 2)
                done(nc.vector.tensor_tensor(bo_row[:, :], w_in[:, W0, :], bo_row[:, :], ALU.add),
                     "bias_row_ready", 1)
                dve.wait_ge(sem("consts_ready"), 1)

                def split(dst, row, width, steps_before):
                    part = p2T[:, SLOTS - 1, 0:3, 0, 0:width]
                    at = steps_before
                    low = [m[:, SLOTS - 1, k, 0:width] for m, k in ((neg0, 0), (neg0, 1), (neg1, 0))]
                    done(nc.vector.tensor_copy(low[0], row), "split_step", at + 1)
                    done(nc.vector.tensor_tensor(part[:, 0, :], row, low[0], ALU.subtract), "split_step", at + 2)
                    done(nc.vector.tensor_copy(low[1], part[:, 0, :]), "split_step", at + 3)
                    done(nc.vector.tensor_tensor(part[:, 1, :], part[:, 0, :], low[1], ALU.subtract),
                         "split_step", at + 4)
                    done(nc.vector.tensor_copy(low[2], part[:, 1, :]), "split_step", at + 5)
                    done(nc.vector.tensor_scalar(dst, low[0], ident[:, 0:1], None, ALU.mult), "split_step", at + 6)
                    for k in (1, 2):
                        done(nc.vector.scalar_tensor_tensor(out=dst, in0=low[k], scalar=ident[:, k:k + 1], in1=dst,
                                                            op0=ALU.mult, op1=ALU.add), "split_step", at + 6 + k)
                    return at + 8

                at = split(bo_parts[:, :], bo_row[:, :], D, 0)
                split(hg_parts[:, :], hg_bias[:, :], 2 * D, at)

            def masks(n, s, r):
                dve.wait_ge(sem(f"adj_loaded{s}"), r * 16 + 16)
                nc.vector.tensor_scalar(neg0[:, s], adj_in[:, s], 0.0, NEG_INF, ALU.is_equal, ALU.mult)
                nc.vector.tensor_scalar(neg1[:, s], adj_in[:, s], 0.0, NEG_L1, ALU.is_le, ALU.mult)
                nc.vector.tensor_scalar(eq1[:, s], adj_in[:, s], 1.0, None, ALU.is_equal)\
                    .then_inc(sem("masks_ready"), 1)

            def moments(layer, n, s, add):
                for k in range(T):
                    add(k).then_inc(sem(f"y{layer}_ready"), 1)
                for k in range(T):
                    dve.wait_ge(sem(f"y{layer}_ready"), n * T + k + 1)
                    nc.vector.bn_stats(stats[:, s, k, :], y[:, s, k, :]).then_inc(sem(f"stats{layer}_ready"), 1)
                for k in range(T):
                    wait_apart(dve, sem(f"stats{layer}_ready"), n * T + k + 1)
                    nc.vector.bn_aggr(mv[:, s, k, :], stats[:, s, k, :]).then_inc(sem(f"mv{layer}_ready"), 1)

            def norm(layer, n, s, r):
                dst = (x1, x2, x3)[layer]
                if is_first(n) and layer == 0:
                    setup_later()
                if not fresh(r) and layer in (0, 2):
                    dve.wait_ge(sem(f"stored{s}" if layer == 0 else f"x3_aside{s}"), r * 16)
                dve.wait_ge(sem(f"rstd{layer}_ready"), n + 1)
                for k in range(T):
                    last = nc.vector.tensor_scalar(dst[:, s, k, :], y[:, s, k, :], mv[:, s, k, 0:1],
                                                   rstd[:, s, k:k + 1], ALU.subtract, ALU.mult)
                last.then_inc(sem(f"x{layer + 1}_ready"), 1)

            def shift0(n, s, r):
                dve.wait_ge(sem("masks_ready"), n + 1)
                wait_apart(dve, sem("s2_ps"), n + 1)
                o = bank("s2_rows", s)
                for k in range(T):
                    last = nc.vector.tensor_tensor_reduce(sm[:, s, k, :], o[:, 0:N], neg0[:, s, k, :], 1.0, LOWEST,
                                                          ALU.add, ALU.max, rowmax[:, s, k:k + 1])
                done(last, "rowmax0_ready", n + 1)
                s1 = xw[:, s, :, 0]
                done(nc.vector.scalar_tensor_tensor(out=small[:, s, 0, :], in0=rowmax[:, s, :], scalar=0.1 * NEG_INF,
                                                    in1=s1, op0=ALU.max, op1=ALU.add), "s12_ready", n + 1)
                done(nc.vector.scalar_tensor_tensor(out=small[:, s, 1, :], in0=small[:, s, 0, :], scalar=SLOPE,
                                                    in1=small[:, s, 0, :], op0=ALU.mult, op1=ALU.max),
                     "m0_ready", n + 1)
                nc.vector.tensor_tensor(small[:, s, 2, :], s1, small[:, s, 1, :], ALU.subtract)
                nc.vector.scalar_tensor_tensor(out=small[:, s, 3, :], in0=s1, scalar=SLOPE, in1=small[:, s, 1, :],
                                               op0=ALU.mult, op1=ALU.subtract).then_inc(sem("shift0_ready"), 1)

            def row_sums(n, s, o):
                done(nc.vector.tensor_scalar(small[:, s, 4, :], o[:, :, D], TINY, None, ALU.max),
                     "sum0_ready", n + 1)
                done(nc.vector.reciprocal(rsum[:, s, :], small[:, s, 4, :]), "rsum0_ready", n + 1)

            def max0(n, s, r):
                dve.wait_ge(sem("branches_ready"), n + 1)
                nc.vector.tensor_tensor(prob[:, s], pa[:, s], pb[:, s], ALU.max).then_inc(sem("p_ready0"), 1)

            def norm0(n, s, r):
                dve.wait_ge(sem("agg0_ps"), n + 1)
                o = bank("agg0", s)[:, 0:T * (D + 1)].rearrange("p (t d) -> p t d", t=T)
                row_sums(n, s, o)
                if not fresh(r):
                    dve.wait_ge(sem("x4_ready"), n - SLOTS + 1)
                moments(0, n, s, lambda k: nc.vector.scalar_tensor_tensor(
                    out=y[:, s, k, :], in0=o[:, k, 0:D], scalar=rsum[:, s, k:k + 1], in1=x_in[:, s, k, :],
                    op0=ALU.mult, op1=ALU.add))

            def shift1(n, s, r):
                dve.wait_ge(sem("z_sb"), n + 1)
                for k in range(T):
                    nc.vector.scalar_tensor_tensor(out=pb[:, s, k, :], in0=pa[:, s, k, :], scalar=SLOPE,
                                                   in1=pa[:, s, k, :], op0=ALU.mult, op1=ALU.max)\
                        .then_inc(sem("leaky1_ready"), 1)
                for k in range(T):
                    wait_apart(dve, sem("leaky1_ready"), n * T + k + 1)
                    last = nc.vector.tensor_tensor_reduce(sm[:, s, k, :], pb[:, s, k, :], neg1[:, s, k, :], 1.0, LOWEST,
                                                          ALU.add, ALU.max, rowmax[:, s, k:k + 1])
                done(last, "rowmax1_ready", n + 1)
                nc.vector.tensor_scalar(small[:, s, 0, :], rowmax[:, s, :], -1.0, None, ALU.mult)\
                    .then_inc(sem("shift1_ready"), 1)

            def elu1(n, s, r):
                if is_first(n):
                    setup_biases()
                dve.wait_ge(sem("agg1_ps"), n + 1)
                o = bank("agg1", s)[:, 0:T * (D + 1)].rearrange("p (t d) -> p t d", t=T)
                done(nc.vector.reciprocal(rsum[:, s, :], o[:, :, D]), "rsum1_ready", n + 1)
                for k in range(T):
                    last = nc.vector.scalar_tensor_tensor(out=hmid[:, s, k, :], in0=o[:, k, 0:D], scalar=rsum[:, s, k:k + 1],
                                                          in1=xw[:, s, k, 0:D], op0=ALU.mult, op1=ALU.add)
                last.then_inc(sem("agg1_read"), 1)
                dve.wait_ge(sem("agg1_read"), n + 1)
                nc.vector.scalar_tensor_tensor(out=y[:, s], in0=hmid[:, s], scalar=0.0, in1=x1[:, s],
                                               op0=ALU.max, op1=ALU.add).then_inc(sem("hpos_ready"), 1)

            def norm1(n, s, r):
                dve.wait_ge(sem("hexp_ready"), n + 1)
                dve.wait_ge(sem("hpos_ready"), n + 1)
                moments(1, n, s, lambda k: nc.vector.scalar_tensor_tensor(
                    out=y[:, s, k, :], in0=hexp[:, s, k, :], scalar=1.0, in1=y[:, s, k, :],
                    op0=ALU.min, op1=ALU.add))

            def shift2(k, n, s):
                dve.wait_ge(sem("neg2_ready"), n + 1)
                wait_apart(dve, sem("scores2_ps"), n * T + k + 1)
                o = bank("scores2" + "ab"[k], s)
                for h in range(HEADS):
                    c = k * HEADS + h
                    last = nc.vector.tensor_tensor_reduce(
                        p2[:, s, k, h, :], o[:, h // 2, (h % 2) * N:(h % 2 + 1) * N], neg2[:, s, k, :], 1.0, LOWEST,
                        ALU.add, ALU.max, rowmax2[:, s, c:c + 1])
                last.then_inc(sem("scores2_read"), 1)
                dve.wait_ge(sem("scores2_read"), n * T + k + 1)
                nc.vector.tensor_scalar(nmax2[:, s, k * HEADS:(k + 1) * HEADS],
                                        rowmax2[:, s, k * HEADS:(k + 1) * HEADS], -SCALE, None, ALU.mult)\
                    .then_inc(sem("shift2_ready"), 1)

            def rsum2_(n, s, r):
                dve.wait_ge(sem("p_ready2"), n * T + T)
                nc.vector.reciprocal(rsum2[:, s, :], sum2[:, s, :]).then_inc(sem("rsum2_ready"), 1)

            def norm_o(n, s, r):
                dve.wait_ge(sem("agg2_ps"), n + 1)
                dve.wait_ge(sem("rsum_rows_sb"), n + 1)
                o = bank("agg2", s)
                nc.vector.tensor_tensor(onT[:, s, :], o[:, 0:N], rsum_rows[:, s, :], ALU.mult)\
                    .then_inc(sem("onT_sb"), 1)

            def norm2(n, s, r):
                dve.wait_ge(sem("wo_ps"), n + 1)
                o = bank("wo", s)[:, 0:T * D].rearrange("p (t d) -> p t d", t=T)
                moments(2, n, s, lambda k: nc.vector.scalar_tensor_tensor(
                    out=y[:, s, k, :], in0=o[:, k, :], scalar=0.0, in1=x2[:, s, k, :], op0=ALU.max, op1=ALU.add))

            def vals3(n, s, r):
                dve.wait_ge(sem("gate_ready"), n + 1)
                o = bank("proj3", s).rearrange("p (t d) -> p t d", t=T)
                nc.vector.scalar_tensor_tensor(out=vals[:, s], in0=gate[:, s], scalar=1.0, in1=o[:, :, 0:D],
                                               op0=ALU.add, op1=ALU.mult).then_inc(sem("vals_ready"), 1)

            def norm3(n, s, r):
                dve.wait_ge(sem("agg3_ps"), n + 1)
                o = bank("agg3", s)[:, 0:T * D].rearrange("p (t d) -> p t d", t=T)
                moments(3, n, s, lambda k: nc.vector.scalar_tensor_tensor(
                    out=y[:, s, k, :], in0=o[:, k, :], scalar=0.0, in1=x3[:, s, k, :], op0=ALU.max, op1=ALU.add))

            steps = {
                "masks": masks, "shift0": shift0, "max0": max0, "sum0": norm0, "shift1": shift1, "elu1": elu1,
                "sum1": norm1,
                "shift2a": lambda n, s, r: shift2(0, n, s), "shift2b": lambda n, s, r: shift2(1, n, s),
                "rsum2": rsum2_, "norm_o": norm_o, "sum2": norm2, "vals3": vals3, "sum3": norm3,
                "norm0": lambda *a: norm(0, *a),
                "norm2": lambda *a: norm(2, *a),
            }

            setup()
            rounds(dve, "vector", steps)

            dve.wait_ge(sem("excess_all_ready"), 1)
            nc.vector.tensor_scalar(excess_flag[:, :], excess_all[:, :], 0.0, None, ALU.is_gt)\
                .then_inc(sem("flag_ready"), 1)

            def relations():
                def relation_steps(k):
                    dve.wait_ge(sem("rel_bias_loaded"), k * 64 + 64)
                    for way in range(2):
                        nc.vector.scalar_tensor_tensor(
                            out=rel_sum[:, way, :, 0:D],
                            in0=rel_bias[:, way, 0:1, :].to_broadcast([P, T, D]), scalar=0.5,
                            in1=rel_hg[:, way, :, 0:D], op0=ALU.mult, op1=ALU.add)
                        last = nc.vector.tensor_tensor(rel_sum[:, way, :, D:2 * D], rel_hg[:, way, :, D:2 * D],
                                                       rel_bias[:, way, 1:2, :].to_broadcast([P, T, D]), ALU.add)
                    last.then_inc(sem("rel_sums_ready"), 1)
                    for way, a in enumerate((rel_adjT_f, rel_adj_f)):
                        last = nc.vector.tensor_scalar(rel_hot[way], a, rel_no[:, 0:1], None, ALU.is_equal)
                    last.then_inc(sem("rel_hot_ready"), 1)
                    dve.wait_ge(sem("rel_hot_ready"), k + 1)
                    nc.vector.tensor_scalar(rel_no[:, :], rel_no[:, :], 1.0, None, ALU.add)\
                        .then_inc(sem("rel_no_ready"), 1)
                    dve.wait_ge(sem("rel_no_ready"), k + 1)
                    dve.wait_ge(sem("rel_gates"), k + 1)
                    for way in range(2):
                        last = nc.vector.scalar_tensor_tensor(
                            out=rel_vals[way], in0=rel_sum[:, way, :, D:2 * D], scalar=1.0,
                            in1=rel_sum[:, way, :, 0:D], op0=ALU.add, op1=ALU.mult)
                    last.then_inc(sem("rel_vals_ready"), 1)
                    dve.wait_ge(sem("rel_ps"), k + 1)
                    o = ps[:, 6, 0:T * D].rearrange("p (t d) -> p t d", t=T)
                    nc.vector.tensor_tensor(rel_acc, o, rel_acc, ALU.add).then_inc(sem("rel_added"), 1)
                    dve.wait_ge(sem("rel_added"), k + 1)

                dve.wait_ge(sem("x4_ready"), B)
                nc.vector.memset(rel_no[:, :], 0.0).then_inc(sem("rel_graph_done"), 1)
                nc.vector.memset(small[:, 0, 5, :], 0.0).then_inc(sem("rel_sums_ready"), 1)
                with dve.Fori(0, B) as g:
                    dve.wait_ge(sem("rel_graph_done"), g + 1)
                    dve.wait_ge(sem("rel_loaded"), g * 32 + 32)
                    nc.vector.memset(rel_no[:, :], 2.0).then_inc(sem("rel_first_no"), 1)
                    nc.vector.tensor_copy(rel_adj_f, rel_adj).then_inc(sem("rel_adj_f_ready"), 1)
                    dve.wait_ge(sem("rel_adj_f_ready"), g + 1)
                    nc.vector.tensor_scalar(rel_hot[0], rel_adj_f, 1.0, None, ALU.is_equal)
                    dve.wait_ge(sem("rel_hg_sb"), g + 1)
                    b = hg_bias[:, :].rearrange("p (a d) -> p a d", a=1).to_broadcast([P, T, 2 * D])
                    nc.vector.tensor_tensor(rel_hg[:, 2], rel_hg[:, 2], b, ALU.add).then_inc(sem("rel_loop_sum"), 1)
                    dve.wait_ge(sem("rel_loop_gate"), g + 1)
                    nc.vector.scalar_tensor_tensor(out=rel_vals[0], in0=rel_hg[:, 2, :, D:2 * D], scalar=1.0,
                                                   in1=rel_hg[:, 2, :, 0:D], op0=ALU.add, op1=ALU.mult)\
                        .then_inc(sem("rel_loop_vals"), 1)
                    dve.wait_ge(sem("rel_loop_ps"), g + 1)
                    nc.vector.tensor_copy(rel_acc, ps[:, 5, 0:T * D].rearrange("p (t d) -> p t d", t=T))\
                        .then_inc(sem("rel_acc_ready"), 1)
                    with dve.Fori(0, NREL) as r:
                        dve.wait_ge(sem("rel_acc_ready"), g + 1)
                        dve.wait_ge(sem("rel_first_no"), g + 1)
                        relation_steps(g * NREL + r)
                    nc.vector.scalar_tensor_tensor(out=hmid[:, 0], in0=rel_acc, scalar=0.0, in1=rel_x,
                                                   op0=ALU.max, op1=ALU.add).then_inc(sem("rel_y_ready"), 1)
                    dve.wait_ge(sem("rel_y_ready"), g + 1)
                    for k in range(T):
                        last = nc.vector.bn_stats(stats[:, 0, k, :], hmid[:, 0, k, :])
                    last.then_inc(sem("rel_stats"), 1)
                    wait_apart(dve, sem("rel_stats"), g + 1)
                    for k in range(T):
                        last = nc.vector.bn_aggr(mv[:, 0, k, :], stats[:, 0, k, :])
                    last.then_inc(sem("rel_mv"), 1)
                    dve.wait_ge(sem("rel_rstd"), g + 1)
                    for k in range(T):
                        last = nc.vector.tensor_scalar(rel_out[:, k, :], hmid[:, 0, k, :], mv[:, 0, k, 0:1],
                                                       rstd[:, 0, k:k + 1], ALU.subtract, ALU.mult)
                    last.then_inc(sem("rel_out_ready"), 1)
                    dve.wait_ge(sem("rel_stored"), g * 16 + 16)
                    nc.vector.memset(small[:, 0, 5, :], 0.0).then_inc(sem("rel_graph_done"), 1)

            with if_relations(dve):
                relations()

        @block.gpsimd
        def _(pool):
            def setup():
                nc.gpsimd.memset(ident[:, :], 0.0)
                nc.gpsimd.memset(excess_sum[:, :], 0.0)
                nc.gpsimd.memset(not_eye[:, :, :], 1.0).then_inc(sem("pool_setup"), 1)
                pool.wait_ge(sem("pool_setup"), 1)
                nc.gpsimd.affine_select(out=ident[:, :], in_=ident[:, :], compare_op=ALU.not_equal, fill=1.0,
                                        base=0, pattern=[[-1, P]], channel_multiplier=1)\
                    .then_inc(sem("consts_ready"), 1)
                for k in range(T):
                    last = nc.gpsimd.affine_select(out=not_eye[:, k, :], in_=not_eye[:, k, :],
                                                   compare_op=ALU.not_equal, fill=0.0, base=k * P,
                                                   pattern=[[-1, N]], channel_multiplier=1)
                last.then_inc(sem("pool_setup"), 1)
                nc.gpsimd.memset(qblk[:, :, :, :], 0.0).then_inc(sem("pool_setup"), 1)
                pool.wait_ge(sem("pool_setup"), 2)

            def mask2(n, s, r):
                pool.wait_ge(sem("masks_ready"), n + 1)
                pool.wait_ge(sem("excess_ready"), n + 1)
                nc.gpsimd.tensor_tensor(neg2[:, s], neg0[:, s], not_eye[:, :, :], ALU.mult)\
                    .then_inc(sem("neg2_ready"), 1)

            def add_excess(n, s, r):
                pool.wait_ge(sem("excess_ready"), n + 1)
                nc.gpsimd.tensor_tensor(excess_sum[:, :], excess_sum[:, :], excess_row[:, s:s + 1], ALU.add)\
                    .then_inc(sem("excess_added"), 1)
                pool.wait_ge(sem("excess_added"), n + 1)

            def rsqrt(layer, n, s):
                wait_apart(pool, sem(f"mv{layer}_ready"), n * T + T)
                nc.gpsimd.tensor_scalar(ve[:, s, :], mv[:, s, :, 1], 1.0, EPS, ALU.mult, ALU.add)\
                    .then_inc(sem(f"ve{layer}_ready"), 1)
                pool.wait_ge(sem(f"ve{layer}_ready"), n + 1)
                nc.gpsimd.tensor_tensor(rstd[:, s, :], ve[:, s, :], minus_half[:, :], ALU.pow)\
                    .then_inc(sem(f"rstd{layer}_ready"), 1)

            def repeat_rsum(n, s, r):
                wait_apart(pool, sem("rsum2_ready"), n + 1)
                nc.gpsimd.tensor_copy(rsum_rep[:, s].rearrange("p t (h d) -> p (t h) d", h=HEADS),
                                      rsum2[:, s, :].rearrange("p (c a) -> p c a", a=1)
                                      .to_broadcast([P, T * HEADS, DK])).then_inc(sem("rsum_rep_ready"), 1)

            def norm_here(layer, n, s):
                dst = (None, x2, None, x4)[layer]
                rsqrt(layer, n, s)
                nc.gpsimd.tensor_scalar(small[:, s, 6, :], mv[:, s, :, 0], -1.0, None, ALU.mult)\
                    .then_inc(sem(f"minus_mean{layer}_ready"), 1)
                pool.wait_ge(sem(f"minus_mean{layer}_ready"), n + 1)
                pool.wait_ge(sem(f"rstd{layer}_ready"), n + 1)
                nc.gpsimd.tensor_tensor(small[:, s, 7, :], small[:, s, 6, :], rstd[:, s, :], ALU.mult)\
                    .then_inc(sem(f"offset{layer}_ready"), 1)
                wait_apart(pool, sem(f"offset{layer}_ready"), n + 1)
                for k in range(T):
                    last = nc.gpsimd.tensor_scalar(dst[:, s, k, :], y[:, s, k, :], rstd[:, s, k:k + 1],
                                                   small[:, s, 7, k:k + 1], ALU.mult, ALU.add)
                last.then_inc(sem(f"x{layer + 1}_ready"), 1)

            steps = {
                "mask2": mask2, "excess": add_excess, "rstd0": lambda n, s, r: rsqrt(0, n, s),
                "norm1": lambda n, s, r: norm_here(1, n, s), "rstd2": lambda n, s, r: rsqrt(2, n, s),
                "rep_rsum": repeat_rsum, "norm3": lambda n, s, r: norm_here(3, n, s),
            }

            def relations():
                with pool.Fori(0, B) as g:
                    wait_apart(pool, sem("rel_mv"), g + 1)
                    nc.gpsimd.tensor_scalar(ve[:, 0, :], mv[:, 0, :, 1], 1.0, EPS, ALU.mult, ALU.add)\
                        .then_inc(sem("rel_ve"), 1)
                    pool.wait_ge(sem("rel_ve"), g + 1)
                    nc.gpsimd.tensor_tensor(rstd[:, 0, :], ve[:, 0, :], minus_half[:, :], ALU.pow)\
                        .then_inc(sem("rel_rstd"), 1)

            setup()
            rounds(pool, "gpsimd", steps)
            nc.gpsimd.partition_all_reduce(excess_all[:, :], excess_sum[:, :], P, bass.bass_isa.ReduceOp.max)\
                .then_inc(sem("excess_all_ready"), 1)
            with if_relations(pool):
                relations()


_INS = ['x', 'adj', 'L0_gnn_W', 'L0_gnn_a', 'L1_gnn_W', 'L1_gnn_a_1', 'L1_gnn_a_2', 'L1_gnn_a_12', 'L1_gnn_W_1',
        'L1_gnn_W_2', 'L2_gnn_Wq', 'L2_gnn_bq', 'L2_gnn_Wk', 'L2_gnn_bk', 'L2_gnn_Wv', 'L2_gnn_bv', 'L2_gnn_Wo',
        'L2_gnn_bo', 'L3_gnn_W_fwd', 'L3_gnn_W_bwd', 'L3_gnn_W_loop', 'L3_gnn_Wg_fwd', 'L3_gnn_Wg_bwd',
        'L3_gnn_Wg_loop', 'L3_gnn_b_fwd', 'L3_gnn_b_bwd', 'L3_gnn_b_loop', 'L3_gnn_bg_fwd', 'L3_gnn_bg_bwd',
        'L3_gnn_bg_loop']


def kernel(**inputs):
    import numpy as _np
    import concourse.bacc as _bacc
    from concourse import mybir as _mybir
    from concourse.bass_utils import run_bass_kernel_spmd as _run

    nc = _bacc.Bacc("TRN2", target_bir_lowering=False, num_devices=1)
    arrays, args = {}, {}
    for name in _INS:
        a = _np.ascontiguousarray(inputs[name])
        arrays[f"in_{name}_dram"] = a
        args[name] = nc.dram_tensor(f"in_{name}_dram", a.shape, _mybir.dt.from_np(a.dtype),
                                    kind="ExternalInput").ap()
    shape = _np.shape(inputs["x"])
    out = nc.dram_tensor("out_0_dram", shape, _mybir.dt.float32, kind="ExternalOutput").ap()
    build(nc, args, out)
    r = _run(nc, [arrays], core_ids=[0])
    return r.results[0]["out_0_dram"]
```
